# Optimizing a Trainium2 kernel written in Bass

```python
import numpy as np
import jax
import jax.numpy as jnp

def _softmax(x, axis=-1):
    return jax.nn.softmax(x, axis=axis)

def _gelu(x):
    return jax.nn.gelu(x, approximate=True)

def _silu(x):
    return jax.nn.silu(x)

def _sigmoid(x):
    return jax.nn.sigmoid(x)

def _layernorm(x, axis=-1, eps=1e-05):
    m = jnp.mean(x, axis=axis, keepdims=True)
    v = jnp.var(x, axis=axis, keepdims=True)
    return (x - m) / jnp.sqrt(v + eps)

def _scatter_add(tgt, idx, src, axis=0):
    return tgt.at[idx].add(src)

def _segment_sum(src, seg, n):
    return jax.ops.segment_sum(src, seg, n)
kernel_name = 'mk_seq_postln_d2_jaxref_r4_e00555'

def setup_inputs(seed: int=0):
    np.random.seed(seed)
    _w = jnp.asarray

    def _L0_attn_setup():
        import jax, jax.numpy as jnp
        import numpy as np
        D_MODEL = 256
        N_HEADS = 16
        key = jax.random.key(seed)
        ks = jax.random.split(key, 5)
        std = (2.0 / (D_MODEL + D_MODEL)) ** 0.5
        x = jax.random.normal(ks[0], (4, 512, D_MODEL), dtype=jnp.float32)
        WQ = jax.random.truncated_normal(ks[1], -3.0, 3.0, (D_MODEL, D_MODEL), jnp.float32) * std
        WK = jax.random.truncated_normal(ks[2], -3.0, 3.0, (D_MODEL, D_MODEL), jnp.float32) * std
        WV = jax.random.truncated_normal(ks[3], -3.0, 3.0, (D_MODEL, D_MODEL), jnp.float32) * std
        WO = jax.random.truncated_normal(ks[4], -3.0, 3.0, (D_MODEL, D_MODEL), jnp.float32) * std
        return {'x': x, 'WQ': WQ, 'WK': WK, 'WV': WV, 'WO': WO}
    _L0_attn_in = _L0_attn_setup()

    def _L0_ffn_setup():
        import jax, jax.numpy as jnp
        import numpy as np
        D = 256
        H = 1024
        E = 64
        K = 3
        B, S = (2, 512)
        C = 128
        key = jax.random.key(seed)
        ks = jax.random.split(key, 6)
        s = 0.02
        return {'x': jax.random.normal(ks[0], (B, S, D), jnp.float32), 'gate_w': jax.random.normal(ks[1], (D, E), jnp.float32) * s, 'gate_b': jnp.zeros((E,), jnp.float32), 'w1': jax.random.normal(ks[2], (E, D, H), jnp.float32) * s, 'b1': jnp.zeros((E, H), jnp.float32), 'w2': jax.random.normal(ks[3], (E, H, D), jnp.float32) * s, 'b2': jnp.zeros((E, D), jnp.float32)}
    _L0_ffn_in = _L0_ffn_setup()

    def _L1_attn_setup():
        import jax, jax.numpy as jnp
        import numpy as np
        EPS = 1e-05
        NUM_HEADS = 16

        def _linear_attention(x, Wq, Wk, Wv, Wo, bo):
            B, L, E = x.shape
            H = NUM_HEADS
            D = E // H
            q = (x @ Wq.T).reshape(B, L, H, D)
            k = (x @ Wk.T).reshape(B, L, H, D)
            v = (x @ Wv.T).reshape(B, L, H, D)
            phi_q = jax.nn.elu(q) + 1.0
            phi_k = jax.nn.elu(k) + 1.0
            pq = jnp.moveaxis(phi_q, 1, 0)
            pk = jnp.moveaxis(phi_k, 1, 0)
            vt = jnp.moveaxis(v, 1, 0)
            S0 = jnp.zeros((B, H, D, D), x.dtype)
            z0 = jnp.zeros((B, H, D), x.dtype)

            def step(carry, inp):
                S, z = carry
                pq_t, pk_t, v_t = inp
                S = S + pk_t[..., :, None] * v_t[..., None, :]
                z = z + pk_t
                num = jnp.einsum('bhd,bhde->bhe', pq_t, S)
                den = jnp.sum(pq_t * z, axis=-1, keepdims=True) + EPS
                return ((S, z), num / den)
            (_, _), out = jax.lax.scan(step, (S0, z0), (pq, pk, vt))
            out = jnp.moveaxis(out, 0, 1).reshape(B, L, E)
            return out @ Wo.T + bo
        key = jax.random.key(seed)
        ks = jax.random.split(key, 6)
        B, L, E = (4, 1024, 256)
        s = 1.0 / np.sqrt(E)
        return {'x': jax.random.normal(ks[0], (B, L, E), jnp.float32), 'Wq': jax.random.normal(ks[1], (E, E), jnp.float32) * s, 'Wk': jax.random.normal(ks[2], (E, E), jnp.float32) * s, 'Wv': jax.random.normal(ks[3], (E, E), jnp.float32) * s, 'Wo': jax.random.normal(ks[4], (E, E), jnp.float32) * s, 'bo': jnp.zeros((E,), jnp.float32)}
    _L1_attn_in = _L1_attn_setup()

    def _L1_ffn_setup():
        import math
        import jax, jax.numpy as jnp
        import numpy as np
        D_MODEL = 256
        D_HIDDEN = 1024
        N_EXPERTS = 8
        TOP_K = 2
        CAPACITY_FACTOR = 1.25
        key = jax.random.key(seed)
        ks = jax.random.split(key, 8)
        s = 0.02
        x = jax.random.normal(ks[0], (4, 512, D_MODEL), dtype=jnp.float32)
        router_w = jax.random.normal(ks[1], (D_MODEL, N_EXPERTS), dtype=jnp.float32) * s
        router_b = jnp.zeros((N_EXPERTS,), dtype=jnp.float32)
        w1 = jax.random.normal(ks[2], (N_EXPERTS, D_MODEL, D_HIDDEN), dtype=jnp.float32) * s
        b1 = jnp.zeros((N_EXPERTS, D_HIDDEN), dtype=jnp.float32)
        w2 = jax.random.normal(ks[3], (N_EXPERTS, D_HIDDEN, D_MODEL), dtype=jnp.float32) * s
        b2 = jnp.zeros((N_EXPERTS, D_MODEL), dtype=jnp.float32)
        return {'x': x, 'router_w': router_w, 'router_b': router_b, 'w1': w1, 'b1': b1, 'w2': w2, 'b2': b2}
    _L1_ffn_in = _L1_ffn_setup()
    _d = {'L0_attn_x': _L0_attn_in['x'], 'L0_attn_WQ': _L0_attn_in['WQ'], 'L0_attn_WK': _L0_attn_in['WK'], 'L0_attn_WV': _L0_attn_in['WV'], 'L0_attn_WO': _L0_attn_in['WO'], 'L0_ffn_gate_w': _L0_ffn_in['gate_w'], 'L0_ffn_gate_b': _L0_ffn_in['gate_b'], 'L0_ffn_w1': _L0_ffn_in['w1'], 'L0_ffn_b1': _L0_ffn_in['b1'], 'L0_ffn_w2': _L0_ffn_in['w2'], 'L0_ffn_b2': _L0_ffn_in['b2'], 'L1_attn_Wq': _L1_attn_in['Wq'], 'L1_attn_Wk': _L1_attn_in['Wk'], 'L1_attn_Wv': _L1_attn_in['Wv'], 'L1_attn_Wo': _L1_attn_in['Wo'], 'L1_attn_bo': _L1_attn_in['bo'], 'L1_ffn_router_w': _L1_ffn_in['router_w'], 'L1_ffn_router_b': _L1_ffn_in['router_b'], 'L1_ffn_w1': _L1_ffn_in['w1'], 'L1_ffn_b1': _L1_ffn_in['b1'], 'L1_ffn_w2': _L1_ffn_in['w2'], 'L1_ffn_b2': _L1_ffn_in['b2']}
    _x0 = _d['L0_attn_x']
    _d['L0_attn_x'] = jax.random.normal(jax.random.fold_in(jax.random.key(seed), 1), (4, 1024, 256), dtype=_x0.dtype)
    del _x0
    return _d

def reference(L0_attn_x, L0_attn_WQ, L0_attn_WK, L0_attn_WV, L0_attn_WO, L0_ffn_gate_w, L0_ffn_gate_b, L0_ffn_w1, L0_ffn_b1, L0_ffn_w2, L0_ffn_b2, L1_attn_Wq, L1_attn_Wk, L1_attn_Wv, L1_attn_Wo, L1_attn_bo, L1_ffn_router_w, L1_ffn_router_b, L1_ffn_w1, L1_ffn_b1, L1_ffn_w2, L1_ffn_b2):

    def _L0_attn_ref(x, WQ, WK, WV, WO):
        import jax, jax.numpy as jnp
        import numpy as np
        D_MODEL = 256
        N_HEADS = 16
        b, s, d = x.shape
        h = N_HEADS
        dk = d // h

        def proj(W):
            Wh = W.reshape(h, dk, d)
            return jnp.einsum('hkd,bsd->bhsk', Wh, x)
        Q, K, V = (proj(WQ), proj(WK), proj(WV))
        scores = jnp.einsum('bhqk,bhsk->bhqs', Q, K) / jnp.sqrt(jnp.asarray(dk, x.dtype))
        mask = jnp.tril(jnp.ones((s, s), dtype=bool))
        scores = jnp.where(mask, scores, jnp.asarray(-jnp.inf, scores.dtype))
        attn = jax.nn.softmax(scores, axis=-1)
        out = jnp.einsum('bhqs,bhsk->bhqk', attn, V)
        out = out.transpose(0, 2, 1, 3).reshape(b, s, d)
        return jnp.einsum('bsf,df->bsd', out, WO)

    def _L0_ffn_ref(x, gate_w, gate_b, w1, b1, w2, b2):
        import jax, jax.numpy as jnp
        import numpy as np
        D = 256
        H = 1024
        E = 64
        K = 3
        B, S = (2, 512)
        C = 128
        xf = x.reshape(-1, D)
        T = xf.shape[0]
        logits = xf @ gate_w + gate_b
        top_l, top_i = jax.lax.top_k(logits, K)
        gates = jax.nn.softmax(top_l, axis=-1)
        fe = top_i.reshape(-1)
        fg = gates.reshape(-1)
        tok = jnp.repeat(jnp.arange(T), K)
        oh = jax.nn.one_hot(fe, E, dtype=jnp.int32)
        pos = (jnp.cumsum(oh, axis=0) * oh).sum(-1) - 1
        valid = pos < C
        buf = jnp.zeros((E, C, D), x.dtype).at[fe, pos].set(xf[tok], mode='drop')
        h = jax.nn.gelu(jnp.einsum('ecd,edh->ech', buf, w1) + b1[:, None, :], approximate=False)
        y = jnp.einsum('ech,ehd->ecd', h, w2) + b2[:, None, :]
        rows = y[fe, jnp.minimum(pos, C - 1)] * (fg * valid.astype(x.dtype))[:, None]
        out = jnp.zeros_like(xf).at[tok].add(rows)
        return out.reshape(x.shape)

    def _L1_attn_ref(x, Wq, Wk, Wv, Wo, bo):
        import jax, jax.numpy as jnp
        import numpy as np
        EPS = 1e-05
        NUM_HEADS = 16

        def _linear_attention(x, Wq, Wk, Wv, Wo, bo):
            B, L, E = x.shape
            H = NUM_HEADS
            D = E // H
            q = (x @ Wq.T).reshape(B, L, H, D)
            k = (x @ Wk.T).reshape(B, L, H, D)
            v = (x @ Wv.T).reshape(B, L, H, D)
            phi_q = jax.nn.elu(q) + 1.0
            phi_k = jax.nn.elu(k) + 1.0
            pq = jnp.moveaxis(phi_q, 1, 0)
            pk = jnp.moveaxis(phi_k, 1, 0)
            vt = jnp.moveaxis(v, 1, 0)
            S0 = jnp.zeros((B, H, D, D), x.dtype)
            z0 = jnp.zeros((B, H, D), x.dtype)

            def step(carry, inp):
                S, z = carry
                pq_t, pk_t, v_t = inp
                S = S + pk_t[..., :, None] * v_t[..., None, :]
                z = z + pk_t
                num = jnp.einsum('bhd,bhde->bhe', pq_t, S)
                den = jnp.sum(pq_t * z, axis=-1, keepdims=True) + EPS
                return ((S, z), num / den)
            (_, _), out = jax.lax.scan(step, (S0, z0), (pq, pk, vt))
            out = jnp.moveaxis(out, 0, 1).reshape(B, L, E)
            return out @ Wo.T + bo
        return _linear_attention(x, Wq, Wk, Wv, Wo, bo)

    def _L1_ffn_ref(x, router_w, router_b, w1, b1, w2, b2):
        import math
        import jax, jax.numpy as jnp
        import numpy as np
        D_MODEL = 256
        D_HIDDEN = 1024
        N_EXPERTS = 8
        TOP_K = 2
        CAPACITY_FACTOR = 1.25
        B, T, D = x.shape
        N = B * T
        E = N_EXPERTS
        capacity = max(1, math.ceil(N / E * CAPACITY_FACTOR))
        x_flat = x.reshape(N, D)
        logits = x_flat.astype(jnp.float32) @ router_w + router_b
        gates = jax.nn.softmax(logits, axis=-1)
        _, topk_idx = jax.lax.top_k(gates, TOP_K)
        expert_mask = jax.nn.one_hot(topk_idx, E, dtype=jnp.int32).sum(1)
        pos = jnp.cumsum(expert_mask, axis=0) - 1
        expert_mask = expert_mask * (pos < capacity)
        valid = expert_mask > 0
        pos_c = jnp.where(valid, pos, capacity)
        e_idx = jnp.broadcast_to(jnp.arange(E), (N, E))
        dispatched = x_flat[:, None, :] * valid[:, :, None].astype(x.dtype)
        buf = jnp.zeros((E, capacity + 1, D), x.dtype).at[e_idx.ravel(), pos_c.ravel()].add(dispatched.reshape(N * E, D))
        buf = buf[:, :capacity]
        h = jax.nn.gelu(jnp.einsum('ecd,edh->ech', buf, w1) + b1[:, None, :], approximate=False)
        out = jnp.einsum('ech,ehd->ecd', h, w2) + b2[:, None, :]
        pos_g = jnp.minimum(pos_c, capacity - 1)
        gathered = out[e_idx, pos_g]
        weights = (gates * valid).astype(x.dtype)
        y = jnp.einsum('ned,ne->nd', gathered, weights)
        return y.reshape(B, T, D)
    x = L0_attn_x
    x = _layernorm(x + _L0_attn_ref(x, L0_attn_WQ, L0_attn_WK, L0_attn_WV, L0_attn_WO), axis=-1)
    x = _layernorm(x + _L0_ffn_ref(x, L0_ffn_gate_w, L0_ffn_gate_b, L0_ffn_w1, L0_ffn_b1, L0_ffn_w2, L0_ffn_b2), axis=-1)
    x = _layernorm(x + _L1_attn_ref(x, L1_attn_Wq, L1_attn_Wk, L1_attn_Wv, L1_attn_Wo, L1_attn_bo), axis=-1)
    x = _layernorm(x + _L1_ffn_ref(x, L1_ffn_router_w, L1_ffn_router_b, L1_ffn_w1, L1_ffn_b1, L1_ffn_w2, L1_ffn_b2), axis=-1)
    return x

_drawn_inputs = setup_inputs


def setup_inputs(seed=0):
    import zlib

    import numpy as np

    out = dict(_drawn_inputs(seed))
    spreads = {'L0_ffn_gate_b': (0.0, 0.1),
     'L0_ffn_b1': (0.0, 0.486),
     'L0_ffn_b2': (0.0, 0.1),
     'L1_attn_bo': (0.0, 0.1),
     'L1_ffn_router_b': (0.0, 0.384),
     'L1_ffn_b1': (0.0, 0.8),
     'L1_ffn_b2': (0.0, 0.401)}
    factors = {'L1_attn_Wq': 5.518, 'L1_attn_Wk': 2.971}
    for name, (base, spread) in spreads.items():
        noise = np.random.default_rng([zlib.crc32(name.encode()), seed]).standard_normal(out[name].shape)
        drawn = base * np.exp(spread * noise) if base else spread * noise
        out[name] = jnp.asarray(drawn.astype(out[name].dtype))
    for name, factor in factors.items():
        out[name] = (out[name] * factor).astype(out[name].dtype)
    return out
```

```python
from contextlib import ExitStack

import concourse.bass as bass
from concourse import mybir

ALU = mybir.AluOpType
ACT = mybir.ActivationFunctionType
AX = mybir.AxisListType
F32 = mybir.dt.float32
BF16 = mybir.dt.bfloat16
I32 = mybir.dt.int32
U32 = mybir.dt.uint32

P = 128
B, S, D = 4, 1024, 256
T = B * S
DT = D // P
ST = S // P
H, DK = 16, 16
HG = 4
G = H // HG
FG = HG * DK
STRIP = P // HG
CH = 512
F = 1024
FT = F // P
EPS = 1e-5
TERMS = ((0, 0), (0, 1), (1, 0), (0, 2), (2, 0), (1, 1))
KR = len(TERMS) * DK
BIG = float(1 << 20)

ROUTERS = ({"E": 64, "K": 3, "C": 128}, {"E": 8, "K": 2, "C": 640})


class Done:

    def __init__(self, eng, sem, base=0):
        self.eng, self.sem, self.base, self.n = eng, sem, base, 0

    def did(self, ins):
        ins.then_inc(self.sem, 1)
        self.n += 1
        return self.n

    def wait(self, n=None):
        self.eng.wait_ge(self.sem, self.base + (self.n if n is None else n))

    def hold(self):
        hold(self.eng, self.sem, self.base + self.n)


def hold(eng, sem, value):
    eng.wait_ge(sem, value)
    eng.nop(nofuse=True)


LAYER_SEMS = []


class Stage:

    def __init__(self, nc, ctx, tag):
        self.nc, self.ctx, self.tag = nc, ctx, tag

    def sb(self, name, shape, dt=F32):
        return self.ctx.enter_context(self.nc.sbuf_tensor(f"{self.tag}_{name}", shape, dt))

    def ps(self, name, shape, dt=F32):
        return self.ctx.enter_context(self.nc.psum_tensor(f"{self.tag}_{name}", shape, dt))

    def sem(self, name):
        sem = self.nc.alloc_semaphore(f"{self.tag}_{name}")
        LAYER_SEMS.append(sem)
        return sem


def constants(nc, ctx, ins, dram):
    st = Stage(nc, ctx, "c")
    c = {
        "ident": st.sb("ident", [P, P]), "identb": st.sb("identb", [P, P], BF16),
        "future": st.sb("future", [P, P], BF16),
        "past": st.sb("past", [P, P]),
        "before": st.sb("before", [P, P], BF16),
        "ones": st.sb("ones", [P, P], BF16),
        "own": st.sb("own", [FG, P]),
        "zero": st.sb("zero", [P, 2048]),
    }
    for r, rt in enumerate(ROUTERS):
        c[f"expert{r}"] = st.sb(f"expert{r}", [P, rt["E"]])
        c[f"first{r}"] = st.sb(f"first{r}", [P, rt["E"]])
    with ExitStack() as tmp:
        s2 = Stage(nc, tmp, "ci")
        made, zeroed, filled = s2.sem("made"), s2.sem("zeroed"), s2.sem("filled")
        block = tmp.enter_context(nc.Block())

        @block.gpsimd
        def _(pool):
            d = Done(pool, made)
            d.did(pool.memset(c["ident"][:], 0.0))
            d.did(pool.memset(c["identb"][:], 0.0))
            d.did(pool.memset(c["future"][:], 0.0))
            d.did(pool.memset(c["past"][:], 1.0))
            d.did(pool.memset(c["before"][:], 1.0))
            d.did(pool.memset(c["ones"][:], 1.0))
            d.did(pool.memset(c["own"][:], 1.0))
            for r, rt in enumerate(ROUTERS):
                d.did(pool.iota(c[f"expert{r}"][:], [[1, rt["E"]]], base=0, channel_multiplier=0,
                                allow_small_or_imprecise_dtypes=True))
                d.did(pool.iota(c[f"first{r}"][:], [[rt["C"], rt["E"]]], base=0, channel_multiplier=0,
                                allow_small_or_imprecise_dtypes=True))
            d.wait()
            for name in ("ident", "identb"):
                d.did(pool.affine_select(out=c[name][:], in_=c[name][:], compare_op=ALU.not_equal, fill=1.0,
                                         base=0, pattern=[[-1, P]], channel_multiplier=1))
            d.did(pool.affine_select(out=c["future"][:], in_=c["future"][:], compare_op=ALU.is_ge, fill=-1e30,
                                     base=0, pattern=[[-1, P]], channel_multiplier=1))
            d.did(pool.affine_select(out=c["past"][:], in_=c["past"][:], compare_op=ALU.is_ge, fill=0.0,
                                     base=0, pattern=[[1, P]], channel_multiplier=-1))
            d.did(pool.affine_select(out=c["before"][:], in_=c["before"][:], compare_op=ALU.is_gt, fill=0.0,
                                     base=0, pattern=[[1, P]], channel_multiplier=-1))
            d.did(pool.affine_select(out=c["own"][:], in_=c["own"][:], compare_op=ALU.is_ge, fill=0.0,
                                     base=0, pattern=[[-DK, HG], [0, STRIP]], channel_multiplier=1))
            d.wait()
            d.did(pool.affine_select(out=c["own"][:], in_=c["own"][:], compare_op=ALU.is_ge, fill=0.0,
                                     base=DK - 1, pattern=[[DK, HG], [0, STRIP]], channel_multiplier=-1))
            d.wait()

        @block.vector
        def _(dve):
            dve.memset(c["zero"][:], 0.0).then_inc(zeroed, 1)

        @block.sync
        def _(sp):
            sp.wait_ge(zeroed, 1)
            n = 0
            for r, rt in enumerate(ROUTERS):
                rows = rt["E"] * rt["C"] // P
                dst = dram[f"slots{r}"].rearrange("(p n) d -> p (n d)", p=P)
                for o in range(0, rows * D, 2048):
                    sp.dma_start(dst[:, o:o + 2048], c["zero"][:]).then_inc(filled, 16)
                    n += 16
            sp.wait_ge(filled, n)
    return c


def load_weights(nc, ctx, ins, layer):
    st = Stage(nc, ctx, f"w{layer}")
    w = {k: st.sb(k, [P, DT, D]) for k in ("wq", "wk", "wv", "wo")}
    with ExitStack() as tmp:
        s2 = Stage(nc, tmp, f"wl{layer}")
        loaded = s2.sem("loaded")
        block = tmp.enter_context(nc.Block())

        @block.sync
        def _(sp):
            for k in w:
                sp.dma_start(w[k][:], ins[f"{k}{layer}"].rearrange("(j p) f -> p j f", p=P)).then_inc(loaded, 16)
            sp.wait_ge(loaded, 16 * len(w))
    return w


def project(nc, c, w, x_dram, dram, layer):
    NT = CH // P
    PER = S // CH
    NSTORE = 6 + G + (2 if layer else 0)
    with ExitStack() as ctx:
        st = Stage(nc, ctx, f"p{layer}")
        xin = [st.sb(f"xin{p}", [P, NT, D]) for p in range(PER)]
        xT = st.sb("xT", [P, DT, CH])
        rest = [st.sb(f"rest{r}", [P, CH]) for r in range(4)]
        neg = [st.sb(f"neg{r}", [P, CH]) for r in range(4)] if layer else None
        phi = [st.sb(f"phi{p}", [P, 4, CH]) for p in range(PER)] if layer else None
        parts = [[st.sb(f"part{p}_{k}", [P, 4, CH], BF16) for k in range(3)] for p in range(PER)]
        vpad = [st.sb(f"vpad{p}", [P, NT, G, P]) for p in range(PER)]
        ps_x = st.ps("ps_x", [P, DT, CH])
        ps_qk = st.ps("ps_qk", [P, 4, CH])
        ps_v = st.ps("ps_v", [P, 2, 2, D])
        x_loaded = [st.sem(f"x_loaded{p}") for p in range(PER)]
        stored = [st.sem(f"stored{p}") for p in range(PER)]
        xT_psum, xT_a, xT_v = st.sem("xT_psum"), st.sem("xT_a"), st.sem("xT_v")
        qk_psum, v_psum, v_ready = st.sem("qk_psum"), st.sem("v_psum"), st.sem("v_ready")
        hi_ready, rest_ready = st.sem("hi_ready"), st.sem("rest_ready")
        mid_ready, pads = st.sem("mid_ready"), st.sem("pads")
        neg_ready, exp_ready, phi_ready = st.sem("neg_ready"), st.sem("exp_ready"), st.sem("phi_ready")
        block = ctx.enter_context(nc.Block())

        @block.sync
        def _(sp):
            for p in range(PER):
                sp.sem_inc(stored[p], 16)

            def load(b, p):
                sp.dma_start(xin[p][:], x_dram[bass.ds(b * S + p * CH, CH), :]
                             .rearrange("(n q) d -> q n d", q=P)).then_inc(x_loaded[p], 16)

            def store(b, p):
                sp.wait_ge(mid_ready, 8 * (PER * b + p) + 16)
                for o, name in enumerate(("q", "k")):
                    for k in range(3):
                        dst = dram[f"{name}parts{layer}"]
                        dst = dst[k, b, :, p * CH:(p + 1) * CH] if o or layer else dst[k, p, b]
                        sp.dma_start(dst.rearrange("(j q) t -> q j t", q=P),
                                     parts[p][k][:, 2 * o:2 * o + 2, :]).then_inc(stored[p], 16)
                    if layer:
                        dst = dram[f"{name}full"][b, :, p * CH:(p + 1) * CH]
                        sp.dma_start(dst.rearrange("(j q) t -> q j t", q=P),
                                     phi[p][:, 2 * o:2 * o + 2, :]).then_inc(stored[p], 16)
                sp.wait_ge(v_ready, 2 * (PER * b + p) + 4)
                for g in range(G):
                    dst = dram[f"values{layer}"][b, g, p * CH:(p + 1) * CH, :]
                    sp.dma_start(dst.rearrange("(n q) e -> q n e", q=P),
                                 vpad[p][:, :, g, :]).then_inc(stored[p], 16)

            for p in range(PER):
                load(0, p)
            with sp.Fori(0, B - 1) as b:
                for p in range(PER):
                    store(b, p)
                    sp.wait_ge(xT_psum, 2 * (PER * b + p) + 2)
                    load(b + 1, p)
            for p in range(PER):
                store(B - 1, p)
            for p in range(PER):
                sp.wait_ge(stored[p], 16 * (B * NSTORE + 1))

        @block.tensor
        def _(pe):
            with pe.Fori(0, B) as b:
                for p in range(PER):
                    n = PER * b + p
                    pe.wait_ge(x_loaded[p], 16 * (b + 1))
                    for j in range(DT):
                        pe.wait_ge((xT_a, xT_v)[j], n + 1)
                        for i in range(NT):
                            mm = pe.transpose(ps_x[:, j, i * P:(i + 1) * P], xin[p][:, i, j * P:(j + 1) * P],
                                              c["ident"][:])
                        mm.then_inc(xT_psum, 1)
                    for j in range(DT):
                        pe.wait_ge((xT_a, xT_v)[j], n + 2)
                    for r in range(4):
                        wt = w[("wq", "wk")[r // 2]]
                        if layer:
                            pe.wait_ge(phi_ready, 4 * n + r + 1)
                        else:
                            pe.wait_ge(hi_ready, 4 * n + r + 1)
                            pe.wait_ge(rest_ready, 4 * n + r + 1)
                        for j in range(DT):
                            mm = pe.matmul(ps_qk[:, r, :], wt[:, j, (r % 2) * P:(r % 2 + 1) * P], xT[:, j, :],
                                           start=(j == 0), stop=(j == DT - 1))
                        mm.then_inc(qk_psum, 1)
                    for v in range(2):
                        pe.wait_ge(v_ready, 2 * n + v + 1)
                        for i in range(2):
                            for j in range(DT):
                                mm = pe.matmul(ps_v[:, v, i, :], xT[:, j, (2 * v + i) * P:(2 * v + i + 1) * P],
                                               w["wv"][:, j, :], start=(j == 0), stop=(j == DT - 1))
                        mm.then_inc(v_psum, 1)

        @block.scalar
        def _(act):
            act.sem_inc(xT_a, 1)
            act.sem_inc(hi_ready, 4)
            with act.Fori(0, B) as b:
                for p in range(PER):
                    n = PER * b + p
                    act.wait_ge(xT_psum, 2 * n + 1)
                    act.copy(xT[:, 0, :], ps_x[:, 0, :]).then_inc(xT_a, 1)
                    act.wait_ge(stored[p], 16 * (NSTORE * b + 1))
                    for r in range(4):
                        if layer:
                            act.wait_ge(neg_ready, 4 * n + r + 1)
                            act.activation(neg[r][:], neg[r][:], ACT.Exp).then_inc(exp_ready, 1)
                            act.wait_ge(phi_ready, 4 * n + r + 5)
                            src = phi[p][:, r, :]
                        else:
                            act.wait_ge(qk_psum, 4 * n + r + 1)
                            src = ps_qk[:, r, :]
                        act.copy(parts[p][0][:, r, :], src).then_inc(hi_ready, 1)

        @block.vector
        def _(dve):
            dve.sem_inc(xT_v, 1)
            dve.sem_inc(rest_ready, 4)
            dve.sem_inc(v_ready, 2)
            dve.sem_inc(phi_ready, 4)
            d = Done(dve, pads)
            for p in range(PER):
                d.did(dve.memset(vpad[p][:], 0.0))
            d.wait()
            for p in range(PER):
                d.did(dve.memset(vpad[p].rearrange("q n g (h e) -> q (n g h) e", h=HG)[:, :, DK:DK + 1], 1.0))
            d.wait()
            with dve.Fori(0, B) as b:
                for p in range(PER):
                    n = PER * b + p
                    dve.wait_ge(xT_psum, 2 * n + 2)
                    dve.tensor_copy(xT[:, 1, :], ps_x[:, 1, :]).then_inc(xT_v, 1)
                    dve.wait_ge(stored[p], 16 * (NSTORE * b + 1))
                    for r in range(4):
                        if layer:
                            dve.wait_ge(qk_psum, 4 * n + r + 1)
                            dve.wait_ge(phi_ready, 4 * n + r + 1)
                            dve.tensor_scalar(neg[r][:], ps_qk[:, r, :], 0.0, None, ALU.min).then_inc(neg_ready, 1)
                    for r in range(4):
                        if layer:
                            dve.wait_ge(exp_ready, 4 * n + r + 1)
                            dve.scalar_tensor_tensor(out=phi[p][:, r, :], in0=ps_qk[:, r, :], scalar=0.0,
                                                     in1=neg[r][:], op0=ALU.max, op1=ALU.add).then_inc(phi_ready, 1)
                            src = phi[p][:, r, :]
                        else:
                            src = ps_qk[:, r, :]
                        dve.wait_ge(hi_ready, 4 * n + r + 5)
                        dve.wait_ge(mid_ready, 8 * n + 2 * r + 2)
                        dve.tensor_tensor(rest[r][:], src, parts[p][0][:, r, :],
                                          ALU.subtract).then_inc(rest_ready, 1)
                    for v in range(2):
                        dve.wait_ge(v_psum, 2 * n + v + 1)
                        for i in range(2):
                            cp = dve.tensor_copy(
                                vpad[p][:, 2 * v + i].rearrange("q g (h e) -> q (g h) e", h=HG)[:, :, 0:DK],
                                ps_v[:, v, i, :].rearrange("q (h e) -> q h e", e=DK))
                        cp.then_inc(v_ready, 1)

        @block.gpsimd
        def _(pool):
            pool.sem_inc(mid_ready, 8)
            with pool.Fori(0, B) as b:
                for p in range(PER):
                    n = PER * b + p
                    pool.wait_ge(stored[p], 16 * (NSTORE * b + 1))
                    for r in range(4):
                        hold(pool, rest_ready, 4 * n + r + 5)
                        pool.tensor_copy(parts[p][1][:, r, :], rest[r][:]).then_inc(mid_ready, 1)
                        pool.wait_ge(mid_ready, 8 * n + 2 * r + 9)
                        pool.tensor_tensor(parts[p][2][:, r, :], rest[r][:], parts[p][1][:, r, :],
                                           ALU.subtract).then_inc(mid_ready, 1)


def attend(nc, c, dram):
    N = B * G
    NBUF = 3
    assert (N - 1) % NBUF == 0
    QT = CH // P
    HALVES = S // CH
    NLOAD = (HALVES + 1) * len(TERMS) + 1
    with ExitStack() as ctx:
        st = Stage(nc, ctx, "a")
        qop = [st.sb(f"qop{p}", [KR + 2, HALVES, HG, CH], BF16) for p in range(NBUF)]
        kop = [st.sb(f"kop{p}", [KR + 2, HG, S], BF16) for p in range(NBUF)]
        val = [st.sb(f"val{p}", [P, ST, P]) for p in range(NBUF)]
        prob = st.sb("prob", [P, 4, HG, CH])
        mlow = st.sb("mlow", [P, HG, QT])
        mpart = st.sb("mpart", [P, HG, QT, 2])
        mhigh = st.sb("mhigh", [P, HG, QT])
        mrow = [st.sb(f"mrow{h}", [HG * QT, 2, P], BF16) for h in range(HALVES)]
        o_sb = st.sb("o_sb", [P, CH])
        recip = st.sb("recip", [P, QT, HG])
        ao = [st.sb(f"ao{h}", [P, QT, FG]) for h in range(HALVES)]
        ps_1 = [st.ps(f"ps_1{i}", [P, CH]) for i in range(2)]
        ps_2 = [st.ps(f"ps_2{i}", [P, 2, CH]) for i in range(2)]
        ps_o = st.ps("ps_o", [P, CH])
        ps_t = st.ps("ps_t", [P, QT, P])
        loaded = [st.sem(f"loaded{p}") for p in range(NBUF)]
        rows_in = [st.sem(f"rows_in{h}") for h in range(HALVES)]
        ao_out = [st.sem(f"ao_out{h}") for h in range(HALVES)]
        s1, maxed = st.sem("s1"), st.sem("maxed")
        s2, exped, masked, used = st.sem("s2"), st.sem("exped"), st.sem("masked"), st.sem("used")
        o_copied, t_done = st.sem("o_copied"), st.sem("t_done")
        mrow_ready, ao_ready = st.sem("mrow_ready"), st.sem("ao_ready")
        hi_done, comb, rec, setup = st.sem("hi_done"), st.sem("comb"), st.sem("rec"), st.sem("setup")
        block = ctx.enter_context(nc.Block())

        pass1 = [(h, q, 0, (q + 1) * P) for q in range(QT) for h in range(HG)]
        for q in range(QT, ST):
            for h in range(HG):
                pass1 += [(h, q, 0, CH), (h, q, CH, (q + 1) * P - CH)]
        N1 = len(pass1)
        pass2 = [(j, k, max(j * CH, k * P), (j + 1) * CH - max(j * CH, k * P))
                 for j in range(HALVES) for k in range(QT * (j + 1))]
        N2 = len(pass2)
        diag = [n for n, (j, k, q0, w) in enumerate(pass2) if q0 == k * P]
        share = [3] * N2 + [(N1 - 3 * N2) // 2] * 2
        assert sum(share) == N1
        upto = [sum(share[:i + 1]) for i in range(len(share))]
        M_AT = (1, 7)

        def queries_done_by(n):
            return upto[n] >= QT * HG

        assert queries_done_by(M_AT[1] - 1)

        @block.sync
        def _(sp):
            def load(s, p):
                for t, (qpart, kpart) in enumerate(TERMS):
                    rows = slice(t * DK, (t + 1) * DK)
                    for x in range(HALVES):
                        src = dram["qparts0"].rearrange("k x b (g h e) t -> k x (b g) e h t", g=G, h=HG)
                        sp.dma_start(qop[p][rows, x], src[qpart, x, s]).then_inc(loaded[p], 16)
                    src = dram["kparts0"].rearrange("k b (g h e) t -> k (b g) e h t", g=G, h=HG)[kpart, s]
                    sp.dma_start(kop[p][rows], src).then_inc(loaded[p], 16)
                src = dram["values0"].rearrange("b g (n q) e -> (b g) q n e", q=P)[s]
                sp.dma_start(val[p][:], src).then_inc(loaded[p], 16)

            def rows(s, p, half):
                sp.wait_ge(mrow_ready, HALVES * s + half + 1)
                for r in range(2):
                    sp.dma_start(qop[p][KR + r:KR + r + 1, half].rearrange("o h t -> o (h t)"),
                                 mrow[half][:, r, :]).then_inc(rows_in[half], 16)

            def out(s, half):
                sp.wait_ge(ao_ready, 1 + HALVES * s + half + 1)
                dst = dram["heads0"].rearrange("b g (x n q) e -> (b g) x q n e", x=HALVES, q=P)
                sp.dma_start(dst[s, half], ao[half][:]).then_inc(ao_out[half], 16)

            def step(s, p, loads=True):
                rows(s, p, 1)
                out(s, 0)
                rows(s + 1, (p + 1) % NBUF, 0)
                out(s, 1)
                if loads:
                    sp.wait_ge(used, 4 + N2 * (s + 1))
                    load(s + NBUF, p)

            for h in range(HALVES):
                sp.sem_inc(ao_out[h], 16)
                sp.sem_inc(rows_in[h], 32)
            for p in range(NBUF):
                load(p, p)
            rows(0, 0, 0)
            with sp.Fori(0, (N - 1) // NBUF - 1) as j:
                for p in range(NBUF):
                    step(j * NBUF + p, p)
            for s in range(N - 1 - NBUF, N - 1):
                step(s, s % NBUF, loads=(s + NBUF < N))
            rows(N - 1, (N - 1) % NBUF, 1)
            out(N - 1, 0)
            out(N - 1, 1)
            for h in range(HALVES):
                sp.wait_ge(ao_out[h], 16 * (N + 1))

        @block.tensor
        def _(pe):
            def scores1(s, p, i, first=False):
                h, q, k0, kn = pass1[i]
                if not (first and i < 2):
                    pe.wait_ge(maxed, N1 * s + i - 1)
                dst = ps_1[i % 2][:, 0:kn]
                last = k0 + kn == (q + 1) * P
                mm = pe.matmul(dst, qop[p][0:KR, q // QT, h, (q % QT) * P:(q % QT + 1) * P], kop[p][0:KR, h, k0:k0 + kn],
                               start=True, stop=not last)
                if last:
                    mm = pe.matmul(dst[:, kn - P:kn], c["identb"][:], c["future"][:], start=False, stop=True)
                mm.then_inc(s1, 1)

            def scores2(s, p, n):
                j, k, q0, w = pass2[n]
                if n == 0 or pass2[n - 1][0] != j:
                    pe.wait_ge(rows_in[j], 32 * (s + 2))
                for u in range(2):
                    pe.wait_ge(exped, 2 * (N2 * s + n) + u + 1)
                    for h in range(2):
                        mm = pe.matmul(ps_2[u][:, h, 0:w], kop[p][:, 2 * u + h, k * P:(k + 1) * P],
                                       qop[p][:, j, 2 * u + h, q0 - j * CH:q0 - j * CH + w], start=True, stop=True)
                    mm.then_inc(s2, 1)

            def values(s, p, n):
                j, k, q0, w = pass2[n]
                last = k == QT * (j + 1) - 1
                if k == 0:
                    pe.wait_ge(o_copied, HALVES * s + j + 1)
                pe.wait_ge(exped, 2 * (N2 * s + n) + 4)
                if n in diag:
                    pe.wait_ge(masked, len(diag) * s + diag.index(n) + 1)
                o0 = q0 - j * CH
                for h in range(HG):
                    sl = slice(h * STRIP, (h + 1) * STRIP)
                    mm = pe.matmul(ps_o[sl, o0:o0 + w], val[p][:, k, sl], prob[:, n % 4, h, 0:w],
                                   start=(k == 0), stop=last)
                mm.then_inc(used, 1)

            def turn_heads(s, j, after_rows=True):
                pe.wait_ge(o_copied, HALVES * s + j + 2)
                if after_rows:
                    pe.wait_ge(mrow_ready, HALVES * s + j + 2)
                else:
                    pe.wait_ge(ao_ready, 1 + HALVES * s + 1)
                for i in range(QT):
                    mm = pe.transpose(ps_t[:, i, :], o_sb[:, i * P:(i + 1) * P], c["ident"][:])
                mm.then_inc(t_done, 1)

            def turn_max(s, half):
                if half:
                    pe.wait_ge(comb, s + 1)
                    pe.wait_ge(mrow_ready, HALVES * s + 1)
                else:
                    pe.wait_ge(maxed, N1 * s + QT * HG)
                pe.wait_ge(ao_ready, HALVES * s + (1 if half else 0))
                m = (mlow, mhigh)[half].rearrange("p h q -> p (h q)")
                pe.transpose(ps_t[0:HG * QT, 0, :], m, c["ident"][:]).then_inc(t_done, 1)

            def step(s, p, ahead=True):
                pn = (p + 1) % NBUF
                done = 0

                def pass1_units(i):
                    nonlocal done
                    if ahead:
                        for u in range(done, upto[i]):
                            scores1(s + 1, pn, u)
                        done = upto[i]

                for n in range(N2):
                    scores2(s, p, n)
                    if n == M_AT[0]:
                        turn_max(s, 1)
                    if n == 6:
                        turn_heads(s, 0)
                    if n == M_AT[1] and ahead:
                        turn_max(s + 1, 0)
                    pass1_units(n)
                    if n >= 2:
                        values(s, p, n - 2)
                for n in (N2 - 2, N2 - 1):
                    pass1_units(n + 2)
                    values(s, p, n)
                turn_heads(s, 1, after_rows=ahead)

            pe.sem_inc(used, 4)
            pe.wait_ge(setup, 1)
            pe.wait_ge(loaded[0], 16 * NLOAD)
            for i in range(N1):
                scores1(0, 0, i, first=True)
            pe.wait_ge(maxed, QT * HG)
            pe.transpose(ps_t[0:HG * QT, 0, :], mlow.rearrange("p h q -> p (h q)"), c["ident"][:]).then_inc(t_done, 1)
            with pe.Fori(0, (N - 1) // NBUF) as j:
                for p in range(NBUF):
                    pe.wait_ge(loaded[(p + 1) % NBUF], 16 * NLOAD * (j + 1 + (p + 1) // NBUF))
                    step(j * NBUF + p, p)
            step(N - 1, (N - 1) % NBUF, ahead=False)

        @block.scalar
        def _(act):
            def step(s):
                for n, (j, k, q0, w) in enumerate(pass2):
                    act.wait_ge(used, N2 * s + n + 1)
                    for u in range(2):
                        act.wait_ge(s2, 2 * (N2 * s + n) + u + 1)
                        act.activation(prob[:, n % 4, 2 * u:2 * u + 2, 0:w], ps_2[u][:, :, 0:w], ACT.Exp,
                                       scale=DK ** -0.5).then_inc(exped, 1)

            act.sem_inc(exped, 2)
            with act.Fori(0, N) as s:
                step(s)

        @block.gpsimd
        def _(pool):
            with pool.Fori(0, N) as s:
                for n in diag:
                    hold(pool, exped, 2 * (N2 * s + n) + 4)
                    blk = prob[:, n % 4, :, 0:P]
                    pool.affine_select(out=blk, in_=blk, compare_op=ALU.is_ge, fill=0.0, base=0,
                                       pattern=[[0, HG], [1, P]], channel_multiplier=-1).then_inc(masked, 1)

        @block.vector
        def _(dve):
            def maxima(s, i):
                h, q, k0, kn = pass1[i]
                dst = mlow[:, h, q:q + 1] if q < QT else mpart[:, h, q - QT, k0 // CH:k0 // CH + 1]
                dve.wait_ge(s1, N1 * s + i + 1)
                dve.tensor_reduce(dst, ps_1[i % 2][:, 0:kn], AX.X, ALU.max).then_inc(maxed, 1)

            def combine(s):
                dve.wait_ge(maxed, N1 * (s + 1))
                dve.tensor_reduce(mhigh[:], mpart[:], AX.X, ALU.max).then_inc(comb, 1)

            def make_rows(s, half, n_t):
                dve.wait_ge(t_done, n_t)
                dve.wait_ge(rows_in[half], 32 * (s + 1))
                src = ps_t[0:HG * QT, 0, :]
                dve.tensor_scalar(mrow[half][:, 0, :], src, -1.0, None, ALU.mult).then_inc(hi_done, 1)
                dve.wait_ge(hi_done, HALVES * s + half + 1)
                dve.scalar_tensor_tensor(out=mrow[half][:, 1, :], in0=src, scalar=-1.0, in1=mrow[half][:, 0, :],
                                         op0=ALU.mult, op1=ALU.subtract).then_inc(mrow_ready, 1)

            def copy_heads(s, j):
                dve.wait_ge(used, 4 + N2 * s + QT * (1, 3)[j])
                dve.tensor_copy(o_sb[:], ps_o[:]).then_inc(o_copied, 1)

            def divide(s, j, n_t):
                dve.wait_ge(t_done, n_t)
                heads = ps_t.rearrange("p n (h e) -> p n h e", h=HG)
                dve.reciprocal(recip[:], heads[:, :, :, DK]).then_inc(rec, 1)
                dve.wait_ge(rec, HALVES * s + j + 1)
                dve.wait_ge(ao_out[j], 16 * (s + 1))
                for i in range(QT):
                    ins = dve.tensor_tensor(ao[j][:, i, :].rearrange("p (h e) -> p h e", h=HG),
                                            heads[:, i, :, 0:DK],
                                            recip[:, i, :].unsqueeze(2).to_broadcast([P, HG, DK]), ALU.mult)
                ins.then_inc(ao_ready, 1)

            def step(s, ahead=True):
                done = 0

                def units(i):
                    nonlocal done
                    if ahead:
                        for u in range(done, upto[i]):
                            maxima(s + 1, u)
                        done = upto[i]

                for n in range(N2):
                    if n == M_AT[0]:
                        make_rows(s, 1, 4 * s + 2)
                    if n == 6:
                        copy_heads(s, 0)
                        divide(s, 0, 4 * s + 3)
                    if n == M_AT[1] and ahead:
                        make_rows(s + 1, 0, 4 * s + 4)
                    units(n)
                for n in (N2, N2 + 1):
                    units(n)
                if ahead:
                    combine(s + 1)
                copy_heads(s, 1)
                divide(s, 1, 4 * s + (5 if ahead else 4))

            dve.sem_inc(o_copied, 1)
            dve.sem_inc(ao_ready, 1)
            for p in range(NBUF):
                ins = dve.memset(kop[p][KR:KR + 2, :, :], 1.0)
            ins.then_inc(setup, 1)
            for i in range(N1):
                maxima(0, i)
            make_rows(0, 0, 1)
            combine(0)
            with dve.Fori(0, N - 1) as s:
                step(s)
            step(N - 1, ahead=False)


def attend_linear(nc, c, dram):
    N = B * G
    QT = CH // P
    HALVES = S // CH
    NLOAD = 2 * len(TERMS) + 3
    with ExitStack() as ctx:
        st = Stage(nc, ctx, "l")
        qop = [st.sb(f"qop{p}", [KR, HG, S], BF16) for p in range(2)]
        kop = [st.sb(f"kop{p}", [KR, HG, S], BF16) for p in range(2)]
        val = [st.sb(f"val{p}", [P, ST, P]) for p in range(2)]
        qf = [st.sb(f"qf{p}", [FG, S]) for p in range(2)]
        kf = [st.sb(f"kf{p}", [FG, S]) for p in range(2)]
        kt = [st.sb(f"kt{p}", [P, ST, FG]) for p in range(2)]
        att = [st.sb(f"att{i}", [P, HG, P]) for i in range(2)]
        state = [st.sb(f"state{i}", [FG, P]) for i in range(2)]
        o_sb = st.sb("o_sb", [P, CH])
        den = st.sb("den", [P, QT, HG])
        ao = [st.sb(f"ao{h}", [P, QT, FG]) for h in range(HALVES)]
        ps_a = [st.ps(f"ps_a{i}", [P, HG, P]) for i in range(2)]
        ps_o = [st.ps(f"ps_o{i}", [P, CH]) for i in range(2)]
        ps_s = st.ps("ps_s", [FG, P])
        ps_t = st.ps("ps_t", [P, QT, P])
        ps_k = st.ps("ps_k", [P, ST, FG])
        loaded = [st.sem(f"loaded{p}") for p in range(2)]
        ao_out = [st.sem(f"ao_out{h}") for h in range(HALVES)]
        k_turned, k_copied = st.sem("k_turned"), st.sem("k_copied")
        scored, att_ready = st.sem("scored"), st.sem("att_ready")
        state_sum, state_ready = st.sem("state_sum"), st.sem("state_ready")
        o_done, o_copied = st.sem("o_done"), st.sem("o_copied")
        t_done, den_ready, ao_ready = st.sem("t_done"), st.sem("den_ready"), st.sem("ao_ready")
        block = ctx.enter_context(nc.Block())

        @block.sync
        def _(sp):
            def load(s, p):
                for t, (qpart, kpart) in enumerate(TERMS):
                    rows = slice(t * DK, (t + 1) * DK)
                    for op, name, part in ((qop, "qparts1", qpart), (kop, "kparts1", kpart)):
                        src = dram[name].rearrange("k b (g h e) t -> k (b g) e h t", g=G, h=HG)[part, s]
                        sp.dma_start(op[p][rows], src).then_inc(loaded[p], 16)
                sp.dma_start(val[p][:], dram["values1"].rearrange("b g (n q) e -> (b g) q n e", q=P)[s])\
                  .then_inc(loaded[p], 16)
                for op, name in ((qf, "qfull"), (kf, "kfull")):
                    src = dram[name].rearrange("b (g f) t -> (b g) f t", g=G)
                    sp.dma_start(op[p][:], src[s]).then_inc(loaded[p], 16)

            def out(s, half):
                sp.wait_ge(ao_ready, 1 + HALVES * s + half + 1)
                dst = dram["heads1"].rearrange("b g (x n q) e -> (b g) x q n e", x=HALVES, q=P)
                sp.dma_start(dst[s, half], ao[half][:]).then_inc(ao_out[half], 16)

            for h in range(HALVES):
                sp.sem_inc(ao_out[h], 16)
            for p in range(2):
                load(p, p)
            with sp.Fori(0, N // 2 - 1) as j:
                for p in range(2):
                    s = 2 * j + p
                    out(s, 0)
                    out(s, 1)
                    load(s + 2, p)
            for s in (N - 2, N - 1):
                out(s, 0)
                out(s, 1)
            for h in range(HALVES):
                sp.wait_ge(ao_out[h], 16 * (N + 1))

        @block.tensor
        def _(pe):
            with pe.Fori(0, N // 2) as j:
                for p in range(2):
                    s = 2 * j + p

                    def scores(n):
                        pe.wait_ge(att_ready, ST * s + n + 1)
                        for h in range(HG):
                            mm = pe.matmul(ps_a[n % 2][:, h, :], kop[p][:, h, n * P:(n + 1) * P],
                                           qop[p][:, h, n * P:(n + 1) * P], start=True, stop=True)
                        mm.then_inc(scored, 1)

                    def add_state(n):
                        pe.wait_ge(state_ready, (ST - 1) * s + n + 1)
                        pe.matmul(ps_s[:], kt[p][:, n, :], val[p][:, n, :], start=(n == 0), stop=True,
                                  skip_group_check=True).then_inc(state_sum, 1)

                    def outputs(n):
                        half, o0 = n // QT, (n % QT) * P
                        if n % QT == 0:
                            pe.wait_ge(o_copied, HALVES * s + half + 1)
                        if n:
                            pe.wait_ge(state_ready, (ST - 1) * s + n + 1)
                            pe.matmul(ps_o[half][:, o0:o0 + P], state[n % 2][:], qf[p][:, n * P:(n + 1) * P],
                                      start=True, stop=False)
                        pe.wait_ge(att_ready, ST * s + n + 3)
                        for h in range(HG):
                            sl = slice(h * STRIP, (h + 1) * STRIP)
                            mm = pe.matmul(ps_o[half][sl, o0:o0 + P], val[p][:, n, sl], att[n % 2][:, h, :],
                                           start=(n == 0), stop=True)
                        mm.then_inc(o_done, 1)

                    def turn(half):
                        pe.wait_ge(o_copied, HALVES * s + half + 3)
                        pe.wait_ge(ao_ready, HALVES * s + half + 1)
                        for i in range(QT):
                            mm = pe.transpose(ps_t[:, i, :], o_sb[:, i * P:(i + 1) * P], c["ident"][:])
                        mm.then_inc(t_done, 1)

                    pe.wait_ge(loaded[p], 16 * NLOAD * (j + 1))
                    hold(pe, k_copied, s + 1)
                    for i in range(ST):
                        mm = pe.transpose(ps_k[:, i, :], kf[p][:, i * P:(i + 1) * P], c["ident"][0:FG, 0:FG])
                    mm.then_inc(k_turned, 1)
                    scores(0)
                    pe.wait_ge(k_copied, s + 2)
                    add_state(0)
                    for n in range(ST):
                        if n + 1 < ST:
                            scores(n + 1)
                            if n:
                                add_state(n)
                        outputs(n)
                        if n == QT + 1:
                            turn(0)
                    turn(1)

        @block.scalar
        def _(act):
            act.sem_inc(k_copied, 1)
            act.sem_inc(o_copied, 2)
            with act.Fori(0, N // 2) as j:
                for p in range(2):
                    s = 2 * j + p
                    act.wait_ge(k_turned, s + 1)
                    act.copy(kt[p][:], ps_k[:]).then_inc(k_copied, 1)
                    for half in range(HALVES):
                        act.wait_ge(o_done, ST * s + QT * (half + 1))
                        act.wait_ge(ao_ready, HALVES * s + half + 1)
                        act.copy(o_sb[:], ps_o[half][:]).then_inc(o_copied, 1)

        @block.vector
        def _(dve):
            dve.sem_inc(att_ready, 2)
            dve.sem_inc(state_ready, 1)
            dve.sem_inc(ao_ready, 1)
            with dve.Fori(0, N // 2) as j:
                for p in range(2):
                    s = 2 * j + p

                    def mask(n):
                        dve.wait_ge(scored, ST * s + n + 1)
                        dve.tensor_tensor(att[n % 2][:], ps_a[n % 2][:],
                                          c["past"][:].unsqueeze(1).to_broadcast([P, HG, P]),
                                          ALU.mult).then_inc(att_ready, 1)

                    def keep_state(n):
                        dve.wait_ge(state_sum, (ST - 1) * s + n + 1)
                        dve.tensor_tensor(state[(n + 1) % 2][:], ps_s[:], c["own"][:],
                                          ALU.mult).then_inc(state_ready, 1)

                    def divide(half):
                        dve.wait_ge(t_done, HALVES * s + half + 1)
                        heads = ps_t.rearrange("p n (h e) -> p n h e", h=HG)
                        dve.tensor_scalar(den[:], heads[:, :, :, DK], EPS, None, ALU.add).then_inc(den_ready, 1)
                        dve.wait_ge(den_ready, 2 * (HALVES * s + half) + 1)
                        dve.reciprocal(den[:], den[:]).then_inc(den_ready, 1)
                        dve.wait_ge(den_ready, 2 * (HALVES * s + half) + 2)
                        dve.wait_ge(ao_out[half], 16 * (s + 1))
                        for i in range(QT):
                            ins = dve.tensor_tensor(ao[half][:, i, :].rearrange("p (h e) -> p h e", h=HG),
                                                    heads[:, i, :, 0:DK],
                                                    den[:, i, :].unsqueeze(2).to_broadcast([P, HG, DK]), ALU.mult)
                        ins.then_inc(ao_ready, 1)

                    mask(0)
                    keep_state(0)
                    for n in range(ST):
                        if n + 1 < ST:
                            mask(n + 1)
                            if n:
                                keep_state(n)
                        if n == QT + 1:
                            divide(0)
                    divide(1)


NT = CH // P
UNITS = T // CH
NORM_OPS = 3 * NT + 5


class Norm:

    def __init__(self, st, halves=1):
        self.stats = st.sb("stats", [P, NT, 6])
        self.mv = st.sb("mv", [P, NT, 2])
        self.ve = st.sb("ve", [P, NT])
        self.sd = st.sb("sd", [P, NT])
        self.rs = st.sb("rs", [P, NT])
        self.tmp = st.sb("ntmp", [P, NT])
        self.var_ready, self.sqrt_ready = st.sem("var_ready"), st.sem("sqrt_ready")

    def vector(self, dve, d, u, res, y):
        for i in range(NT):
            d.did(dve.bn_stats(self.stats[:, i, :], res[:, i, :]))
        d.hold()
        for i in range(NT):
            d.did(dve.bn_aggr(self.mv[:, i, :], self.stats[:, i, :]))
        d.wait()
        dve.tensor_scalar(self.ve[:], self.mv[:, :, 1], EPS, None, ALU.add).then_inc(self.var_ready, 1)
        dve.wait_ge(self.sqrt_ready, u + 1)
        d.did(dve.reciprocal(self.rs[:], self.sd[:]))
        d.wait()
        d.did(dve.tensor_tensor(self.tmp[:], self.rs[:], self.rs[:], ALU.mult))
        d.wait()
        d.did(dve.tensor_tensor(self.tmp[:], self.tmp[:], self.ve[:], ALU.mult))
        d.wait()
        d.did(dve.tensor_scalar(self.tmp[:], self.tmp[:], -0.5, 1.5, ALU.mult, ALU.add))
        d.wait()
        d.did(dve.tensor_tensor(self.rs[:], self.rs[:], self.tmp[:], ALU.mult))
        d.wait()
        for i in range(NT):
            d.did(dve.tensor_scalar(y[:, i, :], res[:, i, :], self.mv[:, i, 0:1], self.rs[:, i:i + 1],
                                    ALU.subtract, ALU.mult))

    def scalar(self, act, u):
        act.wait_ge(self.var_ready, u + 1)
        act.activation(self.sd[:], self.ve[:], ACT.Sqrt).then_inc(self.sqrt_ready, 1)



def route(nc, ctx, c, w, ins, dram, x_dram, layer):
    rt = ROUTERS[layer]
    E, K, C = rt["E"], rt["K"], rt["C"]
    keep = Stage(nc, ctx, f"k{layer}")
    gidx = keep.sb("gidx", [P, UNITS, NT, K], I32)
    gate = keep.sb("gate", [P, UNITS, NT, K])
    with ExitStack() as tmp:
        st = Stage(nc, tmp, f"r{layer}")
        ao = [st.sb(f"ao{p}", [P, NT, G, FG]) for p in range(2)]
        xr = [st.sb(f"xr{p}", [P, NT, D]) for p in range(2)]
        tT = st.sb("tT", [P, DT, CH])
        res = st.sb("res", [P, NT, D])
        y = [st.sb(f"y{p}", [P, NT, D]) for p in range(2)]
        gw = st.sb("gw", [P, DT, E])
        gb = st.sb("gb", [P, E])
        bo = st.sb("bo", [P, D])
        lg = st.sb("lg", [P, NT, E])
        mx = st.sb("mx", [P, NT])
        top = st.sb("top", [P, NT, 8])
        topi = st.sb("topi", [P, NT, 8], U32)
        topf = st.sb("topf", [P, NT, 8])
        hot = [st.sb(f"hot{k}", [P, NT, E]) for k in range(K)]
        chosen = st.sb("chosen", [P, NT, E])
        chosenb = st.sb("chosenb", [P, NT, E], BF16)
        unit_sum = st.sb("unit_sum", [P, E])
        count = st.sb("count", [P, E], BF16)
        over = st.sb("over", [P, NT, E])
        slot = st.sb("slot", [P, NT, K])
        valid = st.sb("valid", [P, NT, K])
        ex = st.sb("ex", [P, NT, K if layer == 0 else E])
        sm = st.sb("sm", [P, NT])
        sidx = [st.sb(f"sidx{p}", [P, NT, K], I32) for p in range(2)]
        norm = Norm(st)
        ps_t = st.ps("ps_t", [P, DT, CH])
        ps_w = st.ps("ps_w", [P, 2, 2, D])
        ps_l = st.ps("ps_l", [P, NT, E])
        ps_p = st.ps("ps_p", [P, NT, E])
        setup, setup_v = st.sem("setup"), st.sem("setup_v")
        loaded = [st.sem(f"loaded{p}") for p in range(2)]
        scattered = [st.sem(f"scattered{p}") for p in range(2)]
        stored = [st.sem(f"stored{p}") for p in range(2)]
        turned, copied_a, copied_v = st.sem("turned"), st.sem("copied_a"), st.sem("copied_v")
        out_done, res_done, biased = st.sem("out_done"), st.sem("res_done"), st.sem("biased")
        y_ready, logit_done, logit_read = st.sem("y_ready"), st.sem("logit_done"), st.sem("logit_read")
        exp_in, exp_done = st.sem("exp_in"), st.sem("exp_done")
        chosen_ready, pos_done, count_ready = st.sem("chosen_ready"), st.sem("pos_done"), st.sem("count_ready")
        sidx_ready, own, y_free = st.sem("sidx_ready"), st.sem("own"), st.sem("y_free")
        block = tmp.enter_context(nc.Block())
        NLOAD = G + 1

        @block.sync
        def _(sp):
            def load(b, p):
                src = dram[f"heads{layer}"].rearrange("b g (x n q) e -> b x g q n e", x=2, q=P)
                for g in range(G):
                    sp.dma_start(ao[p][:, :, g, :], src[b, p, g]).then_inc(loaded[p], 16)
                src = x_dram.rearrange("(b x n q) d -> b x q n d", b=B, x=2, q=P)
                sp.dma_start(xr[p][:], src[b, p]).then_inc(loaded[p], 16)

            def store(b, p):
                sp.wait_ge(y_ready, 2 * b + p + 1)
                dst = dram[f"normed{layer}"].rearrange("(b x n q) d -> b x q n d", b=B, x=2, q=P)
                sp.dma_start(dst[b, p], y[p][:]).then_inc(stored[p], 16)

            sp.dma_start(gw[:], ins[f"gate{layer}"].rearrange("(j q) e -> q j e", q=P)).then_inc(setup, 16)
            sp.dma_start(gb[:], ins[f"gbias{layer}"].rearrange("(o e) -> o e", o=1).to_broadcast([P, E]))\
              .then_inc(setup, 16)
            if layer:
                sp.dma_start(bo[:], ins["bo1"].rearrange("(o d) -> o d", o=1).to_broadcast([P, D]))\
                  .then_inc(setup, 16)
            for p in range(2):
                sp.sem_inc(stored[p], 16)
                load(0, p)
            with sp.Fori(0, B - 1) as b:
                for p in range(2):
                    store(b, p)
                    sp.wait_ge(res_done, 2 * b + p + 1)
                    load(b + 1, p)
            for p in range(2):
                store(B - 1, p)
            for p in range(2):
                sp.wait_ge(stored[p], 16 * (B + 1))

        @block.tensor
        def _(pe):
            pe.wait_ge(setup, 16 * (3 if layer else 2))
            with pe.Fori(0, B) as b:
                for p in range(2):
                    u = 2 * b + p
                    pe.wait_ge(loaded[p], 16 * NLOAD * (b + 1))
                    aot = ao[p].rearrange("q n g e -> q n (g e)")
                    for half, src in enumerate((aot, y[p])):
                        if half:
                            pe.wait_ge(y_ready, u + 1)
                        for j in range(DT):
                            pe.wait_ge((copied_a, copied_v)[j], 2 * u + half + 1)
                            for i in range(NT):
                                mm = pe.transpose(ps_t[:, j, i * P:(i + 1) * P], src[:, i, j * P:(j + 1) * P],
                                                  c["ident"][:])
                            mm.then_inc(turned, 1)
                        for j in range(DT):
                            pe.wait_ge((copied_a, copied_v)[j], 2 * u + half + 2)
                        if half == 0:
                            for i in range(NT):
                                for j in range(DT):
                                    mm = pe.matmul(ps_w[:, i // 2, i % 2, :], tT[:, j, i * P:(i + 1) * P],
                                                   w["wo"][:, j, :], start=(j == 0), stop=(j == DT - 1))
                            mm.then_inc(out_done, 1)
                        else:
                            for i in range(NT):
                                for j in range(DT):
                                    mm = pe.matmul(ps_l[:, i, :], tT[:, j, i * P:(i + 1) * P], gw[:, j, :],
                                                   start=(j == 0), stop=(j == DT - 1))
                            mm.then_inc(logit_done, 1)
                    pe.wait_ge(chosen_ready, u + 1)
                    pe.wait_ge(count_ready, u + 1)
                    for i in range(NT):
                        pe.matmul(ps_p[:, i, :], c["before"][:], chosenb[:, i, :], start=True, stop=False)
                        for o in range(i):
                            pe.matmul(ps_p[:, i, :], c["ones"][:], chosenb[:, o, :], start=False, stop=False)
                        mm = pe.matmul(ps_p[:, i, :], c["ones"][:], count[:], start=False, stop=True)
                    mm.then_inc(pos_done, 1)

        @block.scalar
        def _(act):
            act.sem_inc(copied_a, 1)
            with act.Fori(0, B) as b:
                for p in range(2):
                    u = 2 * b + p
                    act.wait_ge(turned, 4 * u + 1)
                    act.copy(tT[:, 0, :], ps_t[:, 0, :]).then_inc(copied_a, 1)
                    norm.scalar(act, u)
                    act.wait_ge(turned, 4 * u + 3)
                    act.copy(tT[:, 0, :], ps_t[:, 0, :]).then_inc(copied_a, 1)
                    act.wait_ge(exp_in, u + 1)
                    act.activation(ex[:], ex[:], ACT.Exp).then_inc(exp_done, 1)

        @block.gpsimd
        def _(pool):
            if layer:
                pool.wait_ge(setup, 48)
            with pool.Fori(0, B) as b:
                for p in range(2):
                    u = 2 * b + p
                    if layer:
                        pool.wait_ge(loaded[p], 16 * NLOAD * (b + 1))
                        for i in range(NT):
                            add = pool.tensor_tensor(xr[p][:, i, :], xr[p][:, i, :], bo[:], ALU.add)
                        add.then_inc(biased, 1)
                    hold(pool, sidx_ready, u + 1)
                    for i in range(NT):
                        for k in range(K):
                            pool.indirect_dma_start(
                                dram[f"slots{layer}"], bass.IndirectOffsetOnAxis(ap=sidx[p][:, i, k:k + 1], axis=0),
                                y[p][:, i, :], None, bounds_check=E * C - 1, oob_is_err=False)\
                                .then_inc(scattered[p], 16)
                    pool.wait_ge(scattered[p], 16 * NT * K * (b + 1))
                    pool.sem_inc(y_free, 1)

        @block.vector
        def _(dve):
            dve.sem_inc(copied_v, 1)
            dve.sem_inc(y_free, 2)
            dve.memset(count[:], 0.0).then_inc(count_ready, 1)
            dve.wait_ge(setup, 16 * (3 if layer else 2))
            NOWN = NORM_OPS + (32 if layer == 0 else 29)
            with dve.Fori(0, B) as b:
                for p in range(2):
                    u = 2 * b + p
                    d = Done(dve, own, u * NOWN)

                    def then(ins):
                        d.did(ins)
                        d.wait()

                    dve.wait_ge(turned, 4 * u + 2)
                    dve.tensor_copy(tT[:, 1, :], ps_t[:, 1, :]).then_inc(copied_v, 1)
                    dve.wait_ge(out_done, u + 1)
                    dve.wait_ge(loaded[p], 16 * NLOAD * (b + 1))
                    if layer:
                        dve.wait_ge(biased, u + 1)
                    dve.tensor_tensor(res.rearrange("q n d -> q (n d)"), ps_w.rearrange("q a i d -> q (a i d)"),
                                      xr[p].rearrange("q n d -> q (n d)"), ALU.add).then_inc(res_done, 1)
                    dve.wait_ge(res_done, u + 1)
                    dve.wait_ge(stored[p], 16 * (b + 1))
                    hold(dve, y_free, u + 1)
                    norm.vector(dve, d, u, res, y[p])
                    d.wait()
                    dve.sem_inc(y_ready, 1)
                    dve.wait_ge(turned, 4 * u + 4)
                    dve.tensor_copy(tT[:, 1, :], ps_t[:, 1, :]).then_inc(copied_v, 1)
                    dve.wait_ge(logit_done, u + 1)
                    then(dve.tensor_tensor(lg[:], ps_l[:], gb[:].unsqueeze(1).to_broadcast([P, NT, E]), ALU.add))
                    if layer:
                        then(dve.tensor_reduce(mx[:], lg[:], AX.X, ALU.max))
                        dve.tensor_tensor(ex[:], lg[:], mx[:].unsqueeze(2).to_broadcast([P, NT, E]),
                                          ALU.subtract).then_inc(exp_in, 1)
                        dve.wait_ge(exp_done, u + 1)
                        then(dve.tensor_reduce(sm[:], ex[:], AX.X, ALU.add))
                        then(dve.reciprocal(sm[:], sm[:]))
                        then(dve.tensor_tensor(lg[:], ex[:], sm[:].unsqueeze(2).to_broadcast([P, NT, E]), ALU.mult))
                    d.hold()
                    for i in range(NT):
                        d.did(dve.max(top[:, i, :], lg[:, i, :]))
                    d.hold()
                    for i in range(NT):
                        d.did(dve.max_index(topi[:, i, :], top[:, i, :], lg[:, i, :]))
                    d.wait()
                    if not layer:
                        dve.tensor_tensor(ex[:], top[:, :, 0:K], top[:, :, 0:1].to_broadcast([P, NT, K]),
                                          ALU.subtract).then_inc(exp_in, 1)
                    then(dve.tensor_copy(topf[:], topi[:]))
                    for k in range(K):
                        d.did(dve.tensor_tensor(hot[k][:], c[f"expert{layer}"][:].unsqueeze(1).to_broadcast([P, NT, E]),
                                                topf[:, :, k:k + 1].to_broadcast([P, NT, E]), ALU.is_equal))
                    d.wait()
                    then(dve.tensor_tensor(chosen[:], hot[0][:], hot[1][:], ALU.add))
                    for k in range(2, K):
                        then(dve.tensor_tensor(chosen[:], chosen[:], hot[k][:], ALU.add))
                    dve.tensor_copy(chosenb[:], chosen[:]).then_inc(chosen_ready, 1)
                    then(dve.tensor_reduce(unit_sum[:], chosen.rearrange("q n e -> q e n"), AX.X, ALU.add))
                    dve.wait_ge(pos_done, u + 1)
                    dve.tensor_tensor(count[:], count[:], unit_sum[:], ALU.add).then_inc(count_ready, 1)
                    then(dve.tensor_scalar(over[:], ps_p[:], float(C), BIG, ALU.is_ge, ALU.mult))
                    then(dve.tensor_tensor(over[:], over[:], ps_p[:], ALU.add))
                    then(dve.tensor_tensor(over[:], over[:], c[f"first{layer}"][:].unsqueeze(1).to_broadcast([P, NT, E]),
                                           ALU.add))
                    for k in range(K):
                        d.did(dve.tensor_tensor(hot[k][:], hot[k][:], over[:], ALU.mult))
                    d.wait()
                    for k in range(K):
                        d.did(dve.tensor_reduce(slot[:, :, k], hot[k][:], AX.X, ALU.add))
                    d.wait()
                    dve.tensor_copy(sidx[p][:], slot[:]).then_inc(sidx_ready, 1)
                    then(dve.tensor_scalar(valid[:], slot[:], BIG, None, ALU.is_lt))
                    then(dve.tensor_tensor(slot[:], slot[:], valid[:], ALU.mult))
                    d.did(dve.tensor_copy(gidx[:, u], slot[:]))
                    if layer:
                        then(dve.tensor_tensor(gate[:, u], top[:, :, 0:K], valid[:], ALU.mult))
                    else:
                        dve.wait_ge(exp_done, u + 1)
                        then(dve.tensor_reduce(sm[:], ex[:], AX.X, ALU.add))
                        then(dve.reciprocal(sm[:], sm[:]))
                        then(dve.tensor_tensor(valid[:], valid[:], sm[:].unsqueeze(2).to_broadcast([P, NT, K]), ALU.mult))
                        then(dve.tensor_tensor(gate[:, u], ex[:], valid[:], ALU.mult))
                    assert d.n == NOWN, (d.n, NOWN)
    return gidx, gate


def experts(nc, c, ins, dram, layer):
    rt = ROUTERS[layer]
    E, C = rt["E"], rt["C"]
    TL = C // P
    with ExitStack() as ctx:
        st = Stage(nc, ctx, f"e{layer}")
        w1 = [st.sb(f"w1_{p}", [P, DT, F]) for p in range(2)]
        w2 = [st.sb(f"w2_{p}", [P, FT, D]) for p in range(2)]
        b2 = [st.sb(f"b2_{p}", [P, D]) for p in range(2)]
        b1 = st.sb("b1", [P, E, FT])
        xs = [st.sb(f"xs{p}", [P, TL, D]) for p in range(2)]
        xT = [st.sb(f"xT{t}", [P, DT, P]) for t in range(2)]
        hT = [st.sb(f"hT{t}", [P, FT, P]) for t in range(2)]
        ys = [st.sb(f"ys{p}", [P, TL, D]) for p in range(2)]
        ps_x = st.ps("ps_x", [P, DT, P])
        ps_h = [[st.ps(f"ps_h{t}{i}", [P, FT // 2, P]) for i in range(2)] for t in range(2)]
        ps_y = [st.ps(f"ps_y{t}", [P, D]) for t in range(2)]
        b1_in = st.sem("b1_in")
        x_in = [st.sem(f"x_in{p}") for p in range(2)]
        w1_in = [st.sem(f"w1_in{p}") for p in range(2)]
        w2_in = [st.sem(f"w2_in{p}") for p in range(2)]
        stored = [st.sem(f"stored{p}") for p in range(2)]
        x_turned, x_copied = st.sem("x_turned"), st.sem("x_copied")
        hid_done, gelu_done = st.sem("hid_done"), st.sem("gelu_done")
        y_done, y_ready = st.sem("y_done"), st.sem("y_ready")
        block = ctx.enter_context(nc.Block())

        def steps(eng, step):
            step(0, 0, 0, True)
            with eng.Fori(0, (E - 2) // 2) as j:
                step(2 * j + 1, 1, j, False)
                step(2 * j + 2, 0, j + 1, False)
            step(E - 1, 1, (E - 2) // 2, False)

        @block.sync
        def _(sp):
            def load(e, p):
                sp.dma_start(w1[p][:], ins[f"w1_{layer}"][e].rearrange("(j q) h -> q j h", q=P)).then_inc(w1_in[p], 16)
                sp.dma_start(xs[p][:], dram[f"slots{layer}"].rearrange("(e n q) d -> e q n d", e=E, q=P)[e])\
                  .then_inc(x_in[p], 16)

            def load2(e, p):
                sp.dma_start(w2[p][:], ins[f"w2_{layer}"][e].rearrange("(j q) d -> q j d", q=P)).then_inc(w2_in[p], 16)
                sp.dma_start(b2[p][:], ins[f"b2_{layer}"].rearrange("(o e) d -> e o d", o=1)[e]
                             .to_broadcast([P, D])).then_inc(w2_in[p], 16)

            def step(e, p, j, first, more=True):
                if more:
                    sp.wait_ge(hid_done, 2 * TL * (e + 1))
                    load(e + 2, p)
                    sp.wait_ge(y_ready, TL * (e + 1))
                    load2(e + 2, p)
                else:
                    sp.wait_ge(y_ready, TL * (e + 1))
                dst = dram[f"answers{layer}"].rearrange("(e n q) d -> e q n d", e=E, q=P)[e]
                sp.dma_start(dst, ys[p][:]).then_inc(stored[p], 16)

            sp.dma_start(b1[:], ins[f"b1_{layer}"]).then_inc(b1_in, 16)
            for p in range(2):
                load(p, p)
                load2(p, p)
                sp.sem_inc(stored[p], 16)
            with sp.Fori(0, (E - 2) // 2) as j:
                step(2 * j, 0, j, False)
                step(2 * j + 1, 1, j, False)
            step(E - 2, 0, 0, False, more=False)
            step(E - 1, 1, 0, False, more=False)
            for p in range(2):
                sp.wait_ge(stored[p], 16 * (E // 2 + 1))

        @block.tensor
        def _(pe):
            def second(n, t, p, j):
                pe.wait_ge(w2_in[p], 32 * (j + 1))
                pe.wait_ge(gelu_done, FT * (n + 1))
                for f in range(FT):
                    mm = pe.matmul(ps_y[t][:], hT[t][:, f, :], w2[p][:, f, :], start=(f == 0), stop=(f == FT - 1))
                mm.then_inc(y_done, 1)

            def step(e, p, j, first):
                for i in range(TL):
                    n = e * TL + i
                    t = (p + i) % 2
                    if i == 0:
                        pe.wait_ge(x_in[p], 16 * (j + 1))
                        pe.wait_ge(w1_in[p], 16 * (j + 1))
                    for k in range(DT):
                        mm = pe.transpose(ps_x[:, k, :], xs[p][:, i, k * P:(k + 1) * P], c["ident"][:])
                    mm.then_inc(x_turned, 1)
                    pe.wait_ge(x_copied, n + 1)
                    for f in range(FT):
                        for k in range(DT):
                            mm = pe.matmul(ps_h[t][f // 4][:, f % 4, :], w1[p][:, k, f * P:(f + 1) * P],
                                           xT[t][:, k, :], start=(k == 0), stop=(k == DT - 1))
                        if f % 4 == 3:
                            mm.then_inc(hid_done, 1)
                    if i:
                        second(n - 1, 1 - t, p, j)
                    elif not first:
                        second(n - 1, 1 - t, 1 - p, j if p else j - 1)

            steps(pe, step)
            second(E * TL - 1, 1, 1, (E - 2) // 2)

        @block.scalar
        def _(act):
            def step(e, p, j, first):
                for i in range(TL):
                    n = e * TL + i
                    t = (p + i) % 2
                    if not (first and i < 2):
                        act.wait_ge(y_done, n - 1)
                    for f in range(FT):
                        if f % 4 == 0:
                            hold(act, hid_done, 2 * n + f // 4 + 1)
                        act.activation(hT[t][:, f, :], ps_h[t][f // 4][:, f % 4, :], ACT.Gelu,
                                       bias=b1[:, e, f:f + 1]).then_inc(gelu_done, 1)

            act.wait_ge(b1_in, 16)
            steps(act, step)

        @block.vector
        def _(dve):
            def answer(n, t, p, i, j):
                dve.wait_ge(y_done, n + 1)
                dve.wait_ge(w2_in[p], 32 * (j + 1))
                if i == 0:
                    dve.wait_ge(stored[p], 16 * (j + 1))
                dve.tensor_tensor(ys[p][:, i, :], ps_y[t][:], b2[p][:], ALU.add).then_inc(y_ready, 1)

            def step(e, p, j, first):
                for i in range(TL):
                    n = e * TL + i
                    t = (p + i) % 2
                    dve.wait_ge(x_turned, n + 1)
                    dve.tensor_copy(xT[t][:], ps_x[:]).then_inc(x_copied, 1)
                    if i:
                        answer(n - 1, 1 - t, p, i - 1, j)
                    elif not first:
                        answer(n - 1, 1 - t, 1 - p, TL - 1, j if p else j - 1)

            steps(dve, step)
            answer(E * TL - 1, 1, 1, TL - 1, (E - 2) // 2)


def combine(nc, dram, gidx, gate, out_dram, layer):
    K = ROUTERS[layer]["K"]
    with ExitStack() as ctx:
        st = Stage(nc, ctx, f"g{layer}")
        ans = [st.sb(f"ans{p}", [P, NT, K, D]) for p in range(2)]
        gi = [st.sb(f"gi{p}", [P, NT, K], I32) for p in range(2)]
        xr = [st.sb(f"xr{p}", [P, NT, D]) for p in range(2)]
        y = [st.sb(f"y{p}", [P, NT, D]) for p in range(2)]
        norm = Norm(st)
        x_in = [st.sem(f"x_in{p}") for p in range(2)]
        gathered = [st.sem(f"gathered{p}") for p in range(2)]
        stored = [st.sem(f"stored{p}") for p in range(2)]
        summed, own, y_ready, gi_ready = st.sem("summed"), st.sem("own"), st.sem("y_ready"), st.sem("gi_ready")
        block = ctx.enter_context(nc.Block())

        @block.sync
        def _(sp):
            def load(b, p):
                src = dram[f"normed{layer}"].rearrange("(b x n q) d -> b x q n d", b=B, x=2, q=P)
                sp.dma_start(xr[p][:], src[b, p]).then_inc(x_in[p], 16)

            def store(b, p):
                sp.wait_ge(y_ready, 2 * b + p + 1)
                dst = out_dram.rearrange("(b x n q) d -> b x q n d", b=B, x=2, q=P)
                sp.dma_start(dst[b, p], y[p][:]).then_inc(stored[p], 16)

            for p in range(2):
                sp.sem_inc(stored[p], 16)
                load(0, p)
            with sp.Fori(0, B - 1) as b:
                for p in range(2):
                    store(b, p)
                    load(b + 1, p)
            for p in range(2):
                store(B - 1, p)
            for p in range(2):
                sp.wait_ge(stored[p], 16 * (B + 1))

        @block.gpsimd
        def _(pool):
            with pool.Fori(0, B) as b:
                for p in range(2):
                    u = 2 * b + p
                    hold(pool, summed, u + 1)
                    pool.tensor_copy(gi[p][:], gidx[:, u]).then_inc(gi_ready, 1)
                    hold(pool, gi_ready, u + 1)
                    for i in range(NT):
                        for k in range(K):
                            pool.indirect_dma_start(
                                ans[p][:, i, k, :], None, dram[f"answers{layer}"],
                                bass.IndirectOffsetOnAxis(ap=gi[p][:, i, k:k + 1], axis=0))\
                                .then_inc(gathered[p], 16)

        @block.scalar
        def _(act):
            with act.Fori(0, UNITS) as u:
                norm.scalar(act, u)

        @block.vector
        def _(dve):
            dve.sem_inc(summed, 2)
            NOWN = NORM_OPS + NT * (K - 1)
            with dve.Fori(0, B) as b:
                for p in range(2):
                    u = 2 * b + p
                    d = Done(dve, own, u * NOWN)
                    dve.wait_ge(x_in[p], 16 * (b + 1))
                    dve.wait_ge(gathered[p], 16 * NT * K * (b + 1))
                    for k in range(K):
                        for i in range(NT):
                            ins = dve.scalar_tensor_tensor(out=xr[p][:, i, :], in0=ans[p][:, i, k, :],
                                                           scalar=gate[:, u, i, k:k + 1], in1=xr[p][:, i, :],
                                                           op0=ALU.mult, op1=ALU.add)
                            if k < K - 1:
                                d.did(ins)
                        if k < K - 1:
                            d.wait()
                    ins.then_inc(summed, 1)
                    dve.wait_ge(summed, u + 3)
                    hold(dve, stored[p], 16 * (b + 1))
                    norm.vector(dve, d, u, xr[p], y[p])
                    d.wait()
                    dve.sem_inc(y_ready, 1)
                    assert d.n == NOWN, (d.n, NOWN)


def build(nc, ins, out):
    dram = {}
    LAYER_SEMS.clear()

    def scratch(name, shape, dt=F32):
        dram[name] = nc.dram_tensor(f"s_{name}", shape, dt, kind="Internal").ap()

    for layer, rt in enumerate(ROUTERS):
        for n in ("q", "k"):
            halves = layer == 0 and n == "q"
            scratch(f"{n}parts{layer}", (3, S // CH, B, D, CH) if halves else (3, B, D, S), BF16)
        scratch(f"values{layer}", (B, G, S, P))
        scratch(f"heads{layer}", (B, G, S, FG))
        scratch(f"slots{layer}", (rt["E"] * rt["C"], D))
        scratch(f"answers{layer}", (rt["E"] * rt["C"], D))
        scratch(f"normed{layer}", (T, D))
    scratch("mid", (T, D))
    for n in ("q", "k"):
        scratch(f"{n}full", (B, D, S))
    tokens = ins["x"].rearrange("b s d -> (b s) d")
    with ExitStack() as ctx:
        c = constants(nc, ctx, ins, dram)
        with ExitStack() as lctx:
            w = load_weights(nc, lctx, ins, 0)
            project(nc, c, w, tokens, dram, 0)
            attend(nc, c, dram)
            gidx, gate = route(nc, lctx, c, w, ins, dram, tokens, 0)
            experts(nc, c, ins, dram, 0)
            combine(nc, dram, gidx, gate, dram["mid"], 0)
        nc.clear_and_free_semaphores(list(LAYER_SEMS))
        LAYER_SEMS.clear()
        nc.all_engine_barrier()
        with ExitStack() as lctx:
            w = load_weights(nc, lctx, ins, 1)
            project(nc, c, w, dram["mid"], dram, 1)
            attend_linear(nc, c, dram)
            gidx, gate = route(nc, lctx, c, w, ins, dram, dram["mid"], 1)
            experts(nc, c, ins, dram, 1)
            combine(nc, dram, gidx, gate, out.rearrange("b s d -> (b s) d"), 1)


_WEIGHTS = {"wq0": "L0_attn_WQ", "wk0": "L0_attn_WK", "wv0": "L0_attn_WV", "wo0": "L0_attn_WO",
            "wq1": "L1_attn_Wq", "wk1": "L1_attn_Wk", "wv1": "L1_attn_Wv", "wo1": "L1_attn_Wo"}
_PLAIN = {"x": "L0_attn_x", "gate0": "L0_ffn_gate_w", "gbias0": "L0_ffn_gate_b",
          "w1_0": "L0_ffn_w1", "w2_0": "L0_ffn_w2", "b2_0": "L0_ffn_b2",
          "gate1": "L1_ffn_router_w", "gbias1": "L1_ffn_router_b",
          "w1_1": "L1_ffn_w1", "w2_1": "L1_ffn_w2", "b2_1": "L1_ffn_b2", "bo1": "L1_attn_bo"}
_TURNED = {"b1_0": "L0_ffn_b1", "b1_1": "L1_ffn_b1"}


def kernel(**inputs):
    import numpy as np
    import concourse.bacc as bacc
    from concourse.bass_utils import run_bass_kernel_spmd

    nc = bacc.Bacc("TRN2", target_bir_lowering=False, num_devices=1)
    arrays = {}
    for name, key in _WEIGHTS.items():
        arrays[name] = np.ascontiguousarray(np.asarray(inputs[key]).T)
    for name, key in _PLAIN.items():
        arrays[name] = np.ascontiguousarray(inputs[key])
    for name, key in _TURNED.items():
        a = np.asarray(inputs[key])
        arrays[name] = np.ascontiguousarray(a.reshape(a.shape[0], FT, P).transpose(2, 0, 1))
    ins = {n: nc.dram_tensor(n, a.shape, mybir.dt.from_np(a.dtype), kind="ExternalInput").ap()
           for n, a in arrays.items()}
    out = nc.dram_tensor("out", (B, S, D), F32, kind="ExternalOutput").ap()
    build(nc, ins, out)
    r = run_bass_kernel_spmd(nc, [arrays], core_ids=[0])
    return r.results[0]["out"]
```

```python
from contextlib import ExitStack

import concourse.bass as bass
from concourse import mybir

ALU = mybir.AluOpType
ACT = mybir.ActivationFunctionType
AX = mybir.AxisListType
F32 = mybir.dt.float32
BF16 = mybir.dt.bfloat16
I32 = mybir.dt.int32
U32 = mybir.dt.uint32

P = 128
B, S, D = 4, 1024, 256
T = B * S
DT = D // P
ST = S // P
H, DK = 16, 16
HG = 4
G = H // HG
FG = HG * DK
STRIP = P // HG
CH = 512
F = 1024
FT = F // P
EPS = 1e-5
TERMS = ((0, 0), (0, 1), (1, 0), (0, 2), (2, 0), (1, 1))
KR = len(TERMS) * DK
BIG = float(1 << 20)

ROUTERS = ({"E": 64, "K": 3, "C": 128}, {"E": 8, "K": 2, "C": 640})


class Done:

    def __init__(self, eng, sem, base=0):
        self.eng, self.sem, self.base, self.n = eng, sem, base, 0

    def did(self, ins):
        ins.then_inc(self.sem, 1)
        self.n += 1
        return self.n

    def wait(self, n=None):
        self.eng.wait_ge(self.sem, self.base + (self.n if n is None else n))

    def hold(self):
        hold(self.eng, self.sem, self.base + self.n)


def hold(eng, sem, value):
    eng.wait_ge(sem, value)
    eng.nop(nofuse=True)


LAYER_SEMS = []


class Stage:

    def __init__(self, nc, ctx, tag):
        self.nc, self.ctx, self.tag = nc, ctx, tag

    def sb(self, name, shape, dt=F32):
        return self.ctx.enter_context(self.nc.sbuf_tensor(f"{self.tag}_{name}", shape, dt))

    def ps(self, name, shape, dt=F32):
        return self.ctx.enter_context(self.nc.psum_tensor(f"{self.tag}_{name}", shape, dt))

    def sem(self, name):
        sem = self.nc.alloc_semaphore(f"{self.tag}_{name}")
        LAYER_SEMS.append(sem)
        return sem


def constants(nc, ctx, ins, dram):
    st = Stage(nc, ctx, "c")
    c = {
        "ident": st.sb("ident", [P, P]), "identb": st.sb("identb", [P, P], BF16),
        "future": st.sb("future", [P, P], BF16),
        "past": st.sb("past", [P, P]),
        "before": st.sb("before", [P, P], BF16),
        "ones": st.sb("ones", [P, P], BF16),
        "own": st.sb("own", [FG, P]),
        "zero": st.sb("zero", [P, 2048]),
    }
    for r, rt in enumerate(ROUTERS):
        c[f"expert{r}"] = st.sb(f"expert{r}", [P, rt["E"]])
        c[f"first{r}"] = st.sb(f"first{r}", [P, rt["E"]])
    with ExitStack() as tmp:
        s2 = Stage(nc, tmp, "ci")
        made, zeroed, filled = s2.sem("made"), s2.sem("zeroed"), s2.sem("filled")
        block = tmp.enter_context(nc.Block())

        @block.gpsimd
        def _(pool):
            d = Done(pool, made)
            d.did(pool.memset(c["ident"][:], 0.0))
            d.did(pool.memset(c["identb"][:], 0.0))
            d.did(pool.memset(c["future"][:], 0.0))
            d.did(pool.memset(c["past"][:], 1.0))
            d.did(pool.memset(c["before"][:], 1.0))
            d.did(pool.memset(c["ones"][:], 1.0))
            d.did(pool.memset(c["own"][:], 1.0))
            for r, rt in enumerate(ROUTERS):
                d.did(pool.iota(c[f"expert{r}"][:], [[1, rt["E"]]], base=0, channel_multiplier=0,
                                allow_small_or_imprecise_dtypes=True))
                d.did(pool.iota(c[f"first{r}"][:], [[rt["C"], rt["E"]]], base=0, channel_multiplier=0,
                                allow_small_or_imprecise_dtypes=True))
            d.wait()
            for name in ("ident", "identb"):
                d.did(pool.affine_select(out=c[name][:], in_=c[name][:], compare_op=ALU.not_equal, fill=1.0,
                                         base=0, pattern=[[-1, P]], channel_multiplier=1))
            d.did(pool.affine_select(out=c["future"][:], in_=c["future"][:], compare_op=ALU.is_ge, fill=-1e30,
                                     base=0, pattern=[[-1, P]], channel_multiplier=1))
            d.did(pool.affine_select(out=c["past"][:], in_=c["past"][:], compare_op=ALU.is_ge, fill=0.0,
                                     base=0, pattern=[[1, P]], channel_multiplier=-1))
            d.did(pool.affine_select(out=c["before"][:], in_=c["before"][:], compare_op=ALU.is_gt, fill=0.0,
                                     base=0, pattern=[[1, P]], channel_multiplier=-1))
            d.did(pool.affine_select(out=c["own"][:], in_=c["own"][:], compare_op=ALU.is_ge, fill=0.0,
                                     base=0, pattern=[[-DK, HG], [0, STRIP]], channel_multiplier=1))
            d.wait()
            d.did(pool.affine_select(out=c["own"][:], in_=c["own"][:], compare_op=ALU.is_ge, fill=0.0,
                                     base=DK - 1, pattern=[[DK, HG], [0, STRIP]], channel_multiplier=-1))
            d.wait()

        @block.vector
        def _(dve):
            dve.memset(c["zero"][:], 0.0).then_inc(zeroed, 1)

        @block.sync
        def _(sp):
            sp.wait_ge(zeroed, 1)
            n = 0
            for r, rt in enumerate(ROUTERS):
                rows = rt["E"] * rt["C"] // P
                dst = dram[f"slots{r}"].rearrange("(p n) d -> p (n d)", p=P)
                for o in range(0, rows * D, 2048):
                    sp.dma_start(dst[:, o:o + 2048], c["zero"][:]).then_inc(filled, 16)
                    n += 16
            sp.wait_ge(filled, n)
    return c


def load_weights(nc, ctx, ins, layer):
    st = Stage(nc, ctx, f"w{layer}")
    w = {k: st.sb(k, [P, DT, D]) for k in ("wq", "wk", "wv", "wo")}
    with ExitStack() as tmp:
        s2 = Stage(nc, tmp, f"wl{layer}")
        loaded = s2.sem("loaded")
        block = tmp.enter_context(nc.Block())

        @block.sync
        def _(sp):
            for k in w:
                sp.dma_start(w[k][:], ins[f"{k}{layer}"].rearrange("(j p) f -> p j f", p=P)).then_inc(loaded, 16)
            sp.wait_ge(loaded, 16 * len(w))
    return w


def project(nc, c, w, x_dram, dram, layer):
    NT = CH // P
    PER = S // CH
    NSTORE = 6 + G + (2 if layer else 0)
    with ExitStack() as ctx:
        st = Stage(nc, ctx, f"p{layer}")
        xin = [st.sb(f"xin{p}", [P, NT, D]) for p in range(PER)]
        xT = st.sb("xT", [P, DT, CH])
        rest = [st.sb(f"rest{r}", [P, CH]) for r in range(4)]
        neg = [st.sb(f"neg{r}", [P, CH]) for r in range(4)] if layer else None
        phi = [st.sb(f"phi{p}", [P, 4, CH]) for p in range(PER)] if layer else None
        parts = [[st.sb(f"part{p}_{k}", [P, 4, CH], BF16) for k in range(3)] for p in range(PER)]
        vpad = [st.sb(f"vpad{p}", [P, NT, G, P]) for p in range(PER)]
        ps_x = st.ps("ps_x", [P, DT, CH])
        ps_qk = st.ps("ps_qk", [P, 4, CH])
        ps_v = st.ps("ps_v", [P, 2, 2, D])
        x_loaded = [st.sem(f"x_loaded{p}") for p in range(PER)]
        stored = [st.sem(f"stored{p}") for p in range(PER)]
        xT_psum, xT_a, xT_v = st.sem("xT_psum"), st.sem("xT_a"), st.sem("xT_v")
        qk_psum, v_psum, v_ready = st.sem("qk_psum"), st.sem("v_psum"), st.sem("v_ready")
        hi_ready, rest_ready = st.sem("hi_ready"), st.sem("rest_ready")
        mid_ready, pads = st.sem("mid_ready"), st.sem("pads")
        neg_ready, exp_ready, phi_ready = st.sem("neg_ready"), st.sem("exp_ready"), st.sem("phi_ready")
        block = ctx.enter_context(nc.Block())

        @block.sync
        def _(sp):
            for p in range(PER):
                sp.sem_inc(stored[p], 16)

            def load(b, p):
                sp.dma_start(xin[p][:], x_dram[bass.ds(b * S + p * CH, CH), :]
                             .rearrange("(n q) d -> q n d", q=P)).then_inc(x_loaded[p], 16)

            def store(b, p):
                sp.wait_ge(mid_ready, 8 * (PER * b + p) + 16)
                for o, name in enumerate(("q", "k")):
                    for k in range(3):
                        dst = dram[f"{name}parts{layer}"]
                        dst = dst[k, b, :, p * CH:(p + 1) * CH] if o or layer else dst[k, p, b]
                        sp.dma_start(dst.rearrange("(j q) t -> q j t", q=P),
                                     parts[p][k][:, 2 * o:2 * o + 2, :]).then_inc(stored[p], 16)
                    if layer:
                        dst = dram[f"{name}full"][b, :, p * CH:(p + 1) * CH]
                        sp.dma_start(dst.rearrange("(j q) t -> q j t", q=P),
                                     phi[p][:, 2 * o:2 * o + 2, :]).then_inc(stored[p], 16)
                sp.wait_ge(v_ready, 2 * (PER * b + p) + 4)
                for g in range(G):
                    dst = dram[f"values{layer}"][b, g, p * CH:(p + 1) * CH, :]
                    sp.dma_start(dst.rearrange("(n q) e -> q n e", q=P),
                                 vpad[p][:, :, g, :]).then_inc(stored[p], 16)

            for p in range(PER):
                load(0, p)
            with sp.Fori(0, B - 1) as b:
                for p in range(PER):
                    store(b, p)
                    sp.wait_ge(xT_psum, 2 * (PER * b + p) + 2)
                    load(b + 1, p)
            for p in range(PER):
                store(B - 1, p)
            for p in range(PER):
                sp.wait_ge(stored[p], 16 * (B * NSTORE + 1))

        @block.tensor
        def _(pe):
            with pe.Fori(0, B) as b:
                for p in range(PER):
                    n = PER * b + p
                    pe.wait_ge(x_loaded[p], 16 * (b + 1))
                    for j in range(DT):
                        pe.wait_ge((xT_a, xT_v)[j], n + 1)
                        for i in range(NT):
                            mm = pe.transpose(ps_x[:, j, i * P:(i + 1) * P], xin[p][:, i, j * P:(j + 1) * P],
                                              c["ident"][:])
                        mm.then_inc(xT_psum, 1)
                    for j in range(DT):
                        pe.wait_ge((xT_a, xT_v)[j], n + 2)
                    for r in range(4):
                        wt = w[("wq", "wk")[r // 2]]
                        if layer:
                            pe.wait_ge(phi_ready, 4 * n + r + 1)
                        else:
                            pe.wait_ge(hi_ready, 4 * n + r + 1)
                            pe.wait_ge(rest_ready, 4 * n + r + 1)
                        for j in range(DT):
                            mm = pe.matmul(ps_qk[:, r, :], wt[:, j, (r % 2) * P:(r % 2 + 1) * P], xT[:, j, :],
                                           start=(j == 0), stop=(j == DT - 1))
                        mm.then_inc(qk_psum, 1)
                    for v in range(2):
                        pe.wait_ge(v_ready, 2 * n + v + 1)
                        for i in range(2):
                            for j in range(DT):
                                mm = pe.matmul(ps_v[:, v, i, :], xT[:, j, (2 * v + i) * P:(2 * v + i + 1) * P],
                                               w["wv"][:, j, :], start=(j == 0), stop=(j == DT - 1))
                        mm.then_inc(v_psum, 1)

        @block.scalar
        def _(act):
            act.sem_inc(xT_a, 1)
            act.sem_inc(hi_ready, 4)
            with act.Fori(0, B) as b:
                for p in range(PER):
                    n = PER * b + p
                    act.wait_ge(xT_psum, 2 * n + 1)
                    act.copy(xT[:, 0, :], ps_x[:, 0, :]).then_inc(xT_a, 1)
                    act.wait_ge(stored[p], 16 * (NSTORE * b + 1))
                    for r in range(4):
                        if layer:
                            act.wait_ge(neg_ready, 4 * n + r + 1)
                            act.activation(neg[r][:], neg[r][:], ACT.Exp).then_inc(exp_ready, 1)
                            act.wait_ge(phi_ready, 4 * n + r + 5)
                            src = phi[p][:, r, :]
                        else:
                            act.wait_ge(qk_psum, 4 * n + r + 1)
                            src = ps_qk[:, r, :]
                        act.copy(parts[p][0][:, r, :], src).then_inc(hi_ready, 1)

        @block.vector
        def _(dve):
            dve.sem_inc(xT_v, 1)
            dve.sem_inc(rest_ready, 4)
            dve.sem_inc(v_ready, 2)
            dve.sem_inc(phi_ready, 4)
            d = Done(dve, pads)
            for p in range(PER):
                d.did(dve.memset(vpad[p][:], 0.0))
            d.wait()
            for p in range(PER):
                d.did(dve.memset(vpad[p].rearrange("q n g (h e) -> q (n g h) e", h=HG)[:, :, DK:DK + 1], 1.0))
            d.wait()
            with dve.Fori(0, B) as b:
                for p in range(PER):
                    n = PER * b + p
                    dve.wait_ge(xT_psum, 2 * n + 2)
                    dve.tensor_copy(xT[:, 1, :], ps_x[:, 1, :]).then_inc(xT_v, 1)
                    dve.wait_ge(stored[p], 16 * (NSTORE * b + 1))
                    for r in range(4):
                        if layer:
                            dve.wait_ge(qk_psum, 4 * n + r + 1)
                            dve.wait_ge(phi_ready, 4 * n + r + 1)
                            dve.tensor_scalar(neg[r][:], ps_qk[:, r, :], 0.0, None, ALU.min).then_inc(neg_ready, 1)
                    for r in range(4):
                        if layer:
                            dve.wait_ge(exp_ready, 4 * n + r + 1)
                            dve.scalar_tensor_tensor(out=phi[p][:, r, :], in0=ps_qk[:, r, :], scalar=0.0,
                                                     in1=neg[r][:], op0=ALU.max, op1=ALU.add).then_inc(phi_ready, 1)
                            src = phi[p][:, r, :]
                        else:
                            src = ps_qk[:, r, :]
                        dve.wait_ge(hi_ready, 4 * n + r + 5)
                        dve.wait_ge(mid_ready, 8 * n + 2 * r + 2)
                        dve.tensor_tensor(rest[r][:], src, parts[p][0][:, r, :],
                                          ALU.subtract).then_inc(rest_ready, 1)
                    for v in range(2):
                        dve.wait_ge(v_psum, 2 * n + v + 1)
                        for i in range(2):
                            cp = dve.tensor_copy(
                                vpad[p][:, 2 * v + i].rearrange("q g (h e) -> q (g h) e", h=HG)[:, :, 0:DK],
                                ps_v[:, v, i, :].rearrange("q (h e) -> q h e", e=DK))
                        cp.then_inc(v_ready, 1)

        @block.gpsimd
        def _(pool):
            pool.sem_inc(mid_ready, 8)
            with pool.Fori(0, B) as b:
                for p in range(PER):
                    n = PER * b + p
                    pool.wait_ge(stored[p], 16 * (NSTORE * b + 1))
                    for r in range(4):
                        hold(pool, rest_ready, 4 * n + r + 5)
                        pool.tensor_copy(parts[p][1][:, r, :], rest[r][:]).then_inc(mid_ready, 1)
                        pool.wait_ge(mid_ready, 8 * n + 2 * r + 9)
                        pool.tensor_tensor(parts[p][2][:, r, :], rest[r][:], parts[p][1][:, r, :],
                                           ALU.subtract).then_inc(mid_ready, 1)


def attend(nc, c, dram):
    N = B * G
    NBUF = 3
    assert (N - 1) % NBUF == 0
    QT = CH // P
    HALVES = S // CH
    NLOAD = (HALVES + 1) * len(TERMS) + 1
    with ExitStack() as ctx:
        st = Stage(nc, ctx, "a")
        qop = [st.sb(f"qop{p}", [KR + 2, HALVES, HG, CH], BF16) for p in range(NBUF)]
        kop = [st.sb(f"kop{p}", [KR + 2, HG, S], BF16) for p in range(NBUF)]
        val = [st.sb(f"val{p}", [P, ST, P]) for p in range(NBUF)]
        prob = st.sb("prob", [P, 4, HG, CH])
        mlow = st.sb("mlow", [P, HG, QT])
        mpart = st.sb("mpart", [P, HG, QT, 2])
        mhigh = st.sb("mhigh", [P, HG, QT])
        mrow = [st.sb(f"mrow{h}", [HG * QT, 2, P], BF16) for h in range(HALVES)]
        o_sb = [st.sb(f"o_sb{h}", [P, CH]) for h in range(HALVES)]
        recip = st.sb("recip", [P, QT, HG])
        ao = [st.sb(f"ao{h}", [P, QT, FG]) for h in range(HALVES)]
        ps_1 = [st.ps(f"ps_1{i}", [P, CH]) for i in range(2)]
        ps_2 = [st.ps(f"ps_2{i}", [P, 2, CH]) for i in range(2)]
        ps_o = st.ps("ps_o", [P, CH])
        ps_t = st.ps("ps_t", [P, QT, P])
        loaded = [st.sem(f"loaded{p}") for p in range(NBUF)]
        rows_in = [st.sem(f"rows_in{h}") for h in range(HALVES)]
        ao_out = [st.sem(f"ao_out{h}") for h in range(HALVES)]
        s1, maxed = st.sem("s1"), st.sem("maxed")
        s2, exped, masked, used = st.sem("s2"), st.sem("exped"), st.sem("masked"), st.sem("used")
        o_copied = [st.sem(f"o_copied{h}") for h in range(HALVES)]
        t_done = st.sem("t_done")
        mrow_ready, ao_ready = st.sem("mrow_ready"), st.sem("ao_ready")
        hi_done, comb, rec, setup = st.sem("hi_done"), st.sem("comb"), st.sem("rec"), st.sem("setup")
        block = ctx.enter_context(nc.Block())

        pass1 = [(h, q, 0, (q + 1) * P) for q in range(QT) for h in range(HG)]
        for q in range(QT, ST):
            for h in range(HG):
                pass1 += [(h, q, 0, CH), (h, q, CH, (q + 1) * P - CH)]
        N1 = len(pass1)
        pass2 = [(j, k, max(j * CH, k * P), (j + 1) * CH - max(j * CH, k * P))
                 for j in range(HALVES) for k in range(QT * (j + 1))]
        N2 = len(pass2)
        diag = [n for n, (j, k, q0, w) in enumerate(pass2) if q0 == k * P]
        LAG = 2

        def make_plan(ahead):
            work = []
            for n in range(LAG, N2):
                w = pass2[n][3]
                work += [(("s2", n, u), 2 * w) for u in range(2)]
                work.append((("av", n - LAG), 4 * pass2[n - LAG][3]))
                if n == QT + LAG:
                    work.insert(-1, (("heads", 0), 512))
            tail = []
            if ahead:
                tail += [("s2", N2, 0), ("s2", N2, 1), ("av", N2 - 2), ("av", N2 - 1),
                         ("s2", N2 + 1, 0), ("s2", N2 + 1, 1)]
            else:
                tail += [("av", N2 - 2), ("av", N2 - 1)]
            tail.append(("heads", 1))
            if not ahead:
                return [a for a, _ in work] + tail
            plan, total, dve_total = [], sum(c_ for _, c_ in work), sum(u[3] + 60 for u in pass1)
            done, dve, i = 0, 0, 0
            for atom, cost in work:
                plan.append(atom)
                done += cost
                while i < N1 and (dve + (pass1[i][3] + 60) / 2) * total <= done * dve_total:
                    dve += pass1[i][3] + 60
                    plan.append(("p1", i))
                    i += 1
                    if i == QT * HG + 2:
                        plan.append(("max", 0))
            plan += [("p1", k) for k in range(i, N1)]
            return plan + tail[:2] + [("max", 1)] + tail[2:]

        full_plan, last_plan = make_plan(True), make_plan(False)

        def turns(plan):
            return [a for a in plan if a[0] in ("heads", "max")]

        def freed(eng, s, plan, use):
            order = turns(plan)
            k = order.index(use)
            if k == 0:
                eng.wait_ge(mrow_ready, HALVES * (s + 1))
                eng.wait_ge(ao_ready, HALVES * s + 1)
            elif order[k - 1][0] == "heads":
                eng.wait_ge(ao_ready, 1 + HALVES * s + order[k - 1][1] + 1)
            else:
                eng.wait_ge(mrow_ready, HALVES * (s + 1) + order[k - 1][1] + 1)

        def turned(eng, s, plan, use):
            eng.wait_ge(t_done, HALVES + 4 * s + turns(plan).index(use) + 1)

        @block.sync
        def _(sp):
            def load(s, p):
                for t, (qpart, kpart) in enumerate(TERMS):
                    rows = slice(t * DK, (t + 1) * DK)
                    for x in range(HALVES):
                        src = dram["qparts0"].rearrange("k x b (g h e) t -> k x (b g) e h t", g=G, h=HG)
                        sp.dma_start(qop[p][rows, x], src[qpart, x, s]).then_inc(loaded[p], 16)
                    src = dram["kparts0"].rearrange("k b (g h e) t -> k (b g) e h t", g=G, h=HG)[kpart, s]
                    sp.dma_start(kop[p][rows], src).then_inc(loaded[p], 16)
                src = dram["values0"].rearrange("b g (n q) e -> (b g) q n e", q=P)[s]
                sp.dma_start(val[p][:], src).then_inc(loaded[p], 16)

            def rows(s, p, half):
                sp.wait_ge(mrow_ready, HALVES * s + half + 1)
                for r in range(2):
                    sp.dma_start(qop[p][KR + r:KR + r + 1, half].rearrange("o h t -> o (h t)"),
                                 mrow[half][:, r, :]).then_inc(rows_in[half], 16)

            def out(s, half):
                sp.wait_ge(ao_ready, 1 + HALVES * s + half + 1)
                dst = dram["heads0"].rearrange("b g (x n q) e -> (b g) x q n e", x=HALVES, q=P)
                sp.dma_start(dst[s, half], ao[half][:]).then_inc(ao_out[half], 16)

            def step(s, p, loads=True):
                for kind, h in turns(full_plan)[:-1]:
                    if kind == "heads":
                        out(s, h)
                    else:
                        rows(s + 1, (p + 1) % NBUF, h)
                if loads:
                    sp.wait_ge(used, 4 + N2 * (s + 1))
                    load(s + NBUF, p)
                out(s, 1)

            for h in range(HALVES):
                sp.sem_inc(ao_out[h], 16)
                sp.sem_inc(rows_in[h], 32)
            for p in range(NBUF):
                load(p, p)
            rows(0, 0, 0)
            rows(0, 0, 1)
            with sp.Fori(0, (N - 1) // NBUF - 1) as j:
                for p in range(NBUF):
                    step(j * NBUF + p, p)
            for s in range(N - 1 - NBUF, N - 1):
                step(s, s % NBUF, loads=(s + NBUF < N))
            out(N - 1, 0)
            out(N - 1, 1)
            for h in range(HALVES):
                sp.wait_ge(ao_out[h], 16 * (N + 1))

        @block.tensor
        def _(pe):
            def scores1(s, p, i, first=False):
                h, q, k0, kn = pass1[i]
                if not (first and i < 2):
                    pe.wait_ge(maxed, N1 * s + i - 1)
                dst = ps_1[i % 2][:, 0:kn]
                last = k0 + kn == (q + 1) * P
                mm = pe.matmul(dst, qop[p][0:KR, q // QT, h, (q % QT) * P:(q % QT + 1) * P], kop[p][0:KR, h, k0:k0 + kn],
                               start=True, stop=not last)
                if last:
                    mm = pe.matmul(dst[:, kn - P:kn], c["identb"][:], c["future"][:], start=False, stop=True)
                mm.then_inc(s1, 1)

            def scores2(s, p, n, u):
                j, k, q0, w = pass2[n]
                if u == 0 and (n == 0 or pass2[n - 1][0] != j):
                    pe.wait_ge(rows_in[j], 32 * (s + 2))
                pe.wait_ge(exped, 2 * (N2 * s + n) + u + 1)
                for h in range(2):
                    mm = pe.matmul(ps_2[u][:, h, 0:w], kop[p][:, 2 * u + h, k * P:(k + 1) * P],
                                   qop[p][:, j, 2 * u + h, q0 - j * CH:q0 - j * CH + w], start=True, stop=True)
                mm.then_inc(s2, 1)

            def values(s, p, n):
                j, k, q0, w = pass2[n]
                last = k == QT * (j + 1) - 1
                if k == 0:
                    pe.wait_ge(o_copied[1 - j], s + 1)
                pe.wait_ge(exped, 2 * (N2 * s + n) + 4)
                if n in diag:
                    pe.wait_ge(masked, len(diag) * s + diag.index(n) + 1)
                o0 = q0 - j * CH
                for h in range(HG):
                    sl = slice(h * STRIP, (h + 1) * STRIP)
                    mm = pe.matmul(ps_o[sl, o0:o0 + w], val[p][:, k, sl], prob[:, n % 4, h, 0:w],
                                   start=(k == 0), stop=last)
                mm.then_inc(used, 1)

            def turn_heads(s, plan, j):
                pe.wait_ge(o_copied[j], s + 1 + j)
                freed(pe, s, plan, ("heads", j))
                for i in range(QT):
                    mm = pe.transpose(ps_t[:, i, :], o_sb[j][:, i * P:(i + 1) * P], c["ident"][:])
                mm.then_inc(t_done, 1)

            def turn_max(s, half):
                if half:
                    pe.wait_ge(comb, s + 1)
                else:
                    pe.wait_ge(maxed, N1 * s + QT * HG)
                m = (mlow, mhigh)[half].rearrange("p h q -> p (h q)")
                pe.transpose(ps_t[0:HG * QT, 0, :], m, c["ident"][:]).then_inc(t_done, 1)

            def step(s, p, plan):
                pn = (p + 1) % NBUF
                for atom in plan:
                    kind, i = atom[:2]
                    if kind == "s2" and i < N2:
                        scores2(s, p, i, atom[2])
                    elif kind == "s2":
                        scores2(s + 1, pn, i - N2, atom[2])
                    elif kind == "p1":
                        scores1(s + 1, pn, i)
                    elif kind == "av":
                        values(s, p, i)
                    elif kind == "max":
                        freed(pe, s, plan, atom)
                        turn_max(s + 1, i)
                    else:
                        turn_heads(s, plan, i)

            pe.sem_inc(used, 4)
            pe.wait_ge(loaded[0], 16 * NLOAD)
            for i in range(N1):
                scores1(0, 0, i, first=True)
            turn_max(0, 0)
            pe.wait_ge(mrow_ready, 1)
            turn_max(0, 1)
            pe.wait_ge(setup, 1)
            for n in range(LAG):
                for u in range(2):
                    scores2(0, 0, n, u)
            with pe.Fori(0, (N - 1) // NBUF) as j:
                for p in range(NBUF):
                    pe.wait_ge(loaded[(p + 1) % NBUF], 16 * NLOAD * (j + 1 + (p + 1) // NBUF))
                    step(j * NBUF + p, p, full_plan)
            step(N - 1, (N - 1) % NBUF, last_plan)

        @block.scalar
        def _(act):
            def step(s):
                for n, (j, k, q0, w) in enumerate(pass2):
                    act.wait_ge(used, N2 * s + n + 1)
                    for u in range(2):
                        act.wait_ge(s2, 2 * (N2 * s + n) + u + 1)
                        act.activation(prob[:, n % 4, 2 * u:2 * u + 2, 0:w], ps_2[u][:, :, 0:w], ACT.Exp,
                                       scale=DK ** -0.5).then_inc(exped, 1)
                    if n == QT + 1:
                        act.wait_ge(used, 4 + N2 * s + QT)
                        act.wait_ge(ao_ready, HALVES * s + 1)
                        act.copy(o_sb[0][:], ps_o[:]).then_inc(o_copied[0], 1)

            act.sem_inc(exped, 2)
            with act.Fori(0, N) as s:
                step(s)

        @block.gpsimd
        def _(pool):
            for p in range(NBUF):
                ins = pool.memset(kop[p][KR:KR + 2, :, :], 1.0)
            ins.then_inc(setup, 1)
            with pool.Fori(0, N) as s:
                for n in diag:
                    hold(pool, exped, 2 * (N2 * s + n) + 4)
                    blk = prob[:, n % 4, :, 0:P]
                    pool.affine_select(out=blk, in_=blk, compare_op=ALU.is_ge, fill=0.0, base=0,
                                       pattern=[[0, HG], [1, P]], channel_multiplier=-1).then_inc(masked, 1)

        @block.vector
        def _(dve):
            def maxima(s, i):
                h, q, k0, kn = pass1[i]
                dst = mlow[:, h, q:q + 1] if q < QT else mpart[:, h, q - QT, k0 // CH:k0 // CH + 1]
                dve.wait_ge(s1, N1 * s + i + 1)
                dve.tensor_reduce(dst, ps_1[i % 2][:, 0:kn], AX.X, ALU.max).then_inc(maxed, 1)

            def combine(s):
                dve.wait_ge(maxed, N1 * (s + 1))
                dve.tensor_reduce(mhigh[:], mpart[:], AX.X, ALU.max).then_inc(comb, 1)

            def make_rows(s, half):
                dve.wait_ge(rows_in[half], 32 * (s + 1))
                src = ps_t[0:HG * QT, 0, :]
                dve.tensor_scalar(mrow[half][:, 0, :], src, -1.0, None, ALU.mult).then_inc(hi_done, 1)
                dve.wait_ge(hi_done, HALVES * s + half + 1)
                dve.scalar_tensor_tensor(out=mrow[half][:, 1, :], in0=src, scalar=-1.0, in1=mrow[half][:, 0, :],
                                         op0=ALU.mult, op1=ALU.subtract).then_inc(mrow_ready, 1)

            def divide(s, plan, j):
                if j:
                    dve.wait_ge(used, 4 + N2 * (s + 1))
                    dve.tensor_copy(o_sb[1][:], ps_o[:]).then_inc(o_copied[1], 1)
                turned(dve, s, plan, ("heads", j))
                heads = ps_t.rearrange("p n (h e) -> p n h e", h=HG)
                dve.reciprocal(recip[:], heads[:, :, :, DK]).then_inc(rec, 1)
                dve.wait_ge(rec, HALVES * s + j + 1)
                dve.wait_ge(ao_out[j], 16 * (s + 1))
                dve.tensor_tensor(ao[j].rearrange("p n (h e) -> p n h e", h=HG), heads[:, :, :, 0:DK],
                                  recip[:].unsqueeze(3).to_broadcast([P, QT, HG, DK]),
                                  ALU.mult).then_inc(ao_ready, 1)

            def step(s, plan):
                DELAY = 2
                queue = []

                def serve(atom):
                    if atom[0] == "heads":
                        divide(s, plan, atom[1])
                    else:
                        turned(dve, s, plan, atom)
                        make_rows(s + 1, atom[1])

                order = []
                for atom in plan:
                    if atom[0] == "p1":
                        order.append(atom)
                        for q in queue:
                            q[1] -= 1
                        while queue and queue[0][1] <= 0:
                            order.append(queue.pop(0)[0])
                    elif atom[0] in ("heads", "max"):
                        queue.append([atom, DELAY])
                order += [q[0] for q in queue]
                for atom in order:
                    if atom[0] == "p1":
                        maxima(s + 1, atom[1])
                        if atom[1] == N1 - 1:
                            combine(s + 1)
                    else:
                        serve(atom)

            dve.sem_inc(o_copied[1], 1)
            dve.sem_inc(ao_ready, 1)
            for i in range(N1):
                maxima(0, i)
            dve.wait_ge(t_done, 1)
            make_rows(0, 0)
            combine(0)
            dve.wait_ge(t_done, 2)
            make_rows(0, 1)
            with dve.Fori(0, N - 1) as s:
                step(s, full_plan)
            step(N - 1, last_plan)


def attend_linear(nc, c, dram):
    N = B * G
    QT = CH // P
    HALVES = S // CH
    NLOAD = 2 * len(TERMS) + 3
    with ExitStack() as ctx:
        st = Stage(nc, ctx, "l")
        qop = [st.sb(f"qop{p}", [KR, HG, S], BF16) for p in range(2)]
        kop = [st.sb(f"kop{p}", [KR, HG, S], BF16) for p in range(2)]
        val = [st.sb(f"val{p}", [P, ST, P]) for p in range(2)]
        qf = [st.sb(f"qf{p}", [FG, S]) for p in range(2)]
        kf = [st.sb(f"kf{p}", [FG, S]) for p in range(2)]
        kt = [st.sb(f"kt{p}", [P, ST, FG]) for p in range(2)]
        att = [st.sb(f"att{i}", [P, HG, P]) for i in range(2)]
        state = [st.sb(f"state{i}", [FG, P]) for i in range(2)]
        o_sb = st.sb("o_sb", [P, CH])
        den = st.sb("den", [P, QT, HG])
        ao = [st.sb(f"ao{h}", [P, QT, FG]) for h in range(HALVES)]
        ps_a = [st.ps(f"ps_a{i}", [P, HG, P]) for i in range(2)]
        ps_o = [st.ps(f"ps_o{i}", [P, CH]) for i in range(2)]
        ps_s = st.ps("ps_s", [FG, P])
        ps_t = st.ps("ps_t", [P, QT, P])
        ps_k = st.ps("ps_k", [P, ST, FG])
        loaded = [st.sem(f"loaded{p}") for p in range(2)]
        ao_out = [st.sem(f"ao_out{h}") for h in range(HALVES)]
        k_turned, k_copied = st.sem("k_turned"), st.sem("k_copied")
        scored, att_ready = st.sem("scored"), st.sem("att_ready")
        state_sum, state_ready = st.sem("state_sum"), st.sem("state_ready")
        o_done, o_copied = st.sem("o_done"), st.sem("o_copied")
        t_done, den_ready, ao_ready = st.sem("t_done"), st.sem("den_ready"), st.sem("ao_ready")
        block = ctx.enter_context(nc.Block())

        @block.sync
        def _(sp):
            def load(s, p):
                for t, (qpart, kpart) in enumerate(TERMS):
                    rows = slice(t * DK, (t + 1) * DK)
                    for op, name, part in ((qop, "qparts1", qpart), (kop, "kparts1", kpart)):
                        src = dram[name].rearrange("k b (g h e) t -> k (b g) e h t", g=G, h=HG)[part, s]
                        sp.dma_start(op[p][rows], src).then_inc(loaded[p], 16)
                sp.dma_start(val[p][:], dram["values1"].rearrange("b g (n q) e -> (b g) q n e", q=P)[s])\
                  .then_inc(loaded[p], 16)
                for op, name in ((qf, "qfull"), (kf, "kfull")):
                    src = dram[name].rearrange("b (g f) t -> (b g) f t", g=G)
                    sp.dma_start(op[p][:], src[s]).then_inc(loaded[p], 16)

            def out(s, half):
                sp.wait_ge(ao_ready, 1 + HALVES * s + half + 1)
                dst = dram["heads1"].rearrange("b g (x n q) e -> (b g) x q n e", x=HALVES, q=P)
                sp.dma_start(dst[s, half], ao[half][:]).then_inc(ao_out[half], 16)

            for h in range(HALVES):
                sp.sem_inc(ao_out[h], 16)
            for p in range(2):
                load(p, p)
            with sp.Fori(0, N // 2 - 1) as j:
                for p in range(2):
                    s = 2 * j + p
                    out(s, 0)
                    out(s, 1)
                    load(s + 2, p)
            for s in (N - 2, N - 1):
                out(s, 0)
                out(s, 1)
            for h in range(HALVES):
                sp.wait_ge(ao_out[h], 16 * (N + 1))

        @block.tensor
        def _(pe):
            with pe.Fori(0, N // 2) as j:
                for p in range(2):
                    s = 2 * j + p

                    def scores(n):
                        pe.wait_ge(att_ready, ST * s + n + 1)
                        for h in range(HG):
                            mm = pe.matmul(ps_a[n % 2][:, h, :], kop[p][:, h, n * P:(n + 1) * P],
                                           qop[p][:, h, n * P:(n + 1) * P], start=True, stop=True)
                        mm.then_inc(scored, 1)

                    def add_state(n):
                        pe.wait_ge(state_ready, (ST - 1) * s + n + 1)
                        pe.matmul(ps_s[:], kt[p][:, n, :], val[p][:, n, :], start=(n == 0), stop=True,
                                  skip_group_check=True).then_inc(state_sum, 1)

                    def outputs(n):
                        half, o0 = n // QT, (n % QT) * P
                        if n % QT == 0:
                            pe.wait_ge(o_copied, HALVES * s + half + 1)
                        if n:
                            pe.wait_ge(state_ready, (ST - 1) * s + n + 1)
                            pe.matmul(ps_o[half][:, o0:o0 + P], state[n % 2][:], qf[p][:, n * P:(n + 1) * P],
                                      start=True, stop=False)
                        pe.wait_ge(att_ready, ST * s + n + 3)
                        for h in range(HG):
                            sl = slice(h * STRIP, (h + 1) * STRIP)
                            mm = pe.matmul(ps_o[half][sl, o0:o0 + P], val[p][:, n, sl], att[n % 2][:, h, :],
                                           start=(n == 0), stop=True)
                        mm.then_inc(o_done, 1)

                    def turn(half):
                        pe.wait_ge(o_copied, HALVES * s + half + 3)
                        pe.wait_ge(ao_ready, HALVES * s + half + 1)
                        for i in range(QT):
                            mm = pe.transpose(ps_t[:, i, :], o_sb[:, i * P:(i + 1) * P], c["ident"][:])
                        mm.then_inc(t_done, 1)

                    pe.wait_ge(loaded[p], 16 * NLOAD * (j + 1))
                    hold(pe, k_copied, s + 1)
                    for i in range(ST):
                        mm = pe.transpose(ps_k[:, i, :], kf[p][:, i * P:(i + 1) * P], c["ident"][0:FG, 0:FG])
                    mm.then_inc(k_turned, 1)
                    scores(0)
                    pe.wait_ge(k_copied, s + 2)
                    add_state(0)
                    for n in range(ST):
                        if n + 1 < ST:
                            scores(n + 1)
                            if n:
                                add_state(n)
                        outputs(n)
                        if n == QT + 1:
                            turn(0)
                    turn(1)

        @block.scalar
        def _(act):
            act.sem_inc(k_copied, 1)
            act.sem_inc(o_copied, 2)
            with act.Fori(0, N // 2) as j:
                for p in range(2):
                    s = 2 * j + p
                    act.wait_ge(k_turned, s + 1)
                    act.copy(kt[p][:], ps_k[:]).then_inc(k_copied, 1)
                    for half in range(HALVES):
                        act.wait_ge(o_done, ST * s + QT * (half + 1))
                        act.wait_ge(ao_ready, HALVES * s + half + 1)
                        act.copy(o_sb[:], ps_o[half][:]).then_inc(o_copied, 1)

        @block.vector
        def _(dve):
            dve.sem_inc(att_ready, 2)
            dve.sem_inc(state_ready, 1)
            dve.sem_inc(ao_ready, 1)
            with dve.Fori(0, N // 2) as j:
                for p in range(2):
                    s = 2 * j + p

                    def mask(n):
                        dve.wait_ge(scored, ST * s + n + 1)
                        dve.tensor_tensor(att[n % 2][:], ps_a[n % 2][:],
                                          c["past"][:].unsqueeze(1).to_broadcast([P, HG, P]),
                                          ALU.mult).then_inc(att_ready, 1)

                    def keep_state(n):
                        dve.wait_ge(state_sum, (ST - 1) * s + n + 1)
                        dve.tensor_tensor(state[(n + 1) % 2][:], ps_s[:], c["own"][:],
                                          ALU.mult).then_inc(state_ready, 1)

                    def divide(half):
                        dve.wait_ge(t_done, HALVES * s + half + 1)
                        heads = ps_t.rearrange("p n (h e) -> p n h e", h=HG)
                        dve.tensor_scalar(den[:], heads[:, :, :, DK], EPS, None, ALU.add).then_inc(den_ready, 1)
                        dve.wait_ge(den_ready, 2 * (HALVES * s + half) + 1)
                        dve.reciprocal(den[:], den[:]).then_inc(den_ready, 1)
                        dve.wait_ge(den_ready, 2 * (HALVES * s + half) + 2)
                        dve.wait_ge(ao_out[half], 16 * (s + 1))
                        for i in range(QT):
                            ins = dve.tensor_tensor(ao[half][:, i, :].rearrange("p (h e) -> p h e", h=HG),
                                                    heads[:, i, :, 0:DK],
                                                    den[:, i, :].unsqueeze(2).to_broadcast([P, HG, DK]), ALU.mult)
                        ins.then_inc(ao_ready, 1)

                    mask(0)
                    keep_state(0)
                    for n in range(ST):
                        if n + 1 < ST:
                            mask(n + 1)
                            if n:
                                keep_state(n)
                        if n == QT + 1:
                            divide(0)
                    divide(1)


NT = CH // P
UNITS = T // CH
NORM_OPS = 3 * NT + 5


class Norm:

    def __init__(self, st, halves=1):
        self.stats = st.sb("stats", [P, NT, 6])
        self.mv = st.sb("mv", [P, NT, 2])
        self.ve = st.sb("ve", [P, NT])
        self.sd = st.sb("sd", [P, NT])
        self.rs = st.sb("rs", [P, NT])
        self.tmp = st.sb("ntmp", [P, NT])
        self.var_ready, self.sqrt_ready = st.sem("var_ready"), st.sem("sqrt_ready")

    def vector(self, dve, d, u, res, y):
        for i in range(NT):
            d.did(dve.bn_stats(self.stats[:, i, :], res[:, i, :]))
        d.hold()
        for i in range(NT):
            d.did(dve.bn_aggr(self.mv[:, i, :], self.stats[:, i, :]))
        d.wait()
        dve.tensor_scalar(self.ve[:], self.mv[:, :, 1], EPS, None, ALU.add).then_inc(self.var_ready, 1)
        dve.wait_ge(self.sqrt_ready, u + 1)
        d.did(dve.reciprocal(self.rs[:], self.sd[:]))
        d.wait()
        d.did(dve.tensor_tensor(self.tmp[:], self.rs[:], self.rs[:], ALU.mult))
        d.wait()
        d.did(dve.tensor_tensor(self.tmp[:], self.tmp[:], self.ve[:], ALU.mult))
        d.wait()
        d.did(dve.tensor_scalar(self.tmp[:], self.tmp[:], -0.5, 1.5, ALU.mult, ALU.add))
        d.wait()
        d.did(dve.tensor_tensor(self.rs[:], self.rs[:], self.tmp[:], ALU.mult))
        d.wait()
        for i in range(NT):
            d.did(dve.tensor_scalar(y[:, i, :], res[:, i, :], self.mv[:, i, 0:1], self.rs[:, i:i + 1],
                                    ALU.subtract, ALU.mult))

    def scalar(self, act, u):
        act.wait_ge(self.var_ready, u + 1)
        act.activation(self.sd[:], self.ve[:], ACT.Sqrt).then_inc(self.sqrt_ready, 1)



def route(nc, ctx, c, w, ins, dram, x_dram, layer):
    rt = ROUTERS[layer]
    E, K, C = rt["E"], rt["K"], rt["C"]
    keep = Stage(nc, ctx, f"k{layer}")
    gidx = keep.sb("gidx", [P, UNITS, NT, K], I32)
    gate = keep.sb("gate", [P, UNITS, NT, K])
    with ExitStack() as tmp:
        st = Stage(nc, tmp, f"r{layer}")
        ao = [st.sb(f"ao{p}", [P, NT, G, FG]) for p in range(2)]
        xr = [st.sb(f"xr{p}", [P, NT, D]) for p in range(2)]
        tT = st.sb("tT", [P, DT, CH])
        res = st.sb("res", [P, NT, D])
        y = [st.sb(f"y{p}", [P, NT, D]) for p in range(2)]
        gw = st.sb("gw", [P, DT, E])
        gb = st.sb("gb", [P, E])
        bo = st.sb("bo", [P, D])
        lg = st.sb("lg", [P, NT, E])
        mx = st.sb("mx", [P, NT])
        top = st.sb("top", [P, NT, 8])
        topi = st.sb("topi", [P, NT, 8], U32)
        topf = st.sb("topf", [P, NT, 8])
        hot = [st.sb(f"hot{k}", [P, NT, E]) for k in range(K)]
        chosen = st.sb("chosen", [P, NT, E])
        chosenb = st.sb("chosenb", [P, NT, E], BF16)
        unit_sum = st.sb("unit_sum", [P, E])
        count = st.sb("count", [P, E], BF16)
        over = st.sb("over", [P, NT, E])
        slot = st.sb("slot", [P, NT, K])
        valid = st.sb("valid", [P, NT, K])
        ex = st.sb("ex", [P, NT, K if layer == 0 else E])
        sm = st.sb("sm", [P, NT])
        sidx = [st.sb(f"sidx{p}", [P, NT, K], I32) for p in range(2)]
        norm = Norm(st)
        ps_t = st.ps("ps_t", [P, DT, CH])
        ps_w = st.ps("ps_w", [P, 2, 2, D])
        ps_l = st.ps("ps_l", [P, NT, E])
        ps_p = st.ps("ps_p", [P, NT, E])
        setup, setup_v = st.sem("setup"), st.sem("setup_v")
        loaded = [st.sem(f"loaded{p}") for p in range(2)]
        scattered = [st.sem(f"scattered{p}") for p in range(2)]
        stored = [st.sem(f"stored{p}") for p in range(2)]
        turned, copied_a, copied_v = st.sem("turned"), st.sem("copied_a"), st.sem("copied_v")
        out_done, res_done, biased = st.sem("out_done"), st.sem("res_done"), st.sem("biased")
        y_ready, logit_done, logit_read = st.sem("y_ready"), st.sem("logit_done"), st.sem("logit_read")
        exp_in, exp_done = st.sem("exp_in"), st.sem("exp_done")
        chosen_ready, pos_done, count_ready = st.sem("chosen_ready"), st.sem("pos_done"), st.sem("count_ready")
        sidx_ready, own, y_free = st.sem("sidx_ready"), st.sem("own"), st.sem("y_free")
        block = tmp.enter_context(nc.Block())
        NLOAD = G + 1

        @block.sync
        def _(sp):
            def load(b, p):
                src = dram[f"heads{layer}"].rearrange("b g (x n q) e -> b x g q n e", x=2, q=P)
                for g in range(G):
                    sp.dma_start(ao[p][:, :, g, :], src[b, p, g]).then_inc(loaded[p], 16)
                src = x_dram.rearrange("(b x n q) d -> b x q n d", b=B, x=2, q=P)
                sp.dma_start(xr[p][:], src[b, p]).then_inc(loaded[p], 16)

            def store(b, p):
                sp.wait_ge(y_ready, 2 * b + p + 1)
                dst = dram[f"normed{layer}"].rearrange("(b x n q) d -> b x q n d", b=B, x=2, q=P)
                sp.dma_start(dst[b, p], y[p][:]).then_inc(stored[p], 16)

            sp.dma_start(gw[:], ins[f"gate{layer}"].rearrange("(j q) e -> q j e", q=P)).then_inc(setup, 16)
            sp.dma_start(gb[:], ins[f"gbias{layer}"].rearrange("(o e) -> o e", o=1).to_broadcast([P, E]))\
              .then_inc(setup, 16)
            if layer:
                sp.dma_start(bo[:], ins["bo1"].rearrange("(o d) -> o d", o=1).to_broadcast([P, D]))\
                  .then_inc(setup, 16)
            for p in range(2):
                sp.sem_inc(stored[p], 16)
                load(0, p)
            with sp.Fori(0, B - 1) as b:
                for p in range(2):
                    store(b, p)
                    sp.wait_ge(res_done, 2 * b + p + 1)
                    load(b + 1, p)
            for p in range(2):
                store(B - 1, p)
            for p in range(2):
                sp.wait_ge(stored[p], 16 * (B + 1))

        @block.tensor
        def _(pe):
            pe.wait_ge(setup, 16 * (3 if layer else 2))
            with pe.Fori(0, B) as b:
                for p in range(2):
                    u = 2 * b + p
                    pe.wait_ge(loaded[p], 16 * NLOAD * (b + 1))
                    aot = ao[p].rearrange("q n g e -> q n (g e)")
                    for half, src in enumerate((aot, y[p])):
                        if half:
                            pe.wait_ge(y_ready, u + 1)
                        for j in range(DT):
                            pe.wait_ge((copied_a, copied_v)[j], 2 * u + half + 1)
                            for i in range(NT):
                                mm = pe.transpose(ps_t[:, j, i * P:(i + 1) * P], src[:, i, j * P:(j + 1) * P],
                                                  c["ident"][:])
                            mm.then_inc(turned, 1)
                        for j in range(DT):
                            pe.wait_ge((copied_a, copied_v)[j], 2 * u + half + 2)
                        if half == 0:
                            for i in range(NT):
                                for j in range(DT):
                                    mm = pe.matmul(ps_w[:, i // 2, i % 2, :], tT[:, j, i * P:(i + 1) * P],
                                                   w["wo"][:, j, :], start=(j == 0), stop=(j == DT - 1))
                            mm.then_inc(out_done, 1)
                        else:
                            for i in range(NT):
                                for j in range(DT):
                                    mm = pe.matmul(ps_l[:, i, :], tT[:, j, i * P:(i + 1) * P], gw[:, j, :],
                                                   start=(j == 0), stop=(j == DT - 1))
                            mm.then_inc(logit_done, 1)
                    pe.wait_ge(chosen_ready, u + 1)
                    pe.wait_ge(count_ready, u + 1)
                    for i in range(NT):
                        pe.matmul(ps_p[:, i, :], c["before"][:], chosenb[:, i, :], start=True, stop=False)
                        for o in range(i):
                            pe.matmul(ps_p[:, i, :], c["ones"][:], chosenb[:, o, :], start=False, stop=False)
                        mm = pe.matmul(ps_p[:, i, :], c["ones"][:], count[:], start=False, stop=True)
                    mm.then_inc(pos_done, 1)

        @block.scalar
        def _(act):
            act.sem_inc(copied_a, 1)
            with act.Fori(0, B) as b:
                for p in range(2):
                    u = 2 * b + p
                    act.wait_ge(turned, 4 * u + 1)
                    act.copy(tT[:, 0, :], ps_t[:, 0, :]).then_inc(copied_a, 1)
                    norm.scalar(act, u)
                    act.wait_ge(turned, 4 * u + 3)
                    act.copy(tT[:, 0, :], ps_t[:, 0, :]).then_inc(copied_a, 1)
                    act.wait_ge(exp_in, u + 1)
                    act.activation(ex[:], ex[:], ACT.Exp).then_inc(exp_done, 1)

        @block.gpsimd
        def _(pool):
            if layer:
                pool.wait_ge(setup, 48)
            with pool.Fori(0, B) as b:
                for p in range(2):
                    u = 2 * b + p
                    if layer:
                        pool.wait_ge(loaded[p], 16 * NLOAD * (b + 1))
                        for i in range(NT):
                            add = pool.tensor_tensor(xr[p][:, i, :], xr[p][:, i, :], bo[:], ALU.add)
                        add.then_inc(biased, 1)
                    hold(pool, sidx_ready, u + 1)
                    for i in range(NT):
                        for k in range(K):
                            pool.indirect_dma_start(
                                dram[f"slots{layer}"], bass.IndirectOffsetOnAxis(ap=sidx[p][:, i, k:k + 1], axis=0),
                                y[p][:, i, :], None, bounds_check=E * C - 1, oob_is_err=False)\
                                .then_inc(scattered[p], 16)
                    pool.wait_ge(scattered[p], 16 * NT * K * (b + 1))
                    pool.sem_inc(y_free, 1)

        @block.vector
        def _(dve):
            dve.sem_inc(copied_v, 1)
            dve.sem_inc(y_free, 2)
            dve.memset(count[:], 0.0).then_inc(count_ready, 1)
            dve.wait_ge(setup, 16 * (3 if layer else 2))
            NOWN = NORM_OPS + (32 if layer == 0 else 29)
            with dve.Fori(0, B) as b:
                for p in range(2):
                    u = 2 * b + p
                    d = Done(dve, own, u * NOWN)

                    def then(ins):
                        d.did(ins)
                        d.wait()

                    dve.wait_ge(turned, 4 * u + 2)
                    dve.tensor_copy(tT[:, 1, :], ps_t[:, 1, :]).then_inc(copied_v, 1)
                    dve.wait_ge(out_done, u + 1)
                    dve.wait_ge(loaded[p], 16 * NLOAD * (b + 1))
                    if layer:
                        dve.wait_ge(biased, u + 1)
                    dve.tensor_tensor(res.rearrange("q n d -> q (n d)"), ps_w.rearrange("q a i d -> q (a i d)"),
                                      xr[p].rearrange("q n d -> q (n d)"), ALU.add).then_inc(res_done, 1)
                    dve.wait_ge(res_done, u + 1)
                    dve.wait_ge(stored[p], 16 * (b + 1))
                    hold(dve, y_free, u + 1)
                    norm.vector(dve, d, u, res, y[p])
                    d.wait()
                    dve.sem_inc(y_ready, 1)
                    dve.wait_ge(turned, 4 * u + 4)
                    dve.tensor_copy(tT[:, 1, :], ps_t[:, 1, :]).then_inc(copied_v, 1)
                    dve.wait_ge(logit_done, u + 1)
                    then(dve.tensor_tensor(lg[:], ps_l[:], gb[:].unsqueeze(1).to_broadcast([P, NT, E]), ALU.add))
                    if layer:
                        then(dve.tensor_reduce(mx[:], lg[:], AX.X, ALU.max))
                        dve.tensor_tensor(ex[:], lg[:], mx[:].unsqueeze(2).to_broadcast([P, NT, E]),
                                          ALU.subtract).then_inc(exp_in, 1)
                        dve.wait_ge(exp_done, u + 1)
                        then(dve.tensor_reduce(sm[:], ex[:], AX.X, ALU.add))
                        then(dve.reciprocal(sm[:], sm[:]))
                        then(dve.tensor_tensor(lg[:], ex[:], sm[:].unsqueeze(2).to_broadcast([P, NT, E]), ALU.mult))
                    d.hold()
                    for i in range(NT):
                        d.did(dve.max(top[:, i, :], lg[:, i, :]))
                    d.hold()
                    for i in range(NT):
                        d.did(dve.max_index(topi[:, i, :], top[:, i, :], lg[:, i, :]))
                    d.wait()
                    if not layer:
                        dve.tensor_tensor(ex[:], top[:, :, 0:K], top[:, :, 0:1].to_broadcast([P, NT, K]),
                                          ALU.subtract).then_inc(exp_in, 1)
                    then(dve.tensor_copy(topf[:], topi[:]))
                    for k in range(K):
                        d.did(dve.tensor_tensor(hot[k][:], c[f"expert{layer}"][:].unsqueeze(1).to_broadcast([P, NT, E]),
                                                topf[:, :, k:k + 1].to_broadcast([P, NT, E]), ALU.is_equal))
                    d.wait()
                    then(dve.tensor_tensor(chosen[:], hot[0][:], hot[1][:], ALU.add))
                    for k in range(2, K):
                        then(dve.tensor_tensor(chosen[:], chosen[:], hot[k][:], ALU.add))
                    dve.tensor_copy(chosenb[:], chosen[:]).then_inc(chosen_ready, 1)
                    then(dve.tensor_reduce(unit_sum[:], chosen.rearrange("q n e -> q e n"), AX.X, ALU.add))
                    dve.wait_ge(pos_done, u + 1)
                    dve.tensor_tensor(count[:], count[:], unit_sum[:], ALU.add).then_inc(count_ready, 1)
                    then(dve.tensor_scalar(over[:], ps_p[:], float(C), BIG, ALU.is_ge, ALU.mult))
                    then(dve.tensor_tensor(over[:], over[:], ps_p[:], ALU.add))
                    then(dve.tensor_tensor(over[:], over[:], c[f"first{layer}"][:].unsqueeze(1).to_broadcast([P, NT, E]),
                                           ALU.add))
                    for k in range(K):
                        d.did(dve.tensor_tensor(hot[k][:], hot[k][:], over[:], ALU.mult))
                    d.wait()
                    for k in range(K):
                        d.did(dve.tensor_reduce(slot[:, :, k], hot[k][:], AX.X, ALU.add))
                    d.wait()
                    dve.tensor_copy(sidx[p][:], slot[:]).then_inc(sidx_ready, 1)
                    then(dve.tensor_scalar(valid[:], slot[:], BIG, None, ALU.is_lt))
                    then(dve.tensor_tensor(slot[:], slot[:], valid[:], ALU.mult))
                    d.did(dve.tensor_copy(gidx[:, u], slot[:]))
                    if layer:
                        then(dve.tensor_tensor(gate[:, u], top[:, :, 0:K], valid[:], ALU.mult))
                    else:
                        dve.wait_ge(exp_done, u + 1)
                        then(dve.tensor_reduce(sm[:], ex[:], AX.X, ALU.add))
                        then(dve.reciprocal(sm[:], sm[:]))
                        then(dve.tensor_tensor(valid[:], valid[:], sm[:].unsqueeze(2).to_broadcast([P, NT, K]), ALU.mult))
                        then(dve.tensor_tensor(gate[:, u], ex[:], valid[:], ALU.mult))
                    assert d.n == NOWN, (d.n, NOWN)
    return gidx, gate


def experts(nc, c, ins, dram, layer):
    rt = ROUTERS[layer]
    E, C = rt["E"], rt["C"]
    TL = C // P
    NBUF = 4
    with ExitStack() as ctx:
        st = Stage(nc, ctx, f"e{layer}")
        w1 = [st.sb(f"w1_{p}", [P, DT, F]) for p in range(NBUF)]
        w2 = [st.sb(f"w2_{p}", [P, FT, D]) for p in range(NBUF)]
        b2 = [st.sb(f"b2_{p}", [P, D]) for p in range(NBUF)]
        b1 = st.sb("b1", [P, E, FT])
        xs = [st.sb(f"xs{p}", [P, TL, D]) for p in range(NBUF)]
        xT = [st.sb(f"xT{t}", [P, DT, P]) for t in range(2)]
        hT = [st.sb(f"hT{t}", [P, FT, P]) for t in range(2)]
        ys = [st.sb(f"ys{p}", [P, TL, D]) for p in range(2)]
        ps_x = st.ps("ps_x", [P, DT, P])
        ps_h = [[st.ps(f"ps_h{t}{i}", [P, FT // 2, P]) for i in range(2)] for t in range(2)]
        ps_y = [st.ps(f"ps_y{t}", [P, D]) for t in range(2)]
        b1_in = st.sem("b1_in")
        x_in = [st.sem(f"x_in{p}") for p in range(NBUF)]
        w1_in = [st.sem(f"w1_in{p}") for p in range(NBUF)]
        w2_in = [st.sem(f"w2_in{p}") for p in range(NBUF)]
        stored = [st.sem(f"stored{p}") for p in range(2)]
        x_turned, x_copied = st.sem("x_turned"), st.sem("x_copied")
        hid_done, gelu_done = st.sem("hid_done"), st.sem("gelu_done")
        y_done, y_ready = st.sem("y_done"), st.sem("y_ready")
        block = ctx.enter_context(nc.Block())

        def steps(eng, step):
            step(0, 0, 0, True)
            with eng.Fori(0, E // NBUF - 1) as j:
                for p in range(1, NBUF):
                    step(NBUF * j + p, p, j, False)
                step(NBUF * j + NBUF, 0, j + 1, False)
            for p in range(1, NBUF):
                step(E - NBUF + p, p, E // NBUF - 1, False, last=p == NBUF - 1)

        def before(p, j):
            return (p - 1, j) if p else (NBUF - 1, j - 1)

        def after(p, j):
            return (p + 1, j) if p < NBUF - 1 else (0, j + 1)


        @block.sync
        def _(sp):
            def load(e, p):
                sp.dma_start(w1[p][:], ins[f"w1_{layer}"][e].rearrange("(j q) h -> q j h", q=P)).then_inc(w1_in[p], 16)
                sp.dma_start(xs[p][:], dram[f"slots{layer}"].rearrange("(e n q) d -> e q n d", e=E, q=P)[e])\
                  .then_inc(x_in[p], 16)

            def load2(e, p):
                sp.dma_start(w2[p][:], ins[f"w2_{layer}"][e].rearrange("(j q) d -> q j d", q=P)).then_inc(w2_in[p], 16)
                sp.dma_start(b2[p][:], ins[f"b2_{layer}"].rearrange("(o e) d -> e o d", o=1)[e]
                             .to_broadcast([P, D])).then_inc(w2_in[p], 16)

            def step(e, p, more=True):
                if more:
                    sp.wait_ge(hid_done, 2 * TL * (e + 1))
                    load(e + NBUF, p)
                sp.wait_ge(y_ready, 2 + TL * (e + 1))
                if more:
                    load2(e + NBUF, p)
                dst = dram[f"answers{layer}"].rearrange("(e n q) d -> e q n d", e=E, q=P)[e]
                sp.dma_start(dst, ys[p % 2][:]).then_inc(stored[p % 2], 16)

            sp.dma_start(b1[:], ins[f"b1_{layer}"]).then_inc(b1_in, 16)
            for p in range(NBUF):
                load(p, p)
                load2(p, p)
            for p in range(2):
                sp.sem_inc(stored[p], 16)
            with sp.Fori(0, E // NBUF - 1) as j:
                for p in range(NBUF):
                    step(NBUF * j + p, p)
            for p in range(NBUF):
                step(E - NBUF + p, p, more=False)
            for p in range(2):
                sp.wait_ge(stored[p], 16 * (E // 2 + 1))

        @block.tensor
        def _(pe):
            def second(n, t, p, j):
                pe.wait_ge(w2_in[p], 32 * (j + 1))
                pe.wait_ge(y_ready, n + 1)
                pe.wait_ge(gelu_done, FT * (n + 1))
                for f in range(FT):
                    mm = pe.matmul(ps_y[t][:], hT[t][:, f, :], w2[p][:, f, :], start=(f == 0), stop=(f == FT - 1))
                mm.then_inc(y_done, 1)

            def turn(p, j, i):
                if i == 0:
                    pe.wait_ge(x_in[p], 16 * (j + 1))
                for k in range(DT):
                    mm = pe.transpose(ps_x[:, k, :], xs[p][:, i, k * P:(k + 1) * P], c["ident"][:])
                mm.then_inc(x_turned, 1)

            def step(e, p, j, first, last=False):
                for i in range(TL):
                    n = e * TL + i
                    t = (p + i) % 2
                    pe.wait_ge(x_copied, n + 1)
                    if i + 1 < TL:
                        turn(p, j, i + 1)
                    elif not last:
                        turn(*after(p, j), 0)
                    if i == 0:
                        pe.wait_ge(w1_in[p], 16 * (j + 1))
                    for f in range(FT):
                        for k in range(DT):
                            mm = pe.matmul(ps_h[t][f // 4][:, f % 4, :], w1[p][:, k, f * P:(f + 1) * P],
                                           xT[t][:, k, :], start=(k == 0), stop=(k == DT - 1))
                        if f % 4 == 3:
                            mm.then_inc(hid_done, 1)
                    if i:
                        second(n - 1, 1 - t, p, j)
                    elif not first:
                        second(n - 1, 1 - t, *before(p, j))

            turn(0, 0, 0)
            steps(pe, step)
            second(E * TL - 1, 1, NBUF - 1, E // NBUF - 1)

        @block.scalar
        def _(act):
            def step(e, p, j, first, last=False):
                for i in range(TL):
                    n = e * TL + i
                    t = (p + i) % 2
                    if not (first and i < 2):
                        act.wait_ge(y_done, n - 1)
                    for f in range(FT):
                        if f % 4 == 0:
                            hold(act, hid_done, 2 * n + f // 4 + 1)
                        act.activation(hT[t][:, f, :], ps_h[t][f // 4][:, f % 4, :], ACT.Gelu,
                                       bias=b1[:, e, f:f + 1]).then_inc(gelu_done, 1)

            act.wait_ge(b1_in, 16)
            steps(act, step)

        @block.vector
        def _(dve):
            def copy_x(n, t):
                dve.wait_ge(x_turned, n + 1)
                dve.tensor_copy(xT[t][:], ps_x[:]).then_inc(x_copied, 1)

            def answer(n, t, p, j, i):
                dve.wait_ge(y_done, n + 1)
                dve.wait_ge(w2_in[p], 32 * (j + 1))
                if i == 0:
                    dve.wait_ge(stored[p % 2], 16 * (NBUF // 2 * j + p // 2 + 1))
                dve.tensor_tensor(ys[p % 2][:, i, :], ps_y[t][:], b2[p][:], ALU.add).then_inc(y_ready, 1)

            def step(e, p, j, first, last=False):
                for i in range(TL):
                    n = e * TL + i
                    t = (p + i) % 2
                    if not (last and i == TL - 1):
                        copy_x(n + 1, 1 - t)
                    if i:
                        answer(n - 1, 1 - t, p, j, i - 1)
                    elif not first:
                        answer(n - 1, 1 - t, *before(p, j), TL - 1)

            dve.sem_inc(y_ready, 2)
            copy_x(0, 0)
            steps(dve, step)
            answer(E * TL - 1, 1, NBUF - 1, E // NBUF - 1, TL - 1)


def combine(nc, dram, gidx, gate, out_dram, layer):
    K = ROUTERS[layer]["K"]
    with ExitStack() as ctx:
        st = Stage(nc, ctx, f"g{layer}")
        ans = [st.sb(f"ans{p}", [P, NT, K, D]) for p in range(2)]
        gi = [st.sb(f"gi{p}", [P, NT, K], I32) for p in range(2)]
        xr = [st.sb(f"xr{p}", [P, NT, D]) for p in range(2)]
        y = [st.sb(f"y{p}", [P, NT, D]) for p in range(2)]
        norm = Norm(st)
        x_in = [st.sem(f"x_in{p}") for p in range(2)]
        gathered = [st.sem(f"gathered{p}") for p in range(2)]
        stored = [st.sem(f"stored{p}") for p in range(2)]
        summed, own, y_ready, gi_ready = st.sem("summed"), st.sem("own"), st.sem("y_ready"), st.sem("gi_ready")
        block = ctx.enter_context(nc.Block())

        @block.sync
        def _(sp):
            def load(b, p):
                src = dram[f"normed{layer}"].rearrange("(b x n q) d -> b x q n d", b=B, x=2, q=P)
                sp.dma_start(xr[p][:], src[b, p]).then_inc(x_in[p], 16)

            def store(b, p):
                sp.wait_ge(y_ready, 2 * b + p + 1)
                dst = out_dram.rearrange("(b x n q) d -> b x q n d", b=B, x=2, q=P)
                sp.dma_start(dst[b, p], y[p][:]).then_inc(stored[p], 16)

            for p in range(2):
                sp.sem_inc(stored[p], 16)
                load(0, p)
            with sp.Fori(0, B - 1) as b:
                for p in range(2):
                    store(b, p)
                    load(b + 1, p)
            for p in range(2):
                store(B - 1, p)
            for p in range(2):
                sp.wait_ge(stored[p], 16 * (B + 1))

        @block.gpsimd
        def _(pool):
            with pool.Fori(0, B) as b:
                for p in range(2):
                    u = 2 * b + p
                    hold(pool, summed, u + 1)
                    pool.tensor_copy(gi[p][:], gidx[:, u]).then_inc(gi_ready, 1)
                    hold(pool, gi_ready, u + 1)
                    for i in range(NT):
                        for k in range(K):
                            pool.indirect_dma_start(
                                ans[p][:, i, k, :], None, dram[f"answers{layer}"],
                                bass.IndirectOffsetOnAxis(ap=gi[p][:, i, k:k + 1], axis=0))\
                                .then_inc(gathered[p], 16)

        @block.scalar
        def _(act):
            with act.Fori(0, UNITS) as u:
                norm.scalar(act, u)

        @block.vector
        def _(dve):
            dve.sem_inc(summed, 2)
            NOWN = NORM_OPS + NT * (K - 1)
            with dve.Fori(0, B) as b:
                for p in range(2):
                    u = 2 * b + p
                    d = Done(dve, own, u * NOWN)
                    dve.wait_ge(x_in[p], 16 * (b + 1))
                    dve.wait_ge(gathered[p], 16 * NT * K * (b + 1))
                    for k in range(K):
                        for i in range(NT):
                            ins = dve.scalar_tensor_tensor(out=xr[p][:, i, :], in0=ans[p][:, i, k, :],
                                                           scalar=gate[:, u, i, k:k + 1], in1=xr[p][:, i, :],
                                                           op0=ALU.mult, op1=ALU.add)
                            if k < K - 1:
                                d.did(ins)
                        if k < K - 1:
                            d.wait()
                    ins.then_inc(summed, 1)
                    dve.wait_ge(summed, u + 3)
                    hold(dve, stored[p], 16 * (b + 1))
                    norm.vector(dve, d, u, xr[p], y[p])
                    d.wait()
                    dve.sem_inc(y_ready, 1)
                    assert d.n == NOWN, (d.n, NOWN)


def build(nc, ins, out):
    dram = {}
    LAYER_SEMS.clear()

    def scratch(name, shape, dt=F32):
        dram[name] = nc.dram_tensor(f"s_{name}", shape, dt, kind="Internal").ap()

    for layer, rt in enumerate(ROUTERS):
        for n in ("q", "k"):
            halves = layer == 0 and n == "q"
            scratch(f"{n}parts{layer}", (3, S // CH, B, D, CH) if halves else (3, B, D, S), BF16)
        scratch(f"values{layer}", (B, G, S, P))
        scratch(f"heads{layer}", (B, G, S, FG))
        scratch(f"slots{layer}", (rt["E"] * rt["C"], D))
        scratch(f"answers{layer}", (rt["E"] * rt["C"], D))
        scratch(f"normed{layer}", (T, D))
    scratch("mid", (T, D))
    for n in ("q", "k"):
        scratch(f"{n}full", (B, D, S))
    tokens = ins["x"].rearrange("b s d -> (b s) d")
    with ExitStack() as ctx:
        c = constants(nc, ctx, ins, dram)
        with ExitStack() as lctx:
            w = load_weights(nc, lctx, ins, 0)
            project(nc, c, w, tokens, dram, 0)
            attend(nc, c, dram)
            gidx, gate = route(nc, lctx, c, w, ins, dram, tokens, 0)
            experts(nc, c, ins, dram, 0)
            combine(nc, dram, gidx, gate, dram["mid"], 0)
        nc.clear_and_free_semaphores(list(LAYER_SEMS))
        LAYER_SEMS.clear()
        nc.all_engine_barrier()
        with ExitStack() as lctx:
            w = load_weights(nc, lctx, ins, 1)
            project(nc, c, w, dram["mid"], dram, 1)
            attend_linear(nc, c, dram)
            gidx, gate = route(nc, lctx, c, w, ins, dram, dram["mid"], 1)
            experts(nc, c, ins, dram, 1)
            combine(nc, dram, gidx, gate, out.rearrange("b s d -> (b s) d"), 1)


_WEIGHTS = {"wq0": "L0_attn_WQ", "wk0": "L0_attn_WK", "wv0": "L0_attn_WV", "wo0": "L0_attn_WO",
            "wq1": "L1_attn_Wq", "wk1": "L1_attn_Wk", "wv1": "L1_attn_Wv", "wo1": "L1_attn_Wo"}
_PLAIN = {"x": "L0_attn_x", "gate0": "L0_ffn_gate_w", "gbias0": "L0_ffn_gate_b",
          "w1_0": "L0_ffn_w1", "w2_0": "L0_ffn_w2", "b2_0": "L0_ffn_b2",
          "gate1": "L1_ffn_router_w", "gbias1": "L1_ffn_router_b",
          "w1_1": "L1_ffn_w1", "w2_1": "L1_ffn_w2", "b2_1": "L1_ffn_b2", "bo1": "L1_attn_bo"}
_TURNED = {"b1_0": "L0_ffn_b1", "b1_1": "L1_ffn_b1"}


def kernel(**inputs):
    import numpy as np
    import concourse.bacc as bacc
    from concourse.bass_utils import run_bass_kernel_spmd

    nc = bacc.Bacc("TRN2", target_bir_lowering=False, num_devices=1)
    arrays = {}
    for name, key in _WEIGHTS.items():
        arrays[name] = np.ascontiguousarray(np.asarray(inputs[key]).T)
    for name, key in _PLAIN.items():
        arrays[name] = np.ascontiguousarray(inputs[key])
    for name, key in _TURNED.items():
        a = np.asarray(inputs[key])
        arrays[name] = np.ascontiguousarray(a.reshape(a.shape[0], FT, P).transpose(2, 0, 1))
    ins = {n: nc.dram_tensor(n, a.shape, mybir.dt.from_np(a.dtype), kind="ExternalInput").ap()
           for n, a in arrays.items()}
    out = nc.dram_tensor("out", (B, S, D), F32, kind="ExternalOutput").ap()
    build(nc, ins, out)
    r = run_bass_kernel_spmd(nc, [arrays], core_ids=[0])
    return r.results[0]["out"]
```

```python
from contextlib import ExitStack

import concourse.bass as bass
from concourse import mybir

ALU = mybir.AluOpType
ACT = mybir.ActivationFunctionType
AX = mybir.AxisListType
F32 = mybir.dt.float32
BF16 = mybir.dt.bfloat16
I32 = mybir.dt.int32
U32 = mybir.dt.uint32

P = 128
B, S, D = 4, 1024, 256
T = B * S
DT = D // P
ST = S // P
H, DK = 16, 16
HG = 4
G = H // HG
FG = HG * DK
STRIP = P // HG
CH = 512
F = 1024
FT = F // P
EPS = 1e-5
TERMS = ((0, 0), (0, 1), (1, 0), (0, 2), (2, 0), (1, 1))
KR = len(TERMS) * DK
FILL = 2048
BIG = float(1 << 20)

ROUTERS = ({"E": 64, "K": 3, "C": 128}, {"E": 8, "K": 2, "C": 640})


class Done:

    def __init__(self, eng, sem, base=0):
        self.eng, self.sem, self.base, self.n = eng, sem, base, 0

    def did(self, ins):
        ins.then_inc(self.sem, 1)
        self.n += 1
        return self.n

    def wait(self, n=None):
        self.eng.wait_ge(self.sem, self.base + (self.n if n is None else n))

    def hold(self):
        hold(self.eng, self.sem, self.base + self.n)


def hold(eng, sem, value):
    eng.wait_ge(sem, value)
    eng.nop(nofuse=True)


LAYER_SEMS = []


class Stage:

    def __init__(self, nc, ctx, tag):
        self.nc, self.ctx, self.tag = nc, ctx, tag

    def sb(self, name, shape, dt=F32):
        return self.ctx.enter_context(self.nc.sbuf_tensor(f"{self.tag}_{name}", shape, dt))

    def ps(self, name, shape, dt=F32):
        return self.ctx.enter_context(self.nc.psum_tensor(f"{self.tag}_{name}", shape, dt))

    def sem(self, name):
        sem = self.nc.alloc_semaphore(f"{self.tag}_{name}")
        LAYER_SEMS.append(sem)
        return sem


def constants(nc, ctx):
    st = Stage(nc, ctx, "c")
    c = {
        "ident": st.sb("ident", [P, P]), "identb": st.sb("identb", [P, P], BF16),
        "future": st.sb("future", [P, P], BF16),
        "past": st.sb("past", [P, P]),
        "before": st.sb("before", [P, P], BF16),
        "ones": st.sb("ones", [P, P], BF16),
        "own": st.sb("own", [FG, P]),
        "zero": st.sb("zero", [P, FILL]),
    }
    for r, rt in enumerate(ROUTERS):
        c[f"expert{r}"] = st.sb(f"expert{r}", [P, rt["E"]])
        c[f"first{r}"] = st.sb(f"first{r}", [P, rt["E"]])
    with ExitStack() as tmp:
        s2 = Stage(nc, tmp, "ci")
        made, zeroed = s2.sem("made"), s2.sem("zeroed")
        block = tmp.enter_context(nc.Block())

        @block.gpsimd
        def _(pool):
            d = Done(pool, made)
            d.did(pool.memset(c["ident"][:], 0.0))
            d.did(pool.memset(c["identb"][:], 0.0))
            d.did(pool.memset(c["future"][:], 0.0))
            d.did(pool.memset(c["past"][:], 1.0))
            d.did(pool.memset(c["before"][:], 1.0))
            d.did(pool.memset(c["ones"][:], 1.0))
            d.did(pool.memset(c["own"][:], 1.0))
            for r, rt in enumerate(ROUTERS):
                d.did(pool.iota(c[f"expert{r}"][:], [[1, rt["E"]]], base=0, channel_multiplier=0,
                                allow_small_or_imprecise_dtypes=True))
                d.did(pool.iota(c[f"first{r}"][:], [[rt["C"], rt["E"]]], base=0, channel_multiplier=0,
                                allow_small_or_imprecise_dtypes=True))
            d.wait()
            for name in ("ident", "identb"):
                d.did(pool.affine_select(out=c[name][:], in_=c[name][:], compare_op=ALU.not_equal, fill=1.0,
                                         base=0, pattern=[[-1, P]], channel_multiplier=1))
            d.did(pool.affine_select(out=c["future"][:], in_=c["future"][:], compare_op=ALU.is_ge, fill=-1e30,
                                     base=0, pattern=[[-1, P]], channel_multiplier=1))
            d.did(pool.affine_select(out=c["past"][:], in_=c["past"][:], compare_op=ALU.is_ge, fill=0.0,
                                     base=0, pattern=[[1, P]], channel_multiplier=-1))
            d.did(pool.affine_select(out=c["before"][:], in_=c["before"][:], compare_op=ALU.is_gt, fill=0.0,
                                     base=0, pattern=[[1, P]], channel_multiplier=-1))
            d.did(pool.affine_select(out=c["own"][:], in_=c["own"][:], compare_op=ALU.is_ge, fill=0.0,
                                     base=0, pattern=[[-DK, HG], [0, STRIP]], channel_multiplier=1))
            d.wait()
            d.did(pool.affine_select(out=c["own"][:], in_=c["own"][:], compare_op=ALU.is_ge, fill=0.0,
                                     base=DK - 1, pattern=[[DK, HG], [0, STRIP]], channel_multiplier=-1))
            d.wait()

        @block.vector
        def _(dve):
            dve.memset(c["zero"][:], 0.0).then_inc(zeroed, 1)
            dve.wait_ge(zeroed, 1)
    return c


def weights(nc, ctx, layer):
    st = Stage(nc, ctx, f"w{layer}")
    return {k: st.sb(k, [P, DT, D]) for k in ("wq", "wk", "wv", "wo")}


def project(nc, c, w, ins, x_dram, dram):
    NT = CH // P
    PER = S // CH
    NSTORE = 6 + G
    with ExitStack() as ctx:
        st = Stage(nc, ctx, "p")
        xin = [st.sb(f"xin{p}", [P, NT, D]) for p in range(PER)]
        xT = st.sb("xT", [P, DT, CH])
        rest = [st.sb(f"rest{r}", [P, CH]) for r in range(4)]
        parts = [[st.sb(f"part{p}_{k}", [P, 4, CH], BF16) for k in range(3)] for p in range(PER)]
        vpad = [st.sb(f"vpad{p}", [P, NT, G, P]) for p in range(PER)]
        ps_x = st.ps("ps_x", [P, DT, CH])
        ps_qk = st.ps("ps_qk", [P, 4, CH])
        ps_v = st.ps("ps_v", [P, 2, 2, D])
        w_in = [st.sem(f"{k}_in") for k in w]
        x_loaded = [st.sem(f"x_loaded{p}") for p in range(PER)]
        stored = [st.sem(f"stored{p}") for p in range(PER)]
        xT_psum, xT_a, xT_v = st.sem("xT_psum"), st.sem("xT_a"), st.sem("xT_v")
        qk_psum, v_psum, v_ready = st.sem("qk_psum"), st.sem("v_psum"), st.sem("v_ready")
        hi_ready, rest_ready = st.sem("hi_ready"), st.sem("rest_ready")
        mid_ready, pads = st.sem("mid_ready"), st.sem("pads")
        block = ctx.enter_context(nc.Block())

        @block.sync
        def _(sp):
            for p in range(PER):
                sp.sem_inc(stored[p], 16)

            def load(b, p):
                sp.dma_start(xin[p][:], x_dram[bass.ds(b * S + p * CH, CH), :]
                             .rearrange("(n q) d -> q n d", q=P)).then_inc(x_loaded[p], 16)

            def store(b, p):
                sp.wait_ge(mid_ready, 8 * (PER * b + p) + 16)
                for o, name in enumerate(("q", "k")):
                    for k in range(3):
                        dst = dram[f"{name}parts0"]
                        dst = dst[k, b, :, p * CH:(p + 1) * CH] if o else dst[k, p, b]
                        sp.dma_start(dst.rearrange("(j q) t -> q j t", q=P),
                                     parts[p][k][:, 2 * o:2 * o + 2, :]).then_inc(stored[p], 16)
                sp.wait_ge(v_ready, 2 * (PER * b + p) + 4)
                for g in range(G):
                    dst = dram["values0"][b, g, p * CH:(p + 1) * CH, :]
                    sp.dma_start(dst.rearrange("(n q) e -> q n e", q=P),
                                 vpad[p][:, :, g, :]).then_inc(stored[p], 16)

            load(0, 0)
            for k, sem in zip(w, w_in):
                sp.dma_start(w[k][:], ins[f"{k}0"].rearrange("(j p) f -> p j f", p=P)).then_inc(sem, 16)
            for p in range(1, PER):
                load(0, p)
            with sp.Fori(0, B - 1) as b:
                for p in range(PER):
                    store(b, p)
                    sp.wait_ge(xT_psum, 2 * (PER * b + p) + 2)
                    load(b + 1, p)
            for p in range(PER):
                store(B - 1, p)
            for p in range(PER):
                sp.wait_ge(stored[p], 16 * (B * NSTORE + 1))
            sp.wait_ge(w_in[3], 16)

        @block.tensor
        def _(pe):
            for sem in w_in[:3]:
                pe.wait_ge(sem, 16)
            with pe.Fori(0, B) as b:
                for p in range(PER):
                    n = PER * b + p
                    pe.wait_ge(x_loaded[p], 16 * (b + 1))
                    for j in range(DT):
                        pe.wait_ge((xT_a, xT_v)[j], n + 1)
                        for i in range(NT):
                            mm = pe.transpose(ps_x[:, j, i * P:(i + 1) * P], xin[p][:, i, j * P:(j + 1) * P],
                                              c["ident"][:])
                        mm.then_inc(xT_psum, 1)
                    for j in range(DT):
                        pe.wait_ge((xT_a, xT_v)[j], n + 2)
                    for r in range(4):
                        wt = w[("wq", "wk")[r // 2]]
                        pe.wait_ge(hi_ready, 4 * n + r + 1)
                        pe.wait_ge(rest_ready, 4 * n + r + 1)
                        for j in range(DT):
                            mm = pe.matmul(ps_qk[:, r, :], wt[:, j, (r % 2) * P:(r % 2 + 1) * P], xT[:, j, :],
                                           start=(j == 0), stop=(j == DT - 1))
                        mm.then_inc(qk_psum, 1)
                    for v in range(2):
                        pe.wait_ge(v_ready, 2 * n + v + 1)
                        for i in range(2):
                            for j in range(DT):
                                mm = pe.matmul(ps_v[:, v, i, :], xT[:, j, (2 * v + i) * P:(2 * v + i + 1) * P],
                                               w["wv"][:, j, :], start=(j == 0), stop=(j == DT - 1))
                        mm.then_inc(v_psum, 1)

        @block.scalar
        def _(act):
            act.sem_inc(xT_a, 1)
            act.sem_inc(hi_ready, 4)
            with act.Fori(0, B) as b:
                for p in range(PER):
                    n = PER * b + p
                    act.wait_ge(xT_psum, 2 * n + 1)
                    act.copy(xT[:, 0, :], ps_x[:, 0, :]).then_inc(xT_a, 1)
                    act.wait_ge(stored[p], 16 * (NSTORE * b + 1))
                    for r in range(4):
                        act.wait_ge(qk_psum, 4 * n + r + 1)
                        act.copy(parts[p][0][:, r, :], ps_qk[:, r, :]).then_inc(hi_ready, 1)

        @block.vector
        def _(dve):
            dve.sem_inc(xT_v, 1)
            dve.sem_inc(rest_ready, 4)
            dve.sem_inc(v_ready, 2)
            d = Done(dve, pads)
            for p in range(PER):
                strips = vpad[p].rearrange("q n g (h e) -> q (n g h) e", h=HG)
                d.did(dve.memset(strips[:, :, DK:DK + 1], 1.0))
                d.did(dve.memset(strips[:, :, DK + 1:STRIP], 0.0))
            with dve.Fori(0, B) as b:
                for p in range(PER):
                    n = PER * b + p
                    dve.wait_ge(xT_psum, 2 * n + 2)
                    dve.tensor_copy(xT[:, 1, :], ps_x[:, 1, :]).then_inc(xT_v, 1)
                    dve.wait_ge(stored[p], 16 * (NSTORE * b + 1))
                    for r in range(4):
                        dve.wait_ge(hi_ready, 4 * n + r + 5)
                        dve.wait_ge(mid_ready, 8 * n + 2 * r + 2)
                        dve.tensor_tensor(rest[r][:], ps_qk[:, r, :], parts[p][0][:, r, :],
                                          ALU.subtract).then_inc(rest_ready, 1)
                    if p == 0:
                        d.wait()
                    for v in range(2):
                        dve.wait_ge(v_psum, 2 * n + v + 1)
                        for i in range(2):
                            cp = dve.tensor_copy(
                                vpad[p][:, 2 * v + i].rearrange("q g (h e) -> q (g h) e", h=HG)[:, :, 0:DK],
                                ps_v[:, v, i, :].rearrange("q (h e) -> q h e", e=DK))
                        cp.then_inc(v_ready, 1)

        @block.gpsimd
        def _(pool):
            pool.sem_inc(mid_ready, 8)
            with pool.Fori(0, B) as b:
                for p in range(PER):
                    n = PER * b + p
                    pool.wait_ge(stored[p], 16 * (NSTORE * b + 1))
                    for r in range(4):
                        hold(pool, rest_ready, 4 * n + r + 5)
                        pool.tensor_copy(parts[p][1][:, r, :], rest[r][:]).then_inc(mid_ready, 1)
                        pool.wait_ge(mid_ready, 8 * n + 2 * r + 9)
                        pool.tensor_tensor(parts[p][2][:, r, :], rest[r][:], parts[p][1][:, r, :],
                                           ALU.subtract).then_inc(mid_ready, 1)


def attend(nc, c, dram):
    N = B * G
    NBUF = 3
    assert (N - 1) % NBUF == 0
    QT = CH // P
    HALVES = S // CH
    NLOAD = (HALVES + 1) * len(TERMS) + 1
    PIECES = [rt["E"] * rt["C"] * D // (P * FILL) for rt in ROUTERS]
    assert PIECES == [2 * ((N - 1) // NBUF - 1), (N - 1) // NBUF]
    with ExitStack() as ctx:
        st = Stage(nc, ctx, "a")
        qop = [st.sb(f"qop{p}", [KR + 2, HALVES, HG, CH], BF16) for p in range(NBUF)]
        kop = [st.sb(f"kop{p}", [KR + 2, HG, S], BF16) for p in range(NBUF)]
        val = [st.sb(f"val{p}", [P, ST, P]) for p in range(NBUF)]
        prob = st.sb("prob", [P, 4, HG, CH])
        mlow = st.sb("mlow", [P, HG, QT])
        mpart = st.sb("mpart", [P, HG, QT, 2])
        mhigh = st.sb("mhigh", [P, HG, QT])
        mrow = [st.sb(f"mrow{h}", [HG * QT, 2, P], BF16) for h in range(HALVES)]
        o_sb = [st.sb(f"o_sb{h}", [P, CH]) for h in range(HALVES)]
        recip = st.sb("recip", [P, QT, HG])
        ao = [st.sb(f"ao{h}", [P, QT, FG]) for h in range(HALVES)]
        ps_1 = [st.ps(f"ps_1{i}", [P, CH]) for i in range(2)]
        ps_2 = [st.ps(f"ps_2{i}", [P, 2, CH]) for i in range(2)]
        ps_o = st.ps("ps_o", [P, CH])
        ps_t = st.ps("ps_t", [P, QT, P])
        loaded = [st.sem(f"loaded{p}") for p in range(NBUF)]
        rows_in = [st.sem(f"rows_in{h}") for h in range(HALVES)]
        ao_out = [st.sem(f"ao_out{h}") for h in range(HALVES)]
        s1, maxed = st.sem("s1"), st.sem("maxed")
        s2, exped, masked, used = st.sem("s2"), st.sem("exped"), st.sem("masked"), st.sem("used")
        o_copied = [st.sem(f"o_copied{h}") for h in range(HALVES)]
        t_done, filled = st.sem("t_done"), st.sem("filled")
        mrow_ready, ao_ready = st.sem("mrow_ready"), st.sem("ao_ready")
        hi_done, comb, rec, setup = st.sem("hi_done"), st.sem("comb"), st.sem("rec"), st.sem("setup")
        block = ctx.enter_context(nc.Block())

        def tile(q, k0, kn):
            nh = 1 << (CH // kn).bit_length() - 1
            return [(h, nh, q, k0, kn) for h in range(0, HG, nh)]

        pass1 = [unit for q in range(QT) for unit in tile(q, 0, (q + 1) * P)]
        NLOW = len(pass1)
        for q in range(QT, ST):
            pass1 += tile(q, 0, CH) + tile(q, CH, (q + 1) * P - CH)
        width = [nh * kn for _, nh, _, _, kn in pass1]
        N1 = len(pass1)
        pass2 = [(j, k, max(j * CH, k * P), (j + 1) * CH - max(j * CH, k * P))
                 for j in range(HALVES) for k in range(QT * (j + 1))]
        N2 = len(pass2)
        diag = [n for n, (j, k, q0, w) in enumerate(pass2) if q0 == k * P]
        LAG = 2

        def make_plan(ahead):
            work = []
            for n in range(LAG, N2):
                w = pass2[n][3]
                work += [(("s2", n, u), 3 * w) for u in range(2)]
                work.append((("av", n - LAG), 2 * pass2[n - LAG][3]))
                if n == QT + LAG:
                    work.insert(-1, (("heads", 0), 512))
            tail = []
            if ahead:
                tail += [("s2", N2, 0), ("s2", N2, 1), ("av", N2 - 2), ("av", N2 - 1),
                         ("s2", N2 + 1, 0), ("s2", N2 + 1, 1)]
            else:
                tail += [("av", N2 - 2), ("av", N2 - 1)]
            tail.append(("heads", 1))
            if not ahead:
                return [a for a, _ in work] + tail
            plan, total, dve_total = [], sum(c_ for _, c_ in work), sum(w + 60 for w in width)
            done, dve, i = 0, 0, 0
            for atom, cost in work:
                plan.append(atom)
                done += cost
                while i < N1 and (dve + (width[i] + 60) / 2) * total <= done * dve_total:
                    dve += width[i] + 60
                    plan.append(("p1", i))
                    i += 1
                    if i == NLOW + 2:
                        plan.append(("max", 0))
            plan += [("p1", k) for k in range(i, N1)]
            return plan + tail[:2] + [("max", 1)] + tail[2:]

        full_plan, last_plan = make_plan(True), make_plan(False)

        def turns(plan):
            return [a for a in plan if a[0] in ("heads", "max")]

        def freed(eng, s, plan, use):
            order = turns(plan)
            k = order.index(use)
            if k == 0:
                eng.wait_ge(mrow_ready, HALVES * (s + 1))
                eng.wait_ge(ao_ready, HALVES * s + 1)
            elif order[k - 1][0] == "heads":
                eng.wait_ge(ao_ready, 1 + HALVES * s + order[k - 1][1] + 1)
            else:
                eng.wait_ge(mrow_ready, HALVES * (s + 1) + order[k - 1][1] + 1)

        def turned(eng, s, plan, use):
            eng.wait_ge(t_done, HALVES + 4 * s + turns(plan).index(use) + 1)

        @block.sync
        def _(sp):
            def load(s, p):
                for t, (qpart, kpart) in enumerate(TERMS):
                    rows = slice(t * DK, (t + 1) * DK)
                    for x in range(HALVES):
                        src = dram["qparts0"].rearrange("k x b (g h e) t -> k x (b g) e h t", g=G, h=HG)
                        sp.dma_start(qop[p][rows, x], src[qpart, x, s]).then_inc(loaded[p], 16)
                    src = dram["kparts0"].rearrange("k b (g h e) t -> k (b g) e h t", g=G, h=HG)[kpart, s]
                    sp.dma_start(kop[p][rows], src).then_inc(loaded[p], 16)
                src = dram["values0"].rearrange("b g (n q) e -> (b g) q n e", q=P)[s]
                sp.dma_start(val[p][:], src).then_inc(loaded[p], 16)

            def rows(s, p, half):
                sp.wait_ge(mrow_ready, HALVES * s + half + 1)
                for r in range(2):
                    sp.dma_start(qop[p][KR + r:KR + r + 1, half].rearrange("o h t -> o (h t)"),
                                 mrow[half][:, r, :]).then_inc(rows_in[half], 16)

            def out(s, half):
                sp.wait_ge(ao_ready, 1 + HALVES * s + half + 1)
                dst = dram["heads0"].rearrange("b g (x n q) e -> (b g) x q n e", x=HALVES, q=P)
                sp.dma_start(dst[s, half], ao[half][:]).then_inc(ao_out[half], 16)

            def fill(r, n):
                dst = dram[f"slots{r}"].rearrange("(n p m) d -> n p (m d)", p=P, m=FILL // D)
                sp.dma_start(dst[n], c["zero"][:]).then_inc(filled, 16)

            def step(s, p, loads=True):
                for kind, h in turns(full_plan)[:-1]:
                    if kind == "heads":
                        out(s, h)
                    else:
                        rows(s + 1, (p + 1) % NBUF, h)
                if loads:
                    sp.wait_ge(used, 4 + N2 * (s + 1))
                    load(s + NBUF, p)
                out(s, 1)

            for h in range(HALVES):
                sp.sem_inc(ao_out[h], 16)
                sp.sem_inc(rows_in[h], 32)
            for p in range(NBUF):
                load(p, p)
            rows(0, 0, 0)
            rows(0, 0, 1)
            with sp.Fori(0, (N - 1) // NBUF - 1) as j:
                for p in range(NBUF):
                    step(j * NBUF + p, p)
                    if p < 2:
                        fill(0, 2 * j + p)
                    else:
                        fill(1, j)
            fill(1, PIECES[1] - 1)
            for s in range(N - 1 - NBUF, N - 1):
                step(s, s % NBUF, loads=(s + NBUF < N))
            out(N - 1, 0)
            out(N - 1, 1)
            for h in range(HALVES):
                sp.wait_ge(ao_out[h], 16 * (N + 1))
            sp.wait_ge(filled, 16 * sum(PIECES))

        @block.tensor
        def _(pe):
            def scores1(s, p, i, first=False):
                h0, nh, q, k0, kn = pass1[i]
                if not (first and i < 2):
                    pe.wait_ge(maxed, N1 * s + i - 1)
                last = k0 + kn == (q + 1) * P
                for h in range(nh):
                    dst = ps_1[i % 2][:, h * kn:(h + 1) * kn]
                    mm = pe.matmul(dst, qop[p][0:KR, q // QT, h0 + h, (q % QT) * P:(q % QT + 1) * P],
                                   kop[p][0:KR, h0 + h, k0:k0 + kn], start=True, stop=not last)
                    if last:
                        mm = pe.matmul(dst[:, kn - P:kn], c["identb"][:], c["future"][:], start=False, stop=True)
                mm.then_inc(s1, 1)

            def scores2(s, p, n, u):
                j, k, q0, w = pass2[n]
                if u == 0 and (n == 0 or pass2[n - 1][0] != j):
                    pe.wait_ge(rows_in[j], 32 * (s + 2))
                pe.wait_ge(exped, 2 * (N2 * s + n) + u + 1)
                for h in range(2):
                    mm = pe.matmul(ps_2[u][:, h, 0:w], kop[p][:, 2 * u + h, k * P:(k + 1) * P],
                                   qop[p][:, j, 2 * u + h, q0 - j * CH:q0 - j * CH + w], start=True, stop=True)
                mm.then_inc(s2, 1)

            def values(s, p, n):
                j, k, q0, w = pass2[n]
                last = k == QT * (j + 1) - 1
                if k == 0:
                    pe.wait_ge(o_copied[1 - j], s + 1)
                pe.wait_ge(exped, 2 * (N2 * s + n) + 4)
                if n in diag:
                    pe.wait_ge(masked, len(diag) * s + diag.index(n) + 1)
                o0 = q0 - j * CH
                for h in range(HG):
                    sl = slice(h * STRIP, (h + 1) * STRIP)
                    mm = pe.matmul(ps_o[sl, o0:o0 + w], val[p][:, k, sl], prob[:, n % 4, h, 0:w],
                                   start=(k == 0), stop=last)
                mm.then_inc(used, 1)

            def turn_heads(s, plan, j):
                pe.wait_ge(o_copied[j], s + 1 + j)
                freed(pe, s, plan, ("heads", j))
                for i in range(QT):
                    mm = pe.transpose(ps_t[:, i, :], o_sb[j][:, i * P:(i + 1) * P], c["ident"][:])
                mm.then_inc(t_done, 1)

            def turn_max(s, half):
                if half:
                    pe.wait_ge(comb, s + 1)
                else:
                    pe.wait_ge(maxed, N1 * s + NLOW)
                m = (mlow, mhigh)[half].rearrange("p h q -> p (h q)")
                pe.transpose(ps_t[0:HG * QT, 0, :], m, c["ident"][:]).then_inc(t_done, 1)

            def step(s, p, plan):
                pn = (p + 1) % NBUF
                for atom in plan:
                    kind, i = atom[:2]
                    if kind == "s2" and i < N2:
                        scores2(s, p, i, atom[2])
                    elif kind == "s2":
                        scores2(s + 1, pn, i - N2, atom[2])
                    elif kind == "p1":
                        scores1(s + 1, pn, i)
                    elif kind == "av":
                        values(s, p, i)
                    elif kind == "max":
                        freed(pe, s, plan, atom)
                        turn_max(s + 1, i)
                    else:
                        turn_heads(s, plan, i)

            pe.sem_inc(used, 4)
            pe.wait_ge(loaded[0], 16 * NLOAD)
            for i in range(N1):
                scores1(0, 0, i, first=True)
            turn_max(0, 0)
            pe.wait_ge(mrow_ready, 1)
            turn_max(0, 1)
            pe.wait_ge(setup, 1)
            for n in range(LAG):
                for u in range(2):
                    scores2(0, 0, n, u)
            with pe.Fori(0, (N - 1) // NBUF) as j:
                for p in range(NBUF):
                    pe.wait_ge(loaded[(p + 1) % NBUF], 16 * NLOAD * (j + 1 + (p + 1) // NBUF))
                    step(j * NBUF + p, p, full_plan)
            step(N - 1, (N - 1) % NBUF, last_plan)

        @block.scalar
        def _(act):
            def step(s):
                for n, (j, k, q0, w) in enumerate(pass2):
                    act.wait_ge(used, N2 * s + n + 1)
                    for u in range(2):
                        act.wait_ge(s2, 2 * (N2 * s + n) + u + 1)
                        act.activation(prob[:, n % 4, 2 * u:2 * u + 2, 0:w], ps_2[u][:, :, 0:w], ACT.Exp,
                                       scale=DK ** -0.5).then_inc(exped, 1)
                    if n == QT + 1:
                        act.wait_ge(used, 4 + N2 * s + QT)
                        act.wait_ge(ao_ready, HALVES * s + 1)
                        act.copy(o_sb[0][:], ps_o[:]).then_inc(o_copied[0], 1)

            act.sem_inc(exped, 2)
            with act.Fori(0, N) as s:
                step(s)

        @block.gpsimd
        def _(pool):
            for p in range(NBUF):
                ins = pool.memset(kop[p][KR:KR + 2, :, :], 1.0)
            ins.then_inc(setup, 1)
            with pool.Fori(0, N) as s:
                for n in diag:
                    hold(pool, exped, 2 * (N2 * s + n) + 4)
                    blk = prob[:, n % 4, :, 0:P]
                    pool.affine_select(out=blk, in_=blk, compare_op=ALU.is_ge, fill=0.0, base=0,
                                       pattern=[[0, HG], [1, P]], channel_multiplier=-1).then_inc(masked, 1)

        @block.vector
        def _(dve):
            def maxima(s, i):
                h, nh, q, k0, kn = pass1[i]
                dst = mlow[:, h:h + nh, q] if q < QT else mpart[:, h:h + nh, q - QT, k0 // CH]
                src = ps_1[i % 2][:, 0:nh * kn].rearrange("p (h k) -> p h k", h=nh)
                dve.wait_ge(s1, N1 * s + i + 1)
                dve.tensor_reduce(dst, src, AX.X, ALU.max).then_inc(maxed, 1)

            def combine(s):
                dve.wait_ge(maxed, N1 * (s + 1))
                dve.tensor_reduce(mhigh[:], mpart[:], AX.X, ALU.max).then_inc(comb, 1)

            def make_rows(s, half):
                dve.wait_ge(rows_in[half], 32 * (s + 1))
                src = ps_t[0:HG * QT, 0, :]
                dve.tensor_scalar(mrow[half][:, 0, :], src, -1.0, None, ALU.mult).then_inc(hi_done, 1)
                dve.wait_ge(hi_done, HALVES * s + half + 1)
                dve.scalar_tensor_tensor(out=mrow[half][:, 1, :], in0=src, scalar=-1.0, in1=mrow[half][:, 0, :],
                                         op0=ALU.mult, op1=ALU.subtract).then_inc(mrow_ready, 1)

            def divide(s, plan, j):
                if j:
                    dve.wait_ge(used, 4 + N2 * (s + 1))
                    dve.tensor_copy(o_sb[1][:], ps_o[:]).then_inc(o_copied[1], 1)
                turned(dve, s, plan, ("heads", j))
                heads = ps_t.rearrange("p n (h e) -> p n h e", h=HG)
                dve.reciprocal(recip[:], heads[:, :, :, DK]).then_inc(rec, 1)
                dve.wait_ge(rec, HALVES * s + j + 1)
                dve.wait_ge(ao_out[j], 16 * (s + 1))
                dve.tensor_tensor(ao[j].rearrange("p n (h e) -> p n h e", h=HG), heads[:, :, :, 0:DK],
                                  recip[:].unsqueeze(3).to_broadcast([P, QT, HG, DK]),
                                  ALU.mult).then_inc(ao_ready, 1)

            def step(s, plan):
                DELAY = 1
                queue = []

                def serve(atom):
                    if atom[0] == "heads":
                        divide(s, plan, atom[1])
                    else:
                        turned(dve, s, plan, atom)
                        make_rows(s + 1, atom[1])

                order = []
                for atom in plan:
                    if atom[0] == "p1":
                        order.append(atom)
                        for q in queue:
                            q[1] -= 1
                        while queue and queue[0][1] <= 0:
                            order.append(queue.pop(0)[0])
                    elif atom[0] in ("heads", "max"):
                        queue.append([atom, DELAY])
                order += [q[0] for q in queue]
                for atom in order:
                    if atom[0] == "p1":
                        maxima(s + 1, atom[1])
                        if atom[1] == N1 - 1:
                            combine(s + 1)
                    else:
                        serve(atom)

            dve.sem_inc(o_copied[1], 1)
            dve.sem_inc(ao_ready, 1)
            for i in range(N1):
                maxima(0, i)
            dve.wait_ge(t_done, 1)
            make_rows(0, 0)
            combine(0)
            dve.wait_ge(t_done, 2)
            make_rows(0, 1)
            with dve.Fori(0, N - 1) as s:
                step(s, full_plan)
            step(N - 1, last_plan)


def attend_linear(nc, c, dram):
    N = B * G
    QT = CH // P
    HALVES = S // CH
    NLOAD = 2 * len(TERMS) + 3
    NBUF = 3
    assert (N - 1) % NBUF == 0
    with ExitStack() as ctx:
        st = Stage(nc, ctx, "l")
        qop = [st.sb(f"qop{p}", [KR, HG, S], BF16) for p in range(NBUF)]
        kop = [st.sb(f"kop{p}", [KR, HG, S], BF16) for p in range(NBUF)]
        val = [st.sb(f"val{p}", [P, ST, P]) for p in range(NBUF)]
        qf = [st.sb(f"qf{p}", [FG, S]) for p in range(NBUF)]
        kf = [st.sb(f"kf{p}", [FG, S]) for p in range(NBUF)]
        kt = [st.sb(f"kt{p}", [P, ST, FG]) for p in range(NBUF)]
        att = [st.sb(f"att{i}", [P, HG, P]) for i in range(2)]
        state = [st.sb(f"state{i}", [FG, P]) for i in range(2)]
        o_sb = st.sb("o_sb", [P, CH])
        den = st.sb("den", [P, QT, HG])
        ao = [st.sb(f"ao{h}", [P, QT, FG]) for h in range(HALVES)]
        ps_a = [st.ps(f"ps_a{i}", [P, HG, P]) for i in range(2)]
        ps_o = [st.ps(f"ps_o{i}", [P, CH]) for i in range(2)]
        ps_s = st.ps("ps_s", [FG, P])
        ps_t = st.ps("ps_t", [P, QT, P])
        ps_k = st.ps("ps_k", [P, ST, FG])
        loaded = [st.sem(f"loaded{p}") for p in range(NBUF)]
        ao_out = [st.sem(f"ao_out{h}") for h in range(HALVES)]
        k_turned, k_copied = st.sem("k_turned"), st.sem("k_copied")
        scored, att_ready = st.sem("scored"), st.sem("att_ready")
        state_sum, state_ready = st.sem("state_sum"), st.sem("state_ready")
        o_done, o_copied = st.sem("o_done"), st.sem("o_copied")
        t_done, den_ready, ao_ready = st.sem("t_done"), st.sem("den_ready"), st.sem("ao_ready")
        block = ctx.enter_context(nc.Block())

        @block.sync
        def _(sp):
            def load(s, p):
                for t, (qpart, kpart) in enumerate(TERMS):
                    rows = slice(t * DK, (t + 1) * DK)
                    for op, name, part in ((qop, "qparts1", qpart), (kop, "kparts1", kpart)):
                        src = dram[name].rearrange("k b (g h e) t -> k (b g) e h t", g=G, h=HG)[part, s]
                        sp.dma_start(op[p][rows], src).then_inc(loaded[p], 16)
                sp.dma_start(val[p][:], dram["values1"].rearrange("b g (n q) e -> (b g) q n e", q=P)[s])\
                  .then_inc(loaded[p], 16)
                for op, name in ((qf, "qfull"), (kf, "kfull")):
                    src = dram[name].rearrange("b (g f) t -> (b g) f t", g=G)
                    sp.dma_start(op[p][:], src[s]).then_inc(loaded[p], 16)

            def out(s, half):
                sp.wait_ge(ao_ready, 1 + HALVES * s + half + 1)
                dst = dram["heads1"].rearrange("b g (x n q) e -> (b g) x q n e", x=HALVES, q=P)
                sp.dma_start(dst[s, half], ao[half][:]).then_inc(ao_out[half], 16)

            for h in range(HALVES):
                sp.sem_inc(ao_out[h], 16)
            for p in range(NBUF):
                load(p, p)

            def step(s, p, loads=True):
                out(s, 0)
                if loads:
                    sp.wait_ge(o_done, ST * (s + 1))
                    load(s + NBUF, p)
                out(s, 1)

            with sp.Fori(0, (N - 1) // NBUF - 1) as j:
                for p in range(NBUF):
                    step(NBUF * j + p, p)
            for s in range(N - 1 - NBUF, N):
                step(s, s % NBUF, loads=s + NBUF < N)
            for h in range(HALVES):
                sp.wait_ge(ao_out[h], 16 * (N + 1))

        def steps(eng, step):
            step(0, 0, 0, first=True)
            with eng.Fori(0, (N - 1) // NBUF - 1) as j:
                for i in range(1, NBUF + 1):
                    step(NBUF * j + i, i % NBUF, j + i // NBUF)
            for s in range(N - NBUF, N):
                step(s, s % NBUF, s // NBUF, last=(s == N - 1))

        @block.tensor
        def _(pe):
            def turn_keys(s, p, use):
                pe.wait_ge(loaded[p], 16 * NLOAD * (use + 1))
                hold(pe, k_copied, s + 1)
                for i in range(ST):
                    mm = pe.transpose(ps_k[:, i, :], kf[p][:, i * P:(i + 1) * P], c["ident"][0:FG, 0:FG])
                mm.then_inc(k_turned, 1)

            def scores(s, p, n):
                pe.wait_ge(att_ready, ST * s + n + 1)
                for h in range(HG):
                    mm = pe.matmul(ps_a[n % 2][:, h, :], kop[p][:, h, n * P:(n + 1) * P],
                                   qop[p][:, h, n * P:(n + 1) * P], start=True, stop=True)
                mm.then_inc(scored, 1)

            def add_state(s, p, n):
                pe.wait_ge(state_ready, (ST - 1) * s + n + 1)
                pe.matmul(ps_s[:], kt[p][:, n, :], val[p][:, n, :], start=(n == 0), stop=True,
                          skip_group_check=True).then_inc(state_sum, 1)

            def outputs(s, p, n):
                half, o0 = n // QT, (n % QT) * P
                if n % QT == 0:
                    pe.wait_ge(o_copied, HALVES * s + half + 1)
                if n:
                    pe.wait_ge(state_ready, (ST - 1) * s + n + 1)
                    pe.matmul(ps_o[half][:, o0:o0 + P], state[n % 2][:], qf[p][:, n * P:(n + 1) * P],
                              start=True, stop=False)
                pe.wait_ge(att_ready, ST * s + n + 3)
                for h in range(HG):
                    sl = slice(h * STRIP, (h + 1) * STRIP)
                    mm = pe.matmul(ps_o[half][sl, o0:o0 + P], val[p][:, n, sl], att[n % 2][:, h, :],
                                   start=(n == 0), stop=True)
                mm.then_inc(o_done, 1)

            def turn(s, half):
                pe.wait_ge(o_copied, HALVES * s + half + 3)
                pe.wait_ge(ao_ready, HALVES * s + half + 1)
                for i in range(QT):
                    mm = pe.transpose(ps_t[:, i, :], o_sb[:, i * P:(i + 1) * P], c["ident"][:])
                mm.then_inc(t_done, 1)

            def step(s, p, use, first=False, last=False):
                pe.wait_ge(k_copied, s + 2)
                for n in range(ST):
                    if n < ST - 1:
                        add_state(s, p, n)
                        scores(s, p, n + 1)
                    elif not last:
                        scores(s + 1, (p + 1) % NBUF, 0)
                    outputs(s, p, n)
                    if n == 1 and not first:
                        turn(s - 1, 1)
                    if n == QT + 1:
                        turn(s, 0)
                    if n == QT + 2 and not last:
                        turn_keys(s + 1, (p + 1) % NBUF, use + (p + 1) // NBUF)

            turn_keys(0, 0, 0)
            scores(0, 0, 0)
            steps(pe, step)
            turn(N - 1, 1)

        @block.scalar
        def _(act):
            def copy_keys(s, p):
                act.wait_ge(k_turned, s + 1)
                act.copy(kt[p][:], ps_k[:]).then_inc(k_copied, 1)

            def copy_heads(s, half):
                act.wait_ge(o_done, ST * s + QT * (half + 1))
                act.wait_ge(ao_ready, HALVES * s + half + 1)
                act.copy(o_sb[:], ps_o[half][:]).then_inc(o_copied, 1)

            def step(s, p, use, first=False, last=False):
                copy_heads(s, 0)
                if not last:
                    copy_keys(s + 1, (p + 1) % NBUF)
                copy_heads(s, 1)

            act.sem_inc(k_copied, 1)
            act.sem_inc(o_copied, 2)
            copy_keys(0, 0)
            steps(act, step)

        @block.vector
        def _(dve):
            def mask(s, n):
                dve.wait_ge(scored, ST * s + n + 1)
                dve.tensor_tensor(att[n % 2][:], ps_a[n % 2][:],
                                  c["past"][:].unsqueeze(1).to_broadcast([P, HG, P]),
                                  ALU.mult).then_inc(att_ready, 1)

            def keep_state(s, n):
                dve.wait_ge(state_sum, (ST - 1) * s + n + 1)
                dve.tensor_tensor(state[(n + 1) % 2][:], ps_s[:], c["own"][:],
                                  ALU.mult).then_inc(state_ready, 1)

            def divide(s, half):
                dve.wait_ge(t_done, HALVES * s + half + 1)
                heads = ps_t.rearrange("p n (h e) -> p n h e", h=HG)
                dve.tensor_scalar(den[:], heads[:, :, :, DK], EPS, None, ALU.add).then_inc(den_ready, 1)
                dve.wait_ge(den_ready, 2 * (HALVES * s + half) + 1)
                dve.reciprocal(den[:], den[:]).then_inc(den_ready, 1)
                dve.wait_ge(den_ready, 2 * (HALVES * s + half) + 2)
                dve.wait_ge(ao_out[half], 16 * (s + 1))
                dve.tensor_tensor(ao[half].rearrange("p n (h e) -> p n h e", h=HG), heads[:, :, :, 0:DK],
                                  den[:].unsqueeze(3).to_broadcast([P, QT, HG, DK]),
                                  ALU.mult).then_inc(ao_ready, 1)

            def step(s, p, use, first=False, last=False):
                for n in range(ST):
                    if n < ST - 1:
                        keep_state(s, n)
                        mask(s, n + 1)
                    elif not last:
                        mask(s + 1, 0)
                    if n == 2 and not first:
                        divide(s - 1, 1)
                    if n == QT + 2:
                        divide(s, 0)

            dve.sem_inc(att_ready, 2)
            dve.sem_inc(state_ready, 1)
            dve.sem_inc(ao_ready, 1)
            mask(0, 0)
            steps(dve, step)
            divide(N - 1, 1)


NT = CH // P
UNITS = T // CH
NORM_OPS = 3 * NT + 5


class Norm:

    def __init__(self, st):
        self.stats = st.sb("stats", [P, NT, 6])
        self.mv = st.sb("mv", [P, NT, 2])
        self.ve = st.sb("ve", [P, NT])
        self.sd = st.sb("sd", [P, NT])
        self.rs = st.sb("rs", [P, NT])
        self.tmp = st.sb("ntmp", [P, NT])
        self.var_ready, self.sqrt_ready = st.sem("var_ready"), st.sem("sqrt_ready")

    def vector(self, dve, d, u, res, y):
        self.moments(dve, d, res)
        self.scale(dve, d, u, res, y)

    def moments(self, dve, d, res):
        for i in range(NT):
            d.did(dve.bn_stats(self.stats[:, i, :], res[:, i, :]))
        d.hold()
        for i in range(NT):
            d.did(dve.bn_aggr(self.mv[:, i, :], self.stats[:, i, :]))
        d.wait()
        dve.tensor_scalar(self.ve[:], self.mv[:, :, 1], EPS, None, ALU.add).then_inc(self.var_ready, 1)

    def scale(self, dve, d, u, res, y):
        dve.wait_ge(self.sqrt_ready, u + 1)
        d.did(dve.reciprocal(self.rs[:], self.sd[:]))
        d.wait()
        d.did(dve.tensor_tensor(self.tmp[:], self.rs[:], self.rs[:], ALU.mult))
        d.wait()
        d.did(dve.tensor_tensor(self.tmp[:], self.tmp[:], self.ve[:], ALU.mult))
        d.wait()
        d.did(dve.tensor_scalar(self.tmp[:], self.tmp[:], -0.5, 1.5, ALU.mult, ALU.add))
        d.wait()
        d.did(dve.tensor_tensor(self.rs[:], self.rs[:], self.tmp[:], ALU.mult))
        d.wait()
        for i in range(NT):
            d.did(dve.tensor_scalar(y[:, i, :], res[:, i, :], self.mv[:, i, 0:1], self.rs[:, i:i + 1],
                                    ALU.subtract, ALU.mult))

    def scalar(self, act, u):
        act.wait_ge(self.var_ready, u + 1)
        act.activation(self.sd[:], self.ve[:], ACT.Sqrt).then_inc(self.sqrt_ready, 1)



def choices(nc, ctx, layer):
    keep = Stage(nc, ctx, f"k{layer}")
    shape = [P, UNITS, NT, ROUTERS[layer]["K"]]
    return keep.sb("gidx", shape, I32), keep.sb("gate", shape)


def route(nc, c, w, ins, dram, x_dram, gidx, gate, layer):
    rt = ROUTERS[layer]
    E, K, C = rt["E"], rt["K"], rt["C"]
    with ExitStack() as tmp:
        st = Stage(nc, tmp, f"r{layer}")
        ao = [st.sb(f"ao{p}", [P, NT, G, FG]) for p in range(2)]
        xr = [st.sb(f"xr{p}", [P, NT, D]) for p in range(2)]
        aoT = st.sb("aoT", [P, DT, CH])
        yT = st.sb("yT", [P, DT, CH])
        res = st.sb("res", [P, NT, D])
        y = [st.sb(f"y{p}", [P, NT, D]) for p in range(2)]
        gw = st.sb("gw", [P, DT, E])
        gb = st.sb("gb", [P, E])
        bo = st.sb("bo", [P, D])
        lg = st.sb("lg", [P, NT, E])
        mx = st.sb("mx", [P, NT])
        top = st.sb("top", [P, NT, 8])
        topi = st.sb("topi", [P, NT, 8], U32)
        topf = st.sb("topf", [P, NT, 8])
        hot = [st.sb(f"hot{k}", [P, NT, E]) for k in range(K)]
        chosen = st.sb("chosen", [P, NT, E])
        chosenb = st.sb("chosenb", [P, NT, E], BF16)
        unit_sum = st.sb("unit_sum", [P, E])
        count = st.sb("count", [P, E], BF16)
        over = st.sb("over", [P, NT, E])
        slot = st.sb("slot", [P, NT, K])
        valid = st.sb("valid", [P, NT, K])
        ex = st.sb("ex", [P, NT, K if layer == 0 else E])
        sm = st.sb("sm", [P, NT])
        sidx = [st.sb(f"sidx{p}", [P, NT, K], I32) for p in range(2)]
        norm = Norm(st)
        ps_a = st.ps("ps_a", [P, DT, CH])
        ps_y = st.ps("ps_y", [P, DT, CH])
        ps_w = st.ps("ps_w", [P, 2, 2, D])
        ps_l = st.ps("ps_l", [P, NT, E])
        ps_p = st.ps("ps_p", [P, NT, E])
        setup, setup_v = st.sem("setup"), st.sem("setup_v")
        loaded = [st.sem(f"loaded{p}") for p in range(2)]
        scattered = [st.sem(f"scattered{p}") for p in range(2)]
        stored = [st.sem(f"stored{p}") for p in range(2)]
        heads_turned, heads_copied = st.sem("heads_turned"), st.sem("heads_copied")
        y_turned, y_copied = st.sem("y_turned"), st.sem("y_copied")
        out_done, res_done, biased = st.sem("out_done"), st.sem("res_done"), st.sem("biased")
        y_ready, logit_done, logit_read = st.sem("y_ready"), st.sem("logit_done"), st.sem("logit_read")
        exp_in, exp_done = st.sem("exp_in"), st.sem("exp_done")
        chosen_ready, pos_done, count_ready = st.sem("chosen_ready"), st.sem("pos_done"), st.sem("count_ready")
        sidx_ready, y_free = st.sem("sidx_ready"), st.sem("y_free")
        normed, chose = st.sem("normed"), st.sem("chose")
        block = tmp.enter_context(nc.Block())
        NLOAD = G + 1
        NSETUP = 3 if layer else 2

        @block.sync
        def _(sp):
            def load(b, p):
                src = dram[f"heads{layer}"].rearrange("b g (x n q) e -> b x g q n e", x=2, q=P)
                for g in range(G):
                    sp.dma_start(ao[p][:, :, g, :], src[b, p, g]).then_inc(loaded[p], 16)
                src = x_dram.rearrange("(b x n q) d -> b x q n d", b=B, x=2, q=P)
                sp.dma_start(xr[p][:], src[b, p]).then_inc(loaded[p], 16)

            def store(b, p):
                sp.wait_ge(y_ready, 2 * b + p + 1)
                dst = dram[f"normed{layer}"].rearrange("(b x n q) d -> b x q n d", b=B, x=2, q=P)
                sp.dma_start(dst[b, p], y[p][:]).then_inc(stored[p], 16)

            for p in range(2):
                sp.sem_inc(stored[p], 16)
            load(0, 0)
            sp.dma_start(gw[:], ins[f"gate{layer}"].rearrange("(j q) e -> q j e", q=P)).then_inc(setup, 16)
            sp.dma_start(gb[:], ins[f"gbias{layer}"].rearrange("(o e) -> o e", o=1).to_broadcast([P, E]))\
              .then_inc(setup, 16)
            if layer:
                sp.dma_start(bo[:], ins["bo1"].rearrange("(o d) -> o d", o=1).to_broadcast([P, D]))\
                  .then_inc(setup, 16)
            load(0, 1)
            with sp.Fori(0, B - 1) as b:
                for p in range(2):
                    sp.wait_ge(res_done, 2 * b + p + 1)
                    load(b + 1, p)
                    store(b, p)
            for p in range(2):
                store(B - 1, p)
            for p in range(2):
                sp.wait_ge(stored[p], 16 * (B + 1))

        def steps(eng, first, step):
            first()
            with eng.Fori(0, B - 1) as b:
                for p in range(2):
                    step(2 * b + p, p, b, (1 - p, b + p), (p, b + 1))
            step(UNITS - 2, 0, B - 1, (1, B - 1), None)
            step(UNITS - 1, 1, B - 1, None, None)

        @block.tensor
        def _(pe):
            def turn(ps, src):
                for j in range(DT):
                    for i in range(NT):
                        mm = pe.transpose(ps[:, j, i * P:(i + 1) * P], src[:, i, j * P:(j + 1) * P], c["ident"][:])
                    mm.then_inc(heads_turned if ps is ps_a else y_turned, 1)

            def turn_heads(p, b):
                pe.wait_ge(loaded[p], 16 * NLOAD * (b + 1))
                turn(ps_a, ao[p].rearrange("q n g e -> q n (g e)"))

            def project_heads(u):
                pe.wait_ge(heads_copied, DT * (u + 1))
                for i in range(NT):
                    for j in range(DT):
                        mm = pe.matmul(ps_w[:, i // 2, i % 2, :], aoT[:, j, i * P:(i + 1) * P],
                                       w["wo"][:, j, :], start=(j == 0), stop=(j == DT - 1))
                mm.then_inc(out_done, 1)

            def logits(u, p):
                pe.wait_ge(y_ready, u + 1)
                turn(ps_y, y[p])
                pe.wait_ge(y_copied, DT * (u + 1))
                for i in range(NT):
                    for j in range(DT):
                        mm = pe.matmul(ps_l[:, i, :], yT[:, j, i * P:(i + 1) * P], gw[:, j, :],
                                       start=(j == 0), stop=(j == DT - 1))
                mm.then_inc(logit_done, 1)

            def positions(u):
                pe.wait_ge(chosen_ready, u + 1)
                pe.wait_ge(count_ready, u + 1)
                for i in range(NT):
                    pe.matmul(ps_p[:, i, :], c["before"][:], chosenb[:, i, :], start=True, stop=False)
                    for o in range(i):
                        pe.matmul(ps_p[:, i, :], c["ones"][:], chosenb[:, o, :], start=False, stop=False)
                    mm = pe.matmul(ps_p[:, i, :], c["ones"][:], count[:], start=False, stop=True)
                mm.then_inc(pos_done, 1)

            def first():
                turn_heads(0, 0)
                project_heads(0)
                pe.wait_ge(setup, 16 * NSETUP)
                logits(0, 0)
                pe.wait_ge(res_done, 1)
                turn_heads(1, 0)
                project_heads(1)

            def step(u, p, b, one, two):
                if two:
                    turn_heads(*two)
                positions(u)
                if two:
                    project_heads(u + 2)
                if one:
                    logits(u + 1, one[0])

            steps(pe, first, step)

        @block.scalar
        def _(act):
            def copy_heads(u):
                for j in range(DT):
                    act.wait_ge(heads_turned, DT * u + j + 1)
                    act.copy(aoT[:, j, :], ps_a[:, j, :]).then_inc(heads_copied, 1)

            def copy_y(u):
                for j in range(DT):
                    act.wait_ge(y_turned, DT * u + j + 1)
                    act.copy(yT[:, j, :], ps_y[:, j, :]).then_inc(y_copied, 1)

            def first():
                copy_heads(0)
                norm.scalar(act, 0)
                copy_y(0)
                copy_heads(1)
                norm.scalar(act, 1)

            def exponentials(u):
                act.wait_ge(exp_in, u + 1)
                act.activation(ex[:], ex[:], ACT.Exp).then_inc(exp_done, 1)

            def step(u, p, b, one, two):
                if layer:
                    exponentials(u)
                if two:
                    copy_heads(u + 2)
                if not layer:
                    exponentials(u)
                if one:
                    copy_y(u + 1)
                if two:
                    norm.scalar(act, u + 2)

            steps(act, first, step)

        @block.gpsimd
        def _(pool):
            def bias(u, p, b):
                if layer:
                    pool.wait_ge(loaded[p], 16 * NLOAD * (b + 1))
                    for i in range(NT):
                        add = pool.tensor_tensor(xr[p][:, i, :], xr[p][:, i, :], bo[:], ALU.add)
                    add.then_inc(biased, 1)

            def first():
                bias(0, 0, 0)
                bias(1, 1, 0)

            def step(u, p, b, one, two):
                if two:
                    bias(u + 2, *two)
                hold(pool, sidx_ready, u + 1)
                for i in range(NT):
                    for k in range(K):
                        pool.indirect_dma_start(
                            dram[f"slots{layer}"], bass.IndirectOffsetOnAxis(ap=sidx[p][:, i, k:k + 1], axis=0),
                            y[p][:, i, :], None, bounds_check=E * C - 1, oob_is_err=False)\
                            .then_inc(scattered[p], 16)
                pool.wait_ge(scattered[p], 16 * NT * K * (b + 1))
                pool.sem_inc(y_free, 1)

            if layer:
                pool.wait_ge(setup, 16 * NSETUP)
            steps(pool, first, step)

        @block.vector
        def _(dve):
            NY = 32 if layer == 0 else 29

            def moments(u, p, b):
                dve.wait_ge(out_done, u + 1)
                dve.wait_ge(loaded[p], 16 * NLOAD * (b + 1))
                if layer:
                    dve.wait_ge(biased, u + 1)
                dve.tensor_tensor(res.rearrange("q n d -> q (n d)"), ps_w.rearrange("q a i d -> q (a i d)"),
                                  xr[p].rearrange("q n d -> q (n d)"), ALU.add).then_inc(res_done, 1)
                hold(dve, res_done, u + 1)
                norm.moments(dve, Done(dve, normed, u * NORM_OPS), res)

            def scale(u, p, b):
                d = Done(dve, normed, u * NORM_OPS + 2 * NT)
                dve.wait_ge(stored[p], 16 * (b + 1))
                hold(dve, y_free, u + 1)
                norm.scale(dve, d, u, res, y[p])
                d.wait()
                dve.sem_inc(y_ready, 1)
                assert d.n + 2 * NT == NORM_OPS

            def choose(u):
                d = Done(dve, chose, u * NY)

                def then(ins):
                    d.did(ins)
                    d.wait()

                dve.wait_ge(logit_done, u + 1)
                then(dve.tensor_tensor(lg[:], ps_l[:], gb[:].unsqueeze(1).to_broadcast([P, NT, E]), ALU.add))
                if layer:
                    then(dve.tensor_reduce(mx[:], lg[:], AX.X, ALU.max))
                    dve.tensor_tensor(ex[:], lg[:], mx[:].unsqueeze(2).to_broadcast([P, NT, E]),
                                      ALU.subtract).then_inc(exp_in, 1)
                    dve.wait_ge(exp_done, u + 1)
                    then(dve.tensor_reduce(sm[:], ex[:], AX.X, ALU.add))
                    then(dve.reciprocal(sm[:], sm[:]))
                    then(dve.tensor_tensor(lg[:], ex[:], sm[:].unsqueeze(2).to_broadcast([P, NT, E]), ALU.mult))
                d.hold()
                for i in range(NT):
                    d.did(dve.max(top[:, i, :], lg[:, i, :]))
                d.hold()
                for i in range(NT):
                    d.did(dve.max_index(topi[:, i, :], top[:, i, :], lg[:, i, :]))
                d.wait()
                if not layer:
                    dve.tensor_tensor(ex[:], top[:, :, 0:K], top[:, :, 0:1].to_broadcast([P, NT, K]),
                                      ALU.subtract).then_inc(exp_in, 1)
                then(dve.tensor_copy(topf[:], topi[:]))
                for k in range(K):
                    d.did(dve.tensor_tensor(hot[k][:], c[f"expert{layer}"][:].unsqueeze(1).to_broadcast([P, NT, E]),
                                            topf[:, :, k:k + 1].to_broadcast([P, NT, E]), ALU.is_equal))
                d.wait()
                then(dve.tensor_tensor(chosen[:], hot[0][:], hot[1][:], ALU.add))
                for k in range(2, K):
                    then(dve.tensor_tensor(chosen[:], chosen[:], hot[k][:], ALU.add))
                dve.tensor_copy(chosenb[:], chosen[:]).then_inc(chosen_ready, 1)
                d.did(dve.tensor_reduce(unit_sum[:], chosen.rearrange("q n e -> q e n"), AX.X, ALU.add))
                return d

            def slots(d, u, p):

                def then(ins):
                    d.did(ins)
                    d.wait()

                dve.wait_ge(pos_done, u + 1)
                d.wait()
                dve.tensor_tensor(count[:], count[:], unit_sum[:], ALU.add).then_inc(count_ready, 1)
                then(dve.tensor_scalar(over[:], ps_p[:], float(C), BIG, ALU.is_ge, ALU.mult))
                then(dve.tensor_tensor(over[:], over[:], ps_p[:], ALU.add))
                then(dve.tensor_tensor(over[:], over[:], c[f"first{layer}"][:].unsqueeze(1).to_broadcast([P, NT, E]),
                                       ALU.add))
                for k in range(K):
                    d.did(dve.tensor_tensor(hot[k][:], hot[k][:], over[:], ALU.mult))
                d.wait()
                for k in range(K):
                    d.did(dve.tensor_reduce(slot[:, :, k], hot[k][:], AX.X, ALU.add))
                d.wait()
                dve.tensor_copy(sidx[p][:], slot[:]).then_inc(sidx_ready, 1)

            def gates(d, u):

                def then(ins):
                    d.did(ins)
                    d.wait()

                then(dve.tensor_scalar(valid[:], slot[:], BIG, None, ALU.is_lt))
                then(dve.tensor_tensor(slot[:], slot[:], valid[:], ALU.mult))
                d.did(dve.tensor_copy(gidx[:, u], slot[:]))
                if layer:
                    then(dve.tensor_tensor(gate[:, u], top[:, :, 0:K], valid[:], ALU.mult))
                else:
                    dve.wait_ge(exp_done, u + 1)
                    then(dve.tensor_reduce(sm[:], ex[:], AX.X, ALU.add))
                    then(dve.reciprocal(sm[:], sm[:]))
                    then(dve.tensor_tensor(valid[:], valid[:], sm[:].unsqueeze(2).to_broadcast([P, NT, K]), ALU.mult))
                    then(dve.tensor_tensor(gate[:, u], ex[:], valid[:], ALU.mult))
                assert d.n == NY, (d.n, NY)

            def first():
                moments(0, 0, 0)
                scale(0, 0, 0)
                moments(1, 1, 0)

            def step(u, p, b, one, two):
                y = choose(u)
                slots(y, u, p)
                if one:
                    scale(u + 1, *one)
                gates(y, u)
                if two:
                    moments(u + 2, *two)

            dve.sem_inc(y_free, 2)
            dve.memset(count[:], 0.0).then_inc(count_ready, 1)
            dve.wait_ge(setup, 16 * NSETUP)
            steps(dve, first, step)


def experts(nc, c, ins, dram, layer):
    rt = ROUTERS[layer]
    E, C = rt["E"], rt["C"]
    TL = C // P
    NBUF = 4
    with ExitStack() as ctx:
        st = Stage(nc, ctx, f"e{layer}")
        w1 = [st.sb(f"w1_{p}", [P, DT, F]) for p in range(NBUF)]
        w2 = [st.sb(f"w2_{p}", [P, FT, D]) for p in range(NBUF)]
        b2 = [st.sb(f"b2_{p}", [P, D]) for p in range(NBUF)]
        b1 = st.sb("b1", [P, E, FT])
        xs = [st.sb(f"xs{p}", [P, TL, D]) for p in range(NBUF)]
        xT = [st.sb(f"xT{t}", [P, DT, P]) for t in range(2)]
        hT = [st.sb(f"hT{t}", [P, FT, P]) for t in range(2)]
        ys = [st.sb(f"ys{p}", [P, TL, D]) for p in range(2)]
        ps_x = st.ps("ps_x", [P, DT, P])
        ps_h = [[st.ps(f"ps_h{t}{i}", [P, FT // 2, P]) for i in range(2)] for t in range(2)]
        ps_y = [st.ps(f"ps_y{t}", [P, D]) for t in range(2)]
        b1_in = st.sem("b1_in")
        x_in = [st.sem(f"x_in{p}") for p in range(NBUF)]
        w1_in = [st.sem(f"w1_in{p}") for p in range(NBUF)]
        w2_in = [st.sem(f"w2_in{p}") for p in range(NBUF)]
        stored = [st.sem(f"stored{p}") for p in range(2)]
        x_turned, x_copied = st.sem("x_turned"), st.sem("x_copied")
        hid_done, gelu_done = st.sem("hid_done"), st.sem("gelu_done")
        y_done, y_ready = st.sem("y_done"), st.sem("y_ready")
        block = ctx.enter_context(nc.Block())

        def steps(eng, step):
            step(0, 0, 0, True)
            with eng.Fori(0, E // NBUF - 1) as j:
                for p in range(1, NBUF):
                    step(NBUF * j + p, p, j, False)
                step(NBUF * j + NBUF, 0, j + 1, False)
            for p in range(1, NBUF):
                step(E - NBUF + p, p, E // NBUF - 1, False, last=p == NBUF - 1)

        def before(p, j):
            return (p - 1, j) if p else (NBUF - 1, j - 1)

        def after(p, j):
            return (p + 1, j) if p < NBUF - 1 else (0, j + 1)


        @block.sync
        def _(sp):
            def load(e, p):
                sp.dma_start(w1[p][:], ins[f"w1_{layer}"][e].rearrange("(j q) h -> q j h", q=P)).then_inc(w1_in[p], 16)
                sp.dma_start(xs[p][:], dram[f"slots{layer}"].rearrange("(e n q) d -> e q n d", e=E, q=P)[e])\
                  .then_inc(x_in[p], 16)

            def load2(e, p):
                sp.dma_start(w2[p][:], ins[f"w2_{layer}"][e].rearrange("(j q) d -> q j d", q=P)).then_inc(w2_in[p], 16)
                sp.dma_start(b2[p][:], ins[f"b2_{layer}"].rearrange("(o e) d -> e o d", o=1)[e]
                             .to_broadcast([P, D])).then_inc(w2_in[p], 16)

            def step(e, p, more=True):
                if more:
                    sp.wait_ge(hid_done, 2 * TL * (e + 1))
                    load(e + NBUF, p)
                sp.wait_ge(y_ready, 2 + TL * (e + 1))
                if more:
                    load2(e + NBUF, p)
                dst = dram[f"answers{layer}"].rearrange("(e n q) d -> e q n d", e=E, q=P)[e]
                sp.dma_start(dst, ys[p % 2][:]).then_inc(stored[p % 2], 16)

            sp.dma_start(b1[:], ins[f"b1_{layer}"]).then_inc(b1_in, 16)
            for p in range(NBUF):
                load(p, p)
                load2(p, p)
            for p in range(2):
                sp.sem_inc(stored[p], 16)
            with sp.Fori(0, E // NBUF - 1) as j:
                for p in range(NBUF):
                    step(NBUF * j + p, p)
            for p in range(NBUF):
                step(E - NBUF + p, p, more=False)
            for p in range(2):
                sp.wait_ge(stored[p], 16 * (E // 2 + 1))

        @block.tensor
        def _(pe):
            def second(n, t, p, j):
                pe.wait_ge(w2_in[p], 32 * (j + 1))
                pe.wait_ge(y_ready, n + 1)
                pe.wait_ge(gelu_done, FT * (n + 1))
                for f in range(FT):
                    mm = pe.matmul(ps_y[t][:], hT[t][:, f, :], w2[p][:, f, :], start=(f == 0), stop=(f == FT - 1))
                mm.then_inc(y_done, 1)

            def turn(p, j, i):
                if i == 0:
                    pe.wait_ge(x_in[p], 16 * (j + 1))
                for k in range(DT):
                    mm = pe.transpose(ps_x[:, k, :], xs[p][:, i, k * P:(k + 1) * P], c["ident"][:])
                mm.then_inc(x_turned, 1)

            def step(e, p, j, first, last=False):
                for i in range(TL):
                    n = e * TL + i
                    t = (p + i) % 2
                    pe.wait_ge(x_copied, n + 1)
                    if i + 1 < TL:
                        turn(p, j, i + 1)
                    elif not last:
                        turn(*after(p, j), 0)
                    if i == 0:
                        pe.wait_ge(w1_in[p], 16 * (j + 1))
                    for f in range(FT):
                        for k in range(DT):
                            mm = pe.matmul(ps_h[t][f // 4][:, f % 4, :], w1[p][:, k, f * P:(f + 1) * P],
                                           xT[t][:, k, :], start=(k == 0), stop=(k == DT - 1))
                        if f % 4 == 3:
                            mm.then_inc(hid_done, 1)
                    if i:
                        second(n - 1, 1 - t, p, j)
                    elif not first:
                        second(n - 1, 1 - t, *before(p, j))

            turn(0, 0, 0)
            steps(pe, step)
            second(E * TL - 1, 1, NBUF - 1, E // NBUF - 1)

        @block.scalar
        def _(act):
            def step(e, p, j, first, last=False):
                for i in range(TL):
                    n = e * TL + i
                    t = (p + i) % 2
                    if not (first and i < 2):
                        act.wait_ge(y_done, n - 1)
                    for f in range(FT):
                        if f % 4 == 0:
                            hold(act, hid_done, 2 * n + f // 4 + 1)
                        act.activation(hT[t][:, f, :], ps_h[t][f // 4][:, f % 4, :], ACT.Gelu,
                                       bias=b1[:, e, f:f + 1]).then_inc(gelu_done, 1)

            act.wait_ge(b1_in, 16)
            steps(act, step)

        @block.vector
        def _(dve):
            def copy_x(n, t):
                dve.wait_ge(x_turned, n + 1)
                dve.tensor_copy(xT[t][:], ps_x[:]).then_inc(x_copied, 1)

            def answer(n, t, p, j, i):
                dve.wait_ge(y_done, n + 1)
                dve.wait_ge(w2_in[p], 32 * (j + 1))
                if i == 0:
                    dve.wait_ge(stored[p % 2], 16 * (NBUF // 2 * j + p // 2 + 1))
                dve.tensor_tensor(ys[p % 2][:, i, :], ps_y[t][:], b2[p][:], ALU.add).then_inc(y_ready, 1)

            def step(e, p, j, first, last=False):
                for i in range(TL):
                    n = e * TL + i
                    t = (p + i) % 2
                    if not (last and i == TL - 1):
                        copy_x(n + 1, 1 - t)
                    if i:
                        answer(n - 1, 1 - t, p, j, i - 1)
                    elif not first:
                        answer(n - 1, 1 - t, *before(p, j), TL - 1)

            dve.sem_inc(y_ready, 2)
            copy_x(0, 0)
            steps(dve, step)
            answer(E * TL - 1, 1, NBUF - 1, E // NBUF - 1, TL - 1)


def combine(nc, dram, gidx, gate, out_dram):
    K = ROUTERS[1]["K"]
    with ExitStack() as ctx:
        st = Stage(nc, ctx, "g")
        ans = [st.sb(f"ans{p}", [P, NT, K, D]) for p in range(2)]
        gi = [st.sb(f"gi{p}", [P, NT, K], I32) for p in range(2)]
        xr = [st.sb(f"xr{p}", [P, NT, D]) for p in range(2)]
        y = [st.sb(f"y{p}", [P, NT, D]) for p in range(2)]
        norm = Norm(st)
        x_in = [st.sem(f"x_in{p}") for p in range(2)]
        gathered = [st.sem(f"gathered{p}") for p in range(2)]
        stored = [st.sem(f"stored{p}") for p in range(2)]
        summed, own, y_ready, gi_ready = st.sem("summed"), st.sem("own"), st.sem("y_ready"), st.sem("gi_ready")
        block = ctx.enter_context(nc.Block())

        @block.sync
        def _(sp):
            def load(b, p):
                src = dram["normed1"].rearrange("(b x n q) d -> b x q n d", b=B, x=2, q=P)
                sp.dma_start(xr[p][:], src[b, p]).then_inc(x_in[p], 16)

            def store(b, p):
                sp.wait_ge(y_ready, 2 * b + p + 1)
                dst = out_dram.rearrange("(b x n q) d -> b x q n d", b=B, x=2, q=P)
                sp.dma_start(dst[b, p], y[p][:]).then_inc(stored[p], 16)

            for p in range(2):
                sp.sem_inc(stored[p], 16)
                load(0, p)
            with sp.Fori(0, B - 1) as b:
                for p in range(2):
                    store(b, p)
                    load(b + 1, p)
            for p in range(2):
                store(B - 1, p)
            for p in range(2):
                sp.wait_ge(stored[p], 16 * (B + 1))

        @block.gpsimd
        def _(pool):
            with pool.Fori(0, B) as b:
                for p in range(2):
                    u = 2 * b + p
                    hold(pool, summed, u + 1)
                    pool.tensor_copy(gi[p][:], gidx[:, u]).then_inc(gi_ready, 1)
                    hold(pool, gi_ready, u + 1)
                    for i in range(NT):
                        for k in range(K):
                            pool.indirect_dma_start(
                                ans[p][:, i, k, :], None, dram["answers1"],
                                bass.IndirectOffsetOnAxis(ap=gi[p][:, i, k:k + 1], axis=0))\
                                .then_inc(gathered[p], 16)

        @block.scalar
        def _(act):
            with act.Fori(0, UNITS) as u:
                norm.scalar(act, u)

        @block.vector
        def _(dve):
            dve.sem_inc(summed, 2)
            NOWN = NORM_OPS + NT * (K - 1)
            with dve.Fori(0, B) as b:
                for p in range(2):
                    u = 2 * b + p
                    d = Done(dve, own, u * NOWN)
                    dve.wait_ge(x_in[p], 16 * (b + 1))
                    dve.wait_ge(gathered[p], 16 * NT * K * (b + 1))
                    for k in range(K):
                        for i in range(NT):
                            ins = dve.scalar_tensor_tensor(out=xr[p][:, i, :], in0=ans[p][:, i, k, :],
                                                           scalar=gate[:, u, i, k:k + 1], in1=xr[p][:, i, :],
                                                           op0=ALU.mult, op1=ALU.add)
                            if k < K - 1:
                                d.did(ins)
                        if k < K - 1:
                            d.wait()
                    ins.then_inc(summed, 1)
                    dve.wait_ge(summed, u + 3)
                    hold(dve, stored[p], 16 * (b + 1))
                    norm.vector(dve, d, u, xr[p], y[p])
                    d.wait()
                    dve.sem_inc(y_ready, 1)
                    assert d.n == NOWN, (d.n, NOWN)


def combine_and_project(nc, c, w, ins, dram, gidx, gate):
    K = ROUTERS[0]["K"]
    NSTORE = 6 + 2 + G
    with ExitStack() as ctx:
        st = Stage(nc, ctx, "m")
        ans = [st.sb(f"ans{p}", [P, NT, K, D]) for p in range(2)]
        gi = [st.sb(f"gi{p}", [P, NT, K], I32) for p in range(2)]
        xr = [st.sb(f"xr{p}", [P, NT, D]) for p in range(2)]
        y = [st.sb(f"y{p}", [P, NT, D]) for p in range(2)]
        yT = st.sb("yT", [P, DT, CH])
        neg = [st.sb(f"neg{r}", [P, CH]) for r in range(4)]
        rest = [st.sb(f"rest{r}", [P, CH]) for r in range(4)]
        phi = [st.sb(f"phi{p}", [P, 4, CH]) for p in range(2)]
        parts = [[st.sb(f"part{p}_{k}", [P, 4, CH], BF16) for k in range(3)] for p in range(2)]
        vpad = [st.sb(f"vpad{p}", [P, NT, G, P]) for p in range(2)]
        norm = Norm(st)
        ps_y = st.ps("ps_y", [P, DT, CH])
        ps_qk = st.ps("ps_qk", [P, 4, CH])
        ps_v = st.ps("ps_v", [P, 2, 2, D])
        w_in = [st.sem(f"{k}_in") for k in w]
        x_in = [st.sem(f"x_in{p}") for p in range(2)]
        gathered = [st.sem(f"gathered{p}") for p in range(2)]
        y_stored = [st.sem(f"y_stored{p}") for p in range(2)]
        stored = [st.sem(f"stored{p}") for p in range(2)]
        summed, own, gi_ready, y_ready = st.sem("summed"), st.sem("own"), st.sem("gi_ready"), st.sem("y_ready")
        y_turned, yT_ready = st.sem("y_turned"), st.sem("yT_ready")
        qk_psum, v_psum, v_ready = st.sem("qk_psum"), st.sem("v_psum"), st.sem("v_ready")
        neg_ready, exp_ready, phi_ready = st.sem("neg_ready"), st.sem("exp_ready"), st.sem("phi_ready")
        hi_ready, rest_ready = st.sem("hi_ready"), st.sem("rest_ready")
        mid_ready, low_ready, pads = st.sem("mid_ready"), st.sem("low_ready"), st.sem("pads")
        block = ctx.enter_context(nc.Block())

        def steps(eng, step):
            with eng.Fori(0, B - 1) as b:
                for p in range(2):
                    step(2 * b + p, p, b, (1 - p, b + p))
            step(UNITS - 2, 0, B - 1, (1, B - 1))
            step(UNITS - 1, 1, B - 1, None)

        @block.sync
        def _(sp):
            def load(b, p):
                src = dram["normed0"].rearrange("(b x n q) d -> b x q n d", b=B, x=2, q=P)
                sp.dma_start(xr[p][:], src[b, p]).then_inc(x_in[p], 16)

            def store_y(u, p, b):
                hold(sp, y_ready, u + 1)
                dst = dram["mid"].rearrange("(b x n q) d -> b x q n d", b=B, x=2, q=P)
                sp.dma_start(dst[b, p], y[p][:]).then_inc(y_stored[p], 16)

            def store(u, p, b):
                hold(sp, low_ready, 4 * u + 8)
                for o, name in enumerate(("q", "k")):
                    for k in range(3):
                        dst = dram[f"{name}parts1"][k, b, :, p * CH:(p + 1) * CH]
                        sp.dma_start(dst.rearrange("(j q) t -> q j t", q=P),
                                     parts[p][k][:, 2 * o:2 * o + 2, :]).then_inc(stored[p], 16)
                    dst = dram[f"{name}full"][b, :, p * CH:(p + 1) * CH]
                    sp.dma_start(dst.rearrange("(j q) t -> q j t", q=P),
                                 phi[p][:, 2 * o:2 * o + 2, :]).then_inc(stored[p], 16)
                hold(sp, v_ready, 2 * u + 4)
                for g in range(G):
                    dst = dram["values1"][b, g, p * CH:(p + 1) * CH, :]
                    sp.dma_start(dst.rearrange("(n q) e -> q n e", q=P),
                                 vpad[p][:, :, g, :]).then_inc(stored[p], 16)

            def step(b, p):
                u = 2 * b + p
                store_y(u + 1, 1 - p, b + p if p else b)
                load(b + (p + 1), 1 - p)
                store(u, p, b)

            for p in range(2):
                sp.sem_inc(stored[p], 16)
                sp.sem_inc(y_stored[p], 16)
                load(0, p)
            for k, sem in zip(w, w_in):
                sp.dma_start(w[k][:], ins[f"{k}1"].rearrange("(j p) f -> p j f", p=P)).then_inc(sem, 16)
            store_y(0, 0, 0)
            load(1, 0)
            with sp.Fori(0, B - 2) as b:
                for p in range(2):
                    step(b, p)
            u = UNITS - 4
            store_y(u + 1, 1, B - 2)
            load(B - 1, 1)
            store(u, 0, B - 2)
            for u in range(UNITS - 3, UNITS):
                if u + 1 < UNITS:
                    store_y(u + 1, (u + 1) % 2, (u + 1) // 2)
                store(u, u % 2, u // 2)
            for p in range(2):
                sp.wait_ge(stored[p], 16 * (B * NSTORE + 1))
                sp.wait_ge(y_stored[p], 16 * (B + 1))
            sp.wait_ge(w_in[3], 16)

        @block.gpsimd
        def _(pool):
            def gather(u, p, b):
                hold(pool, summed, u + 1)
                pool.tensor_copy(gi[p][:], gidx[:, u]).then_inc(gi_ready, 1)
                hold(pool, gi_ready, u + 1)
                for i in range(NT):
                    for k in range(K):
                        pool.indirect_dma_start(
                            ans[p][:, i, k, :], None, dram["answers0"],
                            bass.IndirectOffsetOnAxis(ap=gi[p][:, i, k:k + 1], axis=0))\
                            .then_inc(gathered[p], 16)

            def step(u, p, b, more=True):
                if more:
                    gather(u + 2, p, b + 1)
                pool.wait_ge(stored[p], 16 * (NSTORE * b + 1))
                for r in range(4):
                    pool.wait_ge(mid_ready, 4 * u + r + 1)
                    pool.tensor_tensor(parts[p][2][:, r, :], rest[r][:], parts[p][1][:, r, :],
                                       ALU.subtract).then_inc(low_ready, 1)

            pool.sem_inc(low_ready, 4)
            gather(0, 0, 0)
            gather(1, 1, 0)
            with pool.Fori(0, B - 1) as b:
                for p in range(2):
                    step(2 * b + p, p, b)
            for p in range(2):
                step(UNITS - 2 + p, p, B - 1, more=False)

        @block.tensor
        def _(pe):
            def turn(u, p):
                pe.wait_ge(y_ready, u + 1)
                for j in range(DT):
                    for i in range(NT):
                        mm = pe.transpose(ps_y[:, j, i * P:(i + 1) * P], y[p][:, i, j * P:(j + 1) * P],
                                          c["ident"][:])
                    mm.then_inc(y_turned, 1)

            def step(u, p, b, nxt):
                pe.wait_ge(yT_ready, DT * (u + 1))
                for r in range(4):
                    wt = w[("wq", "wk")[r // 2]]
                    pe.wait_ge(phi_ready, 4 * u + r + 1)
                    for j in range(DT):
                        mm = pe.matmul(ps_qk[:, r, :], wt[:, j, (r % 2) * P:(r % 2 + 1) * P], yT[:, j, :],
                                       start=(j == 0), stop=(j == DT - 1))
                    mm.then_inc(qk_psum, 1)
                for v in range(2):
                    pe.wait_ge(v_ready, 2 * u + v + 1)
                    for i in range(2):
                        for j in range(DT):
                            mm = pe.matmul(ps_v[:, v, i, :], yT[:, j, (2 * v + i) * P:(2 * v + i + 1) * P],
                                           w["wv"][:, j, :], start=(j == 0), stop=(j == DT - 1))
                    mm.then_inc(v_psum, 1)
                if nxt:
                    turn(u + 1, nxt[0])

            for sem in w_in[:3]:
                pe.wait_ge(sem, 16)
            turn(0, 0)
            steps(pe, step)

        @block.scalar
        def _(act):
            def copy_y(u):
                for j in range(DT):
                    act.wait_ge(y_turned, DT * u + j + 1)
                    act.copy(yT[:, j, :], ps_y[:, j, :]).then_inc(yT_ready, 1)

            def step(u, p, b, nxt):
                def high(r):
                    act.wait_ge(phi_ready, 4 * u + r + 5)
                    act.copy(parts[p][0][:, r, :], phi[p][:, r, :]).then_inc(hi_ready, 1)

                def middle(r):
                    act.wait_ge(rest_ready, 4 * u + r + 1)
                    act.copy(parts[p][1][:, r, :], rest[r][:]).then_inc(mid_ready, 1)

                for r in range(4):
                    act.wait_ge(neg_ready, 4 * u + r + 1)
                    act.activation(neg[r][:], neg[r][:], ACT.Exp).then_inc(exp_ready, 1)
                if nxt:
                    norm.scalar(act, u + 1)
                act.wait_ge(stored[p], 16 * (NSTORE * b + 1))
                high(0)
                if nxt:
                    copy_y(u + 1)
                high(1)
                high(2)
                middle(0)
                high(3)
                for r in range(1, 4):
                    middle(r)

            norm.scalar(act, 0)
            copy_y(0)
            steps(act, step)

        @block.vector
        def _(dve):
            NOWN = NORM_OPS + NT * (K - 1)

            def add_answers(u, p, b):
                d = Done(dve, own, u * NOWN)
                dve.wait_ge(x_in[p], 16 * (b + 1))
                dve.wait_ge(gathered[p], 16 * NT * K * (b + 1))
                for k in range(K):
                    for i in range(NT):
                        add = dve.scalar_tensor_tensor(out=xr[p][:, i, :], in0=ans[p][:, i, k, :],
                                                       scalar=gate[:, u, i, k:k + 1], in1=xr[p][:, i, :],
                                                       op0=ALU.mult, op1=ALU.add)
                        if k < K - 1:
                            d.did(add)
                    if k < K - 1:
                        d.wait()
                add.then_inc(summed, 1)

            def normalise(u, p, b):
                d = Done(dve, own, u * NOWN + NT * (K - 1))
                dve.wait_ge(summed, u + 3)
                hold(dve, y_stored[p], 16 * (b + 1))
                norm.vector(dve, d, u, xr[p], y[p])
                d.wait()
                dve.sem_inc(y_ready, 1)
                assert d.n == NORM_OPS, (d.n, NORM_OPS)

            def step(u, p, b, nxt):
                if nxt:
                    add_answers(u + 1, *nxt)
                for r in range(4):
                    dve.wait_ge(qk_psum, 4 * u + r + 1)
                    dve.wait_ge(phi_ready, 4 * u + r + 1)
                    dve.tensor_scalar(neg[r][:], ps_qk[:, r, :], 0.0, None, ALU.min).then_inc(neg_ready, 1)
                if nxt:
                    normalise(u + 1, *nxt)
                dve.wait_ge(stored[p], 16 * (NSTORE * b + 1))
                for r in range(4):
                    dve.wait_ge(exp_ready, 4 * u + r + 1)
                    dve.scalar_tensor_tensor(out=phi[p][:, r, :], in0=ps_qk[:, r, :], scalar=0.0,
                                             in1=neg[r][:], op0=ALU.max, op1=ALU.add).then_inc(phi_ready, 1)
                for r in range(4):
                    dve.wait_ge(hi_ready, 4 * u + r + 1)
                    dve.wait_ge(low_ready, 4 * u + r + 1)
                    dve.tensor_tensor(rest[r][:], phi[p][:, r, :], parts[p][0][:, r, :],
                                      ALU.subtract).then_inc(rest_ready, 1)
                if p == 0:
                    dve.wait_ge(pads, 4)
                for v in range(2):
                    dve.wait_ge(v_psum, 2 * u + v + 1)
                    for i in range(2):
                        cp = dve.tensor_copy(
                            vpad[p][:, 2 * v + i].rearrange("q g (h e) -> q (g h) e", h=HG)[:, :, 0:DK],
                            ps_v[:, v, i, :].rearrange("q (h e) -> q h e", e=DK))
                    cp.then_inc(v_ready, 1)

            dve.sem_inc(summed, 2)
            dve.sem_inc(v_ready, 2)
            dve.sem_inc(phi_ready, 4)
            for p in range(2):
                strips = vpad[p].rearrange("q n g (h e) -> q (n g h) e", h=HG)
                dve.memset(strips[:, :, DK:DK + 1], 1.0).then_inc(pads, 1)
                dve.memset(strips[:, :, DK + 1:STRIP], 0.0).then_inc(pads, 1)
            add_answers(0, 0, 0)
            normalise(0, 0, 0)
            steps(dve, step)


def build(nc, ins, out):
    dram = {}
    LAYER_SEMS.clear()

    def scratch(name, shape, dt=F32):
        dram[name] = nc.dram_tensor(f"s_{name}", shape, dt, kind="Internal").ap()

    for layer, rt in enumerate(ROUTERS):
        for n in ("q", "k"):
            halves = layer == 0 and n == "q"
            scratch(f"{n}parts{layer}", (3, S // CH, B, D, CH) if halves else (3, B, D, S), BF16)
        scratch(f"values{layer}", (B, G, S, P))
        scratch(f"heads{layer}", (B, G, S, FG))
        scratch(f"slots{layer}", (rt["E"] * rt["C"], D))
        scratch(f"answers{layer}", (rt["E"] * rt["C"], D))
        scratch(f"normed{layer}", (T, D))
    scratch("mid", (T, D))
    for n in ("q", "k"):
        scratch(f"{n}full", (B, D, S))
    tokens = ins["x"].rearrange("b s d -> (b s) d")
    with ExitStack() as ctx:
        c = constants(nc, ctx)
        gidx, gate = choices(nc, ctx, 0)
        with ExitStack() as lctx:
            w = weights(nc, lctx, 0)
            project(nc, c, w, ins, tokens, dram)
            attend(nc, c, dram)
            route(nc, c, w, ins, dram, tokens, gidx, gate, 0)
        experts(nc, c, ins, dram, 0)
        nc.clear_and_free_semaphores(list(LAYER_SEMS))
        LAYER_SEMS.clear()
        nc.all_engine_barrier()
        with ExitStack() as lctx:
            w = weights(nc, lctx, 1)
            combine_and_project(nc, c, w, ins, dram, gidx, gate)
            attend_linear(nc, c, dram)
            gidx, gate = choices(nc, lctx, 1)
            route(nc, c, w, ins, dram, dram["mid"], gidx, gate, 1)
            experts(nc, c, ins, dram, 1)
            combine(nc, dram, gidx, gate, out.rearrange("b s d -> (b s) d"))


_WEIGHTS = {"wq0": "L0_attn_WQ", "wk0": "L0_attn_WK", "wv0": "L0_attn_WV", "wo0": "L0_attn_WO",
            "wq1": "L1_attn_Wq", "wk1": "L1_attn_Wk", "wv1": "L1_attn_Wv", "wo1": "L1_attn_Wo"}
_PLAIN = {"x": "L0_attn_x", "gate0": "L0_ffn_gate_w", "gbias0": "L0_ffn_gate_b",
          "w1_0": "L0_ffn_w1", "w2_0": "L0_ffn_w2", "b2_0": "L0_ffn_b2",
          "gate1": "L1_ffn_router_w", "gbias1": "L1_ffn_router_b",
          "w1_1": "L1_ffn_w1", "w2_1": "L1_ffn_w2", "b2_1": "L1_ffn_b2", "bo1": "L1_attn_bo"}
_TURNED = {"b1_0": "L0_ffn_b1", "b1_1": "L1_ffn_b1"}


def kernel(**inputs):
    import numpy as np
    import concourse.bacc as bacc
    from concourse.bass_utils import run_bass_kernel_spmd

    nc = bacc.Bacc("TRN2", target_bir_lowering=False, num_devices=1)
    arrays = {}
    for name, key in _WEIGHTS.items():
        arrays[name] = np.ascontiguousarray(np.asarray(inputs[key]).T)
    for name, key in _PLAIN.items():
        arrays[name] = np.ascontiguousarray(inputs[key])
    for name, key in _TURNED.items():
        a = np.asarray(inputs[key])
        arrays[name] = np.ascontiguousarray(a.reshape(a.shape[0], FT, P).transpose(2, 0, 1))
    ins = {n: nc.dram_tensor(n, a.shape, mybir.dt.from_np(a.dtype), kind="ExternalInput").ap()
           for n, a in arrays.items()}
    out = nc.dram_tensor("out", (B, S, D), F32, kind="ExternalOutput").ap()
    build(nc, ins, out)
    r = run_bass_kernel_spmd(nc, [arrays], core_ids=[0])
    return r.results[0]["out"]
```
